# Optimizing a Trainium2 kernel written in Bass

```python
import numpy as np
import jax
import jax.numpy as jnp

def _softmax(x, axis=-1):
    return jax.nn.softmax(x, axis=axis)

def _gelu(x):
    return jax.nn.gelu(x, approximate=True)

def _silu(x):
    return jax.nn.silu(x)

def _sigmoid(x):
    return jax.nn.sigmoid(x)

def _layernorm(x, axis=-1, eps=1e-05):
    m = jnp.mean(x, axis=axis, keepdims=True)
    v = jnp.var(x, axis=axis, keepdims=True)
    return (x - m) / jnp.sqrt(v + eps)

def _scatter_add(tgt, idx, src, axis=0):
    return tgt.at[idx].add(src)

def _segment_sum(src, seg, n):
    return jax.ops.segment_sum(src, seg, n)
kernel_name = 'mk_audio_tower_d2_tok_aud1d768_r4_3c252b'

def setup_inputs(seed: int=0):
    np.random.seed(seed)
    _w = jnp.asarray

    def _rec_inputs():
        import jax
        import jax.numpy as jnp
        _rk = jax.random.key(seed)
        x = -0.000869125 + 1.00042 * jax.random.normal(jax.random.fold_in(_rk, 1), (8, 120000), jnp.float32)
        return x
    x = _rec_inputs()

    def _L0_tok_setup():
        import jax, jax.numpy as jnp
        import numpy as np
        CONVS = [(128, 10, 5)] + [(128, 3, 2)] * 4 + [(128, 2, 2)] * 2

        def _fp32_layernorm(x, g, b, eps=1e-05):
            xf = x.astype(jnp.float32)
            mu = xf.mean(-1, keepdims=True)
            var = xf.var(-1, keepdims=True)
            y = (xf - mu) * jax.lax.rsqrt(var + eps) * g.astype(jnp.float32) + b.astype(jnp.float32)
            return y.astype(x.dtype)

        def _conv1d(x, w, stride):
            return jax.lax.conv_general_dilated(x, w, (stride,), 'VALID', dimension_numbers=('NCH', 'OIH', 'NCH'))
        key = jax.random.key(seed)
        keys = jax.random.split(key, 16)
        inp = {'x': jax.random.normal(keys[0], (8, 40000), jnp.float32)}
        in_d = 1
        for i, (dim, k, s) in enumerate(CONVS):
            fan_in = in_d * k
            inp[f'conv_w{i}'] = jax.random.normal(keys[1 + i], (dim, in_d, k), jnp.float32) * np.float32(np.sqrt(2.0 / fan_in))
            inp[f'ln_g{i}'] = jnp.ones((dim,), jnp.float32)
            inp[f'ln_b{i}'] = jnp.zeros((dim,), jnp.float32)
            in_d = dim
        inp['fln_g'] = jnp.ones((128,), jnp.float32)
        inp['fln_b'] = jnp.zeros((128,), jnp.float32)
        inp['proj_w'] = jax.random.normal(keys[9], (128, 192), jnp.float32) * np.float32(0.02)
        inp['proj_b'] = jnp.zeros((192,), jnp.float32)
        return inp
    _L0_tok_all = _L0_tok_setup()
    _L0_tok_in = {k: v for k, v in _L0_tok_all.items() if k in ('conv_w0', 'ln_g0', 'ln_b0', 'conv_w1', 'ln_g1', 'ln_b1', 'conv_w2', 'ln_g2', 'ln_b2', 'conv_w3', 'ln_g3', 'ln_b3', 'conv_w4', 'ln_g4', 'ln_b4', 'conv_w5', 'ln_g5', 'ln_b5', 'conv_w6', 'ln_g6', 'ln_b6', 'fln_g', 'fln_b', 'proj_w', 'proj_b')}
    del _L0_tok_all

    def _L0_attn_setup():
        import jax, jax.numpy as jnp
        import numpy as np
        STATE_DIM = 128
        FEATURES = 192
        DT_MIN, DT_MAX = (0.001, 0.1)
        key = jax.random.key(seed)
        ks = jax.random.split(key, 8)
        B, S, F, N = (8, 1024, FEATURES, STATE_DIM)
        n = jnp.arange(N, dtype=jnp.float32)
        log_A_real = jnp.log(n + 0.5)
        A_imag = jnp.pi * n
        B_re = jax.random.normal(ks[0], (N, F), jnp.float32) / jnp.sqrt(N)
        B_im = jax.random.normal(ks[1], (N, F), jnp.float32) / jnp.sqrt(N)
        C_re = jax.random.normal(ks[2], (F, N), jnp.float32) / jnp.sqrt(F)
        C_im = jax.random.normal(ks[3], (F, N), jnp.float32) / jnp.sqrt(F)
        D = jax.random.normal(ks[4], (F,), jnp.float32)
        log_dt = jax.random.uniform(ks[5], (N,), jnp.float32, minval=jnp.log(DT_MIN), maxval=jnp.log(DT_MAX))
        u = jax.random.normal(ks[6], (B, S, F), jnp.float32)
        return {'u': u, 'log_A_real': log_A_real, 'A_imag': A_imag, 'B_re': B_re, 'B_im': B_im, 'C_re': C_re, 'C_im': C_im, 'D': D, 'log_dt': log_dt}
    _L0_attn_all = _L0_attn_setup()
    _L0_attn_in = {k: v for k, v in _L0_attn_all.items() if k in ('log_A_real', 'A_imag', 'B_re', 'B_im', 'C_re', 'C_im', 'D', 'log_dt')}
    del _L0_attn_all

    def _L0_ffn_setup():
        import jax, jax.numpy as jnp
        import numpy as np
        B, N, C, H, E = (8, 256, 192, 768, 4)
        key = jax.random.key(seed)
        ks = jax.random.split(key, 8)
        s_in = 1.0 / np.sqrt(C)
        s_h = 1.0 / np.sqrt(H)
        return {'x': jax.random.normal(ks[0], (B, N, C), dtype=jnp.float32), 'gate_w': jax.random.normal(ks[1], (C, E), dtype=jnp.float32) * 0.01, 'gate_b': jnp.zeros((E,), dtype=jnp.float32), 'gate_center': jnp.zeros((E,), dtype=jnp.float32), 'w1': jax.random.uniform(ks[2], (E, C, H), jnp.float32, -s_in, s_in), 'b1': jax.random.uniform(ks[3], (E, H), jnp.float32, -s_in, s_in), 'w2': jax.random.uniform(ks[4], (E, H, C), jnp.float32, -s_h, s_h), 'b2': jax.random.uniform(ks[5], (E, C), jnp.float32, -s_h, s_h)}
    _L0_ffn_all = _L0_ffn_setup()
    _L0_ffn_in = {k: v for k, v in _L0_ffn_all.items() if k in ('gate_w', 'gate_b', 'gate_center', 'w1', 'b1', 'w2', 'b2')}
    del _L0_ffn_all

    def _L1_attn_setup():
        import jax, jax.numpy as jnp
        import numpy as np
        B, L, D = (8, 1024, 192)
        EPS = 1e-05

        def layer_norm(x, g, b):
            mu = jnp.mean(x, axis=-1, keepdims=True)
            var = jnp.mean(jnp.square(x - mu), axis=-1, keepdims=True)
            return (x - mu) * jax.lax.rsqrt(var + EPS) * g + b

        def conv1d_same(x_blc, w_oik, b_o):
            x_ncw = jnp.swapaxes(x_blc, 1, 2)
            y = jax.lax.conv_general_dilated(x_ncw, w_oik, window_strides=(1,), padding=[(1, 1)], dimension_numbers=('NCW', 'OIW', 'NCW'))
            y = y + b_o[None, :, None]
            return jnp.swapaxes(y, 1, 2)

        def simple_ssm(u, a_p, b_p, c_p, d_p):
            a = jax.nn.sigmoid(a_p)

            def step(h, ut):
                h = a * h + b_p * ut
                return (h, c_p * h)
            h0 = jnp.zeros((u.shape[0], u.shape[2]), u.dtype)
            _, y = jax.lax.scan(step, h0, jnp.swapaxes(u, 0, 1))
            return jnp.swapaxes(y, 0, 1) + d_p * u
        key = jax.random.key(seed)
        ks = jax.random.split(key, 16)
        s_lin = 1.0 / np.sqrt(D)
        s_conv = 1.0 / np.sqrt(3 * D)
        return {'x': jax.random.normal(ks[0], (B, L, D), jnp.float32), 'ln_g': jnp.ones((D,), jnp.float32), 'ln_b': jnp.zeros((D,), jnp.float32), 'Wi': jax.random.normal(ks[1], (D, 2 * D), jnp.float32) * s_lin, 'bi': jnp.zeros((2 * D,), jnp.float32), 'Wf_conv': jax.random.normal(ks[2], (D, D, 3), jnp.float32) * s_conv, 'bf_conv': jnp.zeros((D,), jnp.float32), 'af': jax.random.normal(ks[3], (D,), jnp.float32), 'bf': jax.random.normal(ks[4], (D,), jnp.float32) * 0.5, 'cf': jax.random.normal(ks[5], (D,), jnp.float32) * 0.5, 'df': jax.random.normal(ks[6], (D,), jnp.float32) * 0.5, 'Wb_conv': jax.random.normal(ks[7], (D, D, 3), jnp.float32) * s_conv, 'bb_conv': jnp.zeros((D,), jnp.float32), 'ab': jax.random.normal(ks[8], (D,), jnp.float32), 'bb': jax.random.normal(ks[9], (D,), jnp.float32) * 0.5, 'cb': jax.random.normal(ks[10], (D,), jnp.float32) * 0.5, 'db': jax.random.normal(ks[11], (D,), jnp.float32) * 0.5, 'Wo': jax.random.normal(ks[12], (D, D), jnp.float32) * s_lin, 'bo': jnp.zeros((D,), jnp.float32)}
    _L1_attn_all = _L1_attn_setup()
    _L1_attn_in = {k: v for k, v in _L1_attn_all.items() if k in ('ln_g', 'ln_b', 'Wi', 'bi', 'Wf_conv', 'bf_conv', 'af', 'bf', 'cf', 'df', 'Wb_conv', 'bb_conv', 'ab', 'bb', 'cb', 'db', 'Wo', 'bo')}
    del _L1_attn_all

    def _L1_ffn_setup():
        import jax, jax.numpy as jnp
        import numpy as np
        EPS_NORM = 1e-06
        EPS_LN = 1e-05

        def _layernorm(x, g, b):
            mu = jnp.mean(x, axis=-1, keepdims=True)
            var = jnp.mean(jnp.square(x - mu), axis=-1, keepdims=True)
            return (x - mu) * jax.lax.rsqrt(var + EPS_LN) * g + b
        key = jax.random.key(seed)
        ks = jax.random.split(key, 6)
        b, m, d = (8, 256, 192)
        n, p = (64, 16)
        h = 2 * d
        x = jax.random.normal(ks[0], (b, m, d), dtype=jnp.float32)
        phi = jax.random.normal(ks[1], (n, p, d), dtype=jnp.float32)
        ln_g = jnp.ones((n, d), dtype=jnp.float32)
        ln_b = jnp.zeros((n, d), dtype=jnp.float32)
        w1 = jax.random.normal(ks[2], (n, d, h), dtype=jnp.float32) * (1.0 / np.sqrt(d))
        b1 = jax.random.normal(ks[3], (n, h), dtype=jnp.float32) * 0.01
        w2 = jax.random.normal(ks[4], (n, h, d), dtype=jnp.float32) * (1.0 / np.sqrt(h))
        b2 = jax.random.normal(ks[5], (n, d), dtype=jnp.float32) * 0.01
        return {'x': x, 'phi': phi, 'ln_g': ln_g, 'ln_b': ln_b, 'w1': w1, 'b1': b1, 'w2': w2, 'b2': b2}
    _L1_ffn_all = _L1_ffn_setup()
    _L1_ffn_in = {k: v for k, v in _L1_ffn_all.items() if k in ('phi', 'ln_g', 'ln_b', 'w1', 'b1', 'w2', 'b2')}
    del _L1_ffn_all
    return {'x': x, 'L0_tok_conv_w0': _L0_tok_in['conv_w0'], 'L0_tok_ln_g0': _L0_tok_in['ln_g0'], 'L0_tok_ln_b0': _L0_tok_in['ln_b0'], 'L0_tok_conv_w1': _L0_tok_in['conv_w1'], 'L0_tok_ln_g1': _L0_tok_in['ln_g1'], 'L0_tok_ln_b1': _L0_tok_in['ln_b1'], 'L0_tok_conv_w2': _L0_tok_in['conv_w2'], 'L0_tok_ln_g2': _L0_tok_in['ln_g2'], 'L0_tok_ln_b2': _L0_tok_in['ln_b2'], 'L0_tok_conv_w3': _L0_tok_in['conv_w3'], 'L0_tok_ln_g3': _L0_tok_in['ln_g3'], 'L0_tok_ln_b3': _L0_tok_in['ln_b3'], 'L0_tok_conv_w4': _L0_tok_in['conv_w4'], 'L0_tok_ln_g4': _L0_tok_in['ln_g4'], 'L0_tok_ln_b4': _L0_tok_in['ln_b4'], 'L0_tok_conv_w5': _L0_tok_in['conv_w5'], 'L0_tok_ln_g5': _L0_tok_in['ln_g5'], 'L0_tok_ln_b5': _L0_tok_in['ln_b5'], 'L0_tok_conv_w6': _L0_tok_in['conv_w6'], 'L0_tok_ln_g6': _L0_tok_in['ln_g6'], 'L0_tok_ln_b6': _L0_tok_in['ln_b6'], 'L0_tok_fln_g': _L0_tok_in['fln_g'], 'L0_tok_fln_b': _L0_tok_in['fln_b'], 'L0_tok_proj_w': _L0_tok_in['proj_w'], 'L0_tok_proj_b': _L0_tok_in['proj_b'], 'L0_attn_log_A_real': _L0_attn_in['log_A_real'], 'L0_attn_A_imag': _L0_attn_in['A_imag'], 'L0_attn_B_re': _L0_attn_in['B_re'], 'L0_attn_B_im': _L0_attn_in['B_im'], 'L0_attn_C_re': _L0_attn_in['C_re'], 'L0_attn_C_im': _L0_attn_in['C_im'], 'L0_attn_D': _L0_attn_in['D'], 'L0_attn_log_dt': _L0_attn_in['log_dt'], 'L0_ffn_gate_w': _L0_ffn_in['gate_w'], 'L0_ffn_gate_b': _L0_ffn_in['gate_b'], 'L0_ffn_gate_center': _L0_ffn_in['gate_center'], 'L0_ffn_w1': _L0_ffn_in['w1'], 'L0_ffn_b1': _L0_ffn_in['b1'], 'L0_ffn_w2': _L0_ffn_in['w2'], 'L0_ffn_b2': _L0_ffn_in['b2'], 'L1_attn_ln_g': _L1_attn_in['ln_g'], 'L1_attn_ln_b': _L1_attn_in['ln_b'], 'L1_attn_Wi': _L1_attn_in['Wi'], 'L1_attn_bi': _L1_attn_in['bi'], 'L1_attn_Wf_conv': _L1_attn_in['Wf_conv'], 'L1_attn_bf_conv': _L1_attn_in['bf_conv'], 'L1_attn_af': _L1_attn_in['af'], 'L1_attn_bf': _L1_attn_in['bf'], 'L1_attn_cf': _L1_attn_in['cf'], 'L1_attn_df': _L1_attn_in['df'], 'L1_attn_Wb_conv': _L1_attn_in['Wb_conv'], 'L1_attn_bb_conv': _L1_attn_in['bb_conv'], 'L1_attn_ab': _L1_attn_in['ab'], 'L1_attn_bb': _L1_attn_in['bb'], 'L1_attn_cb': _L1_attn_in['cb'], 'L1_attn_db': _L1_attn_in['db'], 'L1_attn_Wo': _L1_attn_in['Wo'], 'L1_attn_bo': _L1_attn_in['bo'], 'L1_ffn_phi': _L1_ffn_in['phi'], 'L1_ffn_ln_g': _L1_ffn_in['ln_g'], 'L1_ffn_ln_b': _L1_ffn_in['ln_b'], 'L1_ffn_w1': _L1_ffn_in['w1'], 'L1_ffn_b1': _L1_ffn_in['b1'], 'L1_ffn_w2': _L1_ffn_in['w2'], 'L1_ffn_b2': _L1_ffn_in['b2']}

def reference(x, L0_tok_conv_w0, L0_tok_ln_g0, L0_tok_ln_b0, L0_tok_conv_w1, L0_tok_ln_g1, L0_tok_ln_b1, L0_tok_conv_w2, L0_tok_ln_g2, L0_tok_ln_b2, L0_tok_conv_w3, L0_tok_ln_g3, L0_tok_ln_b3, L0_tok_conv_w4, L0_tok_ln_g4, L0_tok_ln_b4, L0_tok_conv_w5, L0_tok_ln_g5, L0_tok_ln_b5, L0_tok_conv_w6, L0_tok_ln_g6, L0_tok_ln_b6, L0_tok_fln_g, L0_tok_fln_b, L0_tok_proj_w, L0_tok_proj_b, L0_attn_log_A_real, L0_attn_A_imag, L0_attn_B_re, L0_attn_B_im, L0_attn_C_re, L0_attn_C_im, L0_attn_D, L0_attn_log_dt, L0_ffn_gate_w, L0_ffn_gate_b, L0_ffn_gate_center, L0_ffn_w1, L0_ffn_b1, L0_ffn_w2, L0_ffn_b2, L1_attn_ln_g, L1_attn_ln_b, L1_attn_Wi, L1_attn_bi, L1_attn_Wf_conv, L1_attn_bf_conv, L1_attn_af, L1_attn_bf, L1_attn_cf, L1_attn_df, L1_attn_Wb_conv, L1_attn_bb_conv, L1_attn_ab, L1_attn_bb, L1_attn_cb, L1_attn_db, L1_attn_Wo, L1_attn_bo, L1_ffn_phi, L1_ffn_ln_g, L1_ffn_ln_b, L1_ffn_w1, L1_ffn_b1, L1_ffn_w2, L1_ffn_b2):
    import jax
    import jax.numpy as jnp

    def _L0_tok_ref(x, conv_w0, ln_g0, ln_b0, conv_w1, ln_g1, ln_b1, conv_w2, ln_g2, ln_b2, conv_w3, ln_g3, ln_b3, conv_w4, ln_g4, ln_b4, conv_w5, ln_g5, ln_b5, conv_w6, ln_g6, ln_b6, fln_g, fln_b, proj_w, proj_b):
        import jax, jax.numpy as jnp
        import numpy as np
        CONVS = [(128, 10, 5)] + [(128, 3, 2)] * 4 + [(128, 2, 2)] * 2

        def _fp32_layernorm(x, g, b, eps=1e-05):
            xf = x.astype(jnp.float32)
            mu = xf.mean(-1, keepdims=True)
            var = xf.var(-1, keepdims=True)
            y = (xf - mu) * jax.lax.rsqrt(var + eps) * g.astype(jnp.float32) + b.astype(jnp.float32)
            return y.astype(x.dtype)

        def _conv1d(x, w, stride):
            return jax.lax.conv_general_dilated(x, w, (stride,), 'VALID', dimension_numbers=('NCH', 'OIH', 'NCH'))
        conv_ws = [conv_w0, conv_w1, conv_w2, conv_w3, conv_w4, conv_w5, conv_w6]
        ln_gs = [ln_g0, ln_g1, ln_g2, ln_g3, ln_g4, ln_g5, ln_g6]
        ln_bs = [ln_b0, ln_b1, ln_b2, ln_b3, ln_b4, ln_b5, ln_b6]
        strides = [s for _, _, s in CONVS]
        h = x[:, None, :]
        for w, g, b, s in zip(conv_ws, ln_gs, ln_bs, strides):
            h = _conv1d(h, w, s)
            h = jnp.swapaxes(h, -2, -1)
            h = _fp32_layernorm(h, g, b)
            h = jnp.swapaxes(h, -2, -1)
            h = jax.nn.gelu(h, approximate=False)
        h = jnp.swapaxes(h, 1, 2)
        norm_h = _fp32_layernorm(h, fln_g, fln_b)
        out = norm_h @ proj_w + proj_b
        return out

    def _L0_attn_ref(u, log_A_real, A_imag, B_re, B_im, C_re, C_im, D, log_dt):
        import jax, jax.numpy as jnp
        import numpy as np
        STATE_DIM = 128
        FEATURES = 192
        DT_MIN, DT_MAX = (0.001, 0.1)
        B, S, F = u.shape
        N = log_A_real.shape[0]
        dt = jnp.exp(log_dt)
        A_diag = -jnp.exp(log_A_real) + 1j * A_imag
        A_bar = jnp.exp(A_diag * dt)
        B_complex = B_re + 1j * B_im
        B_bar = (A_bar[:, None] - 1.0) / (A_diag[:, None] + 1e-08) * B_complex
        C_complex = C_re + 1j * C_im
        u_f = u.astype(jnp.float32)
        Bu = jnp.einsum('bsf,nf->bsn', u_f, B_bar)
        A_exp = jnp.broadcast_to(A_bar[None, None, :], (B, S, N))

        def binary_operator(e1, e2):
            a1, b1 = e1
            a2, b2 = e2
            return (a1 * a2, a2 * b1 + b2)
        _, x_states = jax.lax.associative_scan(binary_operator, (A_exp, Bu), axis=1)
        y = jnp.einsum('fn,bsn->bsf', C_complex, x_states).real
        y = y + D[None, None, :] * u_f
        return y.astype(u.dtype)

    def _L0_ffn_ref(x, gate_w, gate_b, gate_center, w1, b1, w2, b2):
        import jax, jax.numpy as jnp
        import numpy as np
        B, N, C, H, E = (8, 256, 192, 768, 4)
        b, n, c = x.shape
        scores = jnp.einsum('bnc,ce->bne', x, gate_w) + gate_b
        p_experts = jax.nn.softmax(scores - gate_center, axis=-1)
        expert = jnp.argmax(p_experts, axis=-1).reshape(-1)
        xt = x.reshape(-1, c)
        h = jax.nn.gelu(jnp.einsum('tc,ech->eth', xt, w1) + b1[:, None, :], approximate=False)
        out_all = jnp.einsum('eth,ehc->etc', h, w2) + b2[:, None, :]
        out = jnp.take_along_axis(out_all, expert[None, :, None], axis=0)[0]
        return out.reshape(b, n, c)

    def _L1_attn_ref(x, ln_g, ln_b, Wi, bi, Wf_conv, bf_conv, af, bf, cf, df, Wb_conv, bb_conv, ab, bb, cb, db, Wo, bo):
        import jax, jax.numpy as jnp
        import numpy as np
        B, L, D = (8, 1024, 192)
        EPS = 1e-05

        def layer_norm(x, g, b):
            mu = jnp.mean(x, axis=-1, keepdims=True)
            var = jnp.mean(jnp.square(x - mu), axis=-1, keepdims=True)
            return (x - mu) * jax.lax.rsqrt(var + EPS) * g + b

        def conv1d_same(x_blc, w_oik, b_o):
            x_ncw = jnp.swapaxes(x_blc, 1, 2)
            y = jax.lax.conv_general_dilated(x_ncw, w_oik, window_strides=(1,), padding=[(1, 1)], dimension_numbers=('NCW', 'OIW', 'NCW'))
            y = y + b_o[None, :, None]
            return jnp.swapaxes(y, 1, 2)

        def simple_ssm(u, a_p, b_p, c_p, d_p):
            a = jax.nn.sigmoid(a_p)

            def step(h, ut):
                h = a * h + b_p * ut
                return (h, c_p * h)
            h0 = jnp.zeros((u.shape[0], u.shape[2]), u.dtype)
            _, y = jax.lax.scan(step, h0, jnp.swapaxes(u, 0, 1))
            return jnp.swapaxes(y, 0, 1) + d_p * u
        residual = x
        xn = layer_norm(x, ln_g, ln_b)
        proj = xn @ Wi + bi
        xg, z = (proj[..., :D], proj[..., D:])
        f = conv1d_same(xg, Wf_conv, bf_conv)
        f = simple_ssm(f, af, bf, cf, df)
        b_in = jnp.flip(xg, axis=1)
        bb_out = conv1d_same(b_in, Wb_conv, bb_conv)
        bb_out = simple_ssm(bb_out, ab, bb, cb, db)
        bb_out = jnp.flip(bb_out, axis=1)
        zg = jax.nn.silu(z)
        y = f * zg + bb_out * zg
        return y @ Wo + bo + residual

    def _L1_ffn_ref(x, phi, ln_g, ln_b, w1, b1, w2, b2):
        import jax, jax.numpy as jnp
        import numpy as np
        EPS_NORM = 1e-06
        EPS_LN = 1e-05

        def _layernorm(x, g, b):
            mu = jnp.mean(x, axis=-1, keepdims=True)
            var = jnp.mean(jnp.square(x - mu), axis=-1, keepdims=True)
            return (x - mu) * jax.lax.rsqrt(var + EPS_LN) * g + b
        phi_n = phi * jax.lax.rsqrt(jnp.sum(jnp.square(phi), axis=0, keepdims=True) + EPS_NORM)
        bsz, m, d = x.shape
        n, p, _ = phi_n.shape
        logits = jnp.einsum('bmd,npd->bmnp', x, phi_n)
        D = jax.nn.softmax(logits, axis=1)
        C = jax.nn.softmax(logits.reshape(bsz, m, n * p), axis=-1)
        Xs = jnp.einsum('bmd,bmnp->bnpd', x, D)
        hdn = _layernorm(Xs, ln_g[:, None, :], ln_b[:, None, :])
        hdn = jnp.einsum('bnpd,ndh->bnph', hdn, w1) + b1[:, None, :]
        hdn = jax.nn.gelu(hdn, approximate=False)
        Ys = jnp.einsum('bnph,nhd->bnpd', hdn, w2) + b2[:, None, :]
        Ys = Ys.reshape(bsz, n * p, d)
        Y = jnp.einsum('bsd,bms->bmd', Ys, C)
        return Y
    h = _L0_tok_ref(x, L0_tok_conv_w0, L0_tok_ln_g0, L0_tok_ln_b0, L0_tok_conv_w1, L0_tok_ln_g1, L0_tok_ln_b1, L0_tok_conv_w2, L0_tok_ln_g2, L0_tok_ln_b2, L0_tok_conv_w3, L0_tok_ln_g3, L0_tok_ln_b3, L0_tok_conv_w4, L0_tok_ln_g4, L0_tok_ln_b4, L0_tok_conv_w5, L0_tok_ln_g5, L0_tok_ln_b5, L0_tok_conv_w6, L0_tok_ln_g6, L0_tok_ln_b6, L0_tok_fln_g, L0_tok_fln_b, L0_tok_proj_w, L0_tok_proj_b)
    h = h + _L0_attn_ref(_layernorm(h, axis=-1), L0_attn_log_A_real, L0_attn_A_imag, L0_attn_B_re, L0_attn_B_im, L0_attn_C_re, L0_attn_C_im, L0_attn_D, L0_attn_log_dt)
    h = h + _L0_ffn_ref(_layernorm(h, axis=-1), L0_ffn_gate_w, L0_ffn_gate_b, L0_ffn_gate_center, L0_ffn_w1, L0_ffn_b1, L0_ffn_w2, L0_ffn_b2)
    h = h + _L1_attn_ref(_layernorm(h, axis=-1), L1_attn_ln_g, L1_attn_ln_b, L1_attn_Wi, L1_attn_bi, L1_attn_Wf_conv, L1_attn_bf_conv, L1_attn_af, L1_attn_bf, L1_attn_cf, L1_attn_df, L1_attn_Wb_conv, L1_attn_bb_conv, L1_attn_ab, L1_attn_bb, L1_attn_cb, L1_attn_db, L1_attn_Wo, L1_attn_bo)
    h = h + _L1_ffn_ref(_layernorm(h, axis=-1), L1_ffn_phi, L1_ffn_ln_g, L1_ffn_ln_b, L1_ffn_w1, L1_ffn_b1, L1_ffn_w2, L1_ffn_b2)
    return h

_drawn_inputs = setup_inputs


def setup_inputs(seed=0):
    import zlib

    import numpy as np

    out = dict(_drawn_inputs(seed))
    spreads = {'L0_tok_ln_g0': (1.0, 0.2),
     'L0_tok_ln_b0': (0.0, 0.1),
     'L0_tok_ln_g1': (1.0, 0.2),
     'L0_tok_ln_b1': (0.0, 0.1),
     'L0_tok_ln_g2': (1.0, 0.2),
     'L0_tok_ln_b2': (0.0, 0.1),
     'L0_tok_ln_g3': (1.0, 0.2),
     'L0_tok_ln_b3': (0.0, 0.1),
     'L0_tok_ln_g4': (1.0, 0.2),
     'L0_tok_ln_b4': (0.0, 0.1),
     'L0_tok_ln_g5': (1.0, 0.2),
     'L0_tok_ln_b5': (0.0, 0.1),
     'L0_tok_ln_g6': (1.0, 0.2),
     'L0_tok_ln_b6': (0.0, 0.1),
     'L0_tok_fln_g': (1.0, 0.2),
     'L0_tok_fln_b': (0.0, 0.1),
     'L0_tok_proj_b': (0.0, 0.1),
     'L0_ffn_gate_b': (0.0, 0.1),
     'L0_ffn_gate_center': (0.0, 0.1),
     'L1_attn_ln_g': (1.0, 0.2),
     'L1_attn_ln_b': (0.0, 0.1),
     'L1_attn_bi': (0.0, 0.1),
     'L1_attn_bf_conv': (0.0, 0.316),
     'L1_attn_bb_conv': (0.0, 0.1),
     'L1_attn_bo': (0.0, 0.1),
     'L1_ffn_ln_g': (1.0, 0.6),
     'L1_ffn_ln_b': (0.0, 0.8)}
    factors = {'L0_ffn_b1': 3.611, 'L1_ffn_b1': 64.0, 'L1_ffn_b2': 63.192}
    for name, (base, spread) in spreads.items():
        noise = np.random.default_rng([zlib.crc32(name.encode()), seed]).standard_normal(out[name].shape)
        drawn = base * np.exp(spread * noise) if base else spread * noise
        out[name] = jnp.asarray(drawn.astype(out[name].dtype))
    for name, factor in factors.items():
        out[name] = (out[name] * factor).astype(out[name].dtype)
    return out
```

```python
import concourse.bass as bass
from concourse import mybir
from contextlib import ExitStack

F32 = mybir.dt.float32
BF16 = mybir.dt.bfloat16
ALU = mybir.AluOpType
ACT = mybir.ActivationFunctionType
AX = mybir.AxisListType

P = 128
B = 8
SAMPLES = 120000
C = 128
TAPS0, STRIDE0 = 10, 5
EPS = 1e-5

CHUNK = 4096
POS = CHUNK // P
WIN = STRIDE0 * (POS - 1) + TAPS0
HALF = POS // 2
WINH = STRIDE0 * (HALF - 1) + TAPS0
STEP = CHUNK * STRIDE0
CHUNKS = -(-B * SAMPLES // STEP)
PAIRS = POS // 2
PARTS = 6
ROWS = PARTS * TAPS0
SPLIT = [(0, 0), (0, 1), (1, 0), (0, 2), (2, 0), (1, 1)]


def view(ap, dims, offset=0):
    return bass.AP(ap.tensor, ap.offset + offset, [list(ap.ap[0])] + [list(d) for d in dims])


def bcast(ap, n):
    return bass.AP(ap.tensor, ap.offset, [list(d) for d in ap.ap] + [[0, n]])


GROUPS = [(1, 0), (1, 1), (4, 0), (1, 2), (1, 3), (3, 0), (2, 0), (2, 1)]
NG = len(GROUPS)
BANK = [g % 3 for g in range(NG)]
BEFORE = [5, 6, 7] + [None] * 5
for _g in range(NG):
    _same = [q for q in range(_g) if BANK[q] == BANK[_g]]
    if _same:
        BEFORE[_g] = _same[-1]
BEFORE[0], BEFORE[1], BEFORE[2] = 6, 7, 5
LAG = 2
L0_AFTER = {4: (0, 1, 2), 5: (3, 4, 5), 6: (6, 7)}
INPUT_OF = {1: 0, 2: 1, 3: 2, 4: 3}


def setup(nc, T, S, io):
    with nc.Block() as block:
        @block.sync
        def _(sp):
            sp.dma_start(T["wt"][:, :, :], io["conv_w"]).then_inc(S["wt_loaded"], 16)
            sp.dma_start(T["w0T"][:, :], io["conv_w0"]).then_inc(S["w0_loaded"], 16)
            sp.dma_start(T["cols"][:, :], io["cols"]).then_inc(S["cols_loaded"], 16)
            sp.dma_start(T["xs"][:, :], x_chunk(io, 0)).then_inc(S["x_loaded"], 16)
            for name in ("proj_w", "CT", "BTa", "BTb", "gate_wa", "gate_wb", "b1", "b2", "Wia", "Wib", "Wca", "Wcb",
                         "Wcc", "Woa", "Wob", "lncol"):
                sp.dma_start(T[name][:], io[name]).then_inc(S["small_loaded"], 16)
            sp.dma_start(T["mcol"][:, 0:15], io["mcol"]).then_inc(S["small_loaded"], 16)
            for name, n in (("rows", 3 * D), ("gate_row", 2 * N_EXPERT)):
                src = bass.AP(io[name].tensor, 0, [[0, TOK], [1, n]])
                sp.dma_start(view(T[name][:], [[1, n]]), src).then_inc(S["rows_loaded"], 16)
            sp.wait_ge(S["gram_ready"], 1)
            for r in range(HALF):
                sp.dma_start(T["band"][STRIDE0 * r:STRIDE0 * r + TAPS0, TAPS0 * r:TAPS0 * (r + 1)],
                             T["gram"][:, :]).then_inc(S["band_loaded"], 16)
            sp.wait_ge(S["w0_split"], 1)
            for slot in range(2):
                for n, (_, part) in enumerate(SPLIT):
                    r = slot * ROWS + n * TAPS0
                    sp.dma_start(T["w60"][r:r + TAPS0, slot, :], T["w0parts"][:, part, :])\
                        .then_inc(S["w60_loaded"], 16)
            sp.wait_ge(S["cols_loaded"], 16)
            sp.wait_ge(S["small_loaded"], 16 * 17)
            sp.wait_ge(S["rows_loaded"], 16 * 2)

        @block.gpsimd
        def _(pool):
            pool.memset(T["ident"][:, :], 0.0).then_inc(S["ident_zero"], 1)
            pool.wait_ge(S["ident_zero"], 1)
            pool.affine_select(out=T["ident"][:, :], in_=T["ident"][:, :], compare_op=ALU.not_equal,
                               fill=1.0, base=0, pattern=[[-1, P]], channel_multiplier=1)\
                .then_inc(S["ident_ready"], 1)
            pool.memset(T["minus_half"][:, :], -0.5)
            pool.memset(T["h"][:, :, :], 0.0)
            pool.memset(T["band"][:, :], 0.0)
            pool.memset(T["w60"][:, :, :], 0.0)
            for name in ("l0", "l1", "l2", "l3"):
                pool.memset(T[name][:, :], 0.0)
            pool.memset(T["yn"][:, :, :], 0.0).then_inc(S["pool_zero"], 1)

        @block.vector
        def _(dve):
            dve.wait_ge(S["pool_zero"], 1)
            dve.wait_ge(S["w0_loaded"], 16)
            dve.reduce_sum(T["w0mean"][:, :], T["w0T"][:, :], axis=AX.X).then_inc(S["dve"], 1)
            dve.wait_ge(S["dve"], 1)
            dve.tensor_scalar(T["w0mean"][:, :], T["w0mean"][:, :], 1.0 / C, None, ALU.mult).then_inc(S["dve"], 1)
            dve.wait_ge(S["dve"], 2)
            dve.tensor_scalar(T["w0T"][:, :], T["w0T"][:, :], T["w0mean"][:, 0:1], None, ALU.subtract)\
                .then_inc(S["w0_centred"], 1)
            dve.wait_ge(S["w0_centred"], 1)
            dve.tensor_copy(T["w0parts"][:, 0, :], T["w0T"][:, :]).then_inc(S["dve"], 1)
            dve.wait_ge(S["dve"], 3)
            dve.tensor_tensor(T["w0rest"][:, :], T["w0T"][:, :], T["w0parts"][:, 0, :], ALU.subtract)\
                .then_inc(S["dve"], 1)
            dve.wait_ge(S["dve"], 4)
            dve.tensor_copy(T["w0parts"][:, 1, :], T["w0rest"][:, :]).then_inc(S["dve"], 1)
            dve.wait_ge(S["dve"], 5)
            dve.tensor_tensor(T["w0parts"][:, 2, :], T["w0rest"][:, :], T["w0parts"][:, 1, :], ALU.subtract)\
                .then_inc(S["w0_split"], 1)
            dve.wait_ge(S["wt_loaded"], 16)
            dve.reduce_sum(T["wmean"][:, :], T["wt"][:, :, :], axis=AX.X).then_inc(S["dve"], 1)
            dve.wait_ge(S["dve"], 6)
            dve.tensor_scalar(T["wmean"][:, :], T["wmean"][:, :], 1.0 / C, None, ALU.mult).then_inc(S["dve"], 1)
            dve.wait_ge(S["dve"], 7)
            dve.tensor_tensor(T["wt"][:, :, :], T["wt"][:, :, :], bcast(T["wmean"][:, :], C), ALU.subtract)\
                .then_inc(S["wt_centred"], 1)
            dve.wait_ge(S["w0c_ready"], 1)
            dve.tensor_copy(T["w0c"][:, :], T["psT"][:, 0:TAPS0]).then_inc(S["w0c_copied"], 1)
            dve.wait_ge(S["gram_done"], 1)
            dve.tensor_copy(T["gram"][:, :], T["psT"][0:TAPS0, 16:16 + TAPS0]).then_inc(S["gram_ready"], 1)

        @block.tensor
        def _(pe):
            pe.wait_ge(S["ident_ready"], 1)
            pe.wait_ge(S["w0_centred"], 1)
            pe.transpose(T["psT"][:, 0:TAPS0], T["w0T"][:, :], T["ident"][0:TAPS0, 0:TAPS0])\
                .then_inc(S["w0c_ready"], 1)
            pe.wait_ge(S["w0c_copied"], 1)
            pe.matmul(T["psT"][0:TAPS0, 16:16 + TAPS0], T["w0c"][:, :], T["w0c"][:, :], start=True, stop=True)\
                .then_inc(S["gram_done"], 1)
        @block.scalar
        def _(act):
            act.wait_ge(S["ident_ready"], 1)
            act.activation(T["identb"][:, :], T["ident"][:, :], ACT.Copy).then_inc(S["identb_ready"], 1)


def x_chunk(io, c):
    return bass.AP(io["x"].tensor, io["x"].offset + c * STEP, [[STEP // P, P], [1, WIN]])


def stream(nc, T, S, io):
    lbuf = {0: T["l0"], 1: T["l1"], 2: T["l2"], 3: T["l3"]}
    psY, psT, psL, psPX = T["psY"], T["psT"], T["psL"], T["psPX"]
    psPb = psPX[:, :].bitcast(BF16)
    xs, p60, p60T = T["xs"], T["p60"], T["p60T"]
    patches = view(xs[:, :], [[STRIDE0, POS], [1, TAPS0]])

    def count(j, g):
        return (j + 1) * NG + g + 1

    def event(j, g):
        return GROUPS[g] + (BANK[g], g % 2, count(j, g), 256 * j)

    END = (CHUNKS + 1) * NG
    TAIL = [(4, 0, 0, 0, END + 1, 256 * CHUNKS), (3, 0, 1, 1, END + 2, 0), (4, 0, 0, 0, END + 3, 256 * (CHUNKS + 1))]

    def tiles(layer):
        return 2 if layer == 4 else 4

    NEEDS = {2: (5, 1), 5: (7, 1), 6: (1, 0), 7: (4, 0)}

    def conv(pe, j, g):
        layer = GROUPS[g][0]
        if BEFORE[g] < g:
            pe.wait_ge(S["normed"], count(j, BEFORE[g]))
        else:
            pe.wait_ge(S["normed"], count(j - 1, BEFORE[g]))
        if layer == 1:
            if g == 0:
                pe.wait_ge(S["l0_ready"], 8 * (j + 1))
        else:
            need, back = NEEDS[g]
            pe.wait_ge(S["h_ready"], count(j - back, need))
        products(pe, event(j, g))

    def products(pe, e):
        layer, half, bank, _, _, _ = e
        src = lbuf[INPUT_OF[layer]]
        for t in range(tiles(layer)):
            for k in range(3):
                at = 2 * (512 * half + P * t) + k
                mm = pe.matmul(psY[bank][:, t * C:(t + 1) * C], src[:, at:at + 2 * P - 1:2],
                               T["wt"][:, 3 * (layer - 1) + k, :], start=(k == 0), stop=(k == 2))
        mm.then_inc(S["conv_done"], 1)

    def transposes(pe, e):
        layer, _, _, par, number, _ = e
        pe.wait_ge(S["normed"], number)
        pe.wait_ge(S["h_ready"], number - 1)
        for t in range(tiles(layer)):
            mm = pe.transpose(psT[:, t * P:(t + 1) * P], T["yn"][:, par, t * C:(t + 1) * C], T["ident"][:, :])
        mm.then_inc(S["turned"], 1)

    def patch_transposes(pe, c, half):
        pe.wait_ge(S["patch_ready"], c + 1)
        if half == 0:
            pe.wait_ge(S["zz_done"], c + 1)
        else:
            pe.wait_ge(S["patch_copied"], 2 * c + 1)
        for n in range(8):
            q = 8 * half + n
            mm = pe.transpose(psPb[0:2 * ROWS, n * P:(n + 1) * P],
                              p60[:, 2 * q:2 * q + 2, :].rearrange("p a r -> p (a r)"), T["identb"][:, :])
        mm.then_inc(S["patch_turned"], 1)

    def window_transposes(pe, c):
        pe.wait_ge(S["x_loaded"], 16 * (c + 1))
        pe.wait_ge(S["patch_copied"], 2 * c)
        for h in range(2):
            at = h * STRIDE0 * HALF
            mm = pe.transpose(psPX[0:WINH, h * P:(h + 1) * P], xs[:, at:at + WINH], T["ident"][:, :])
        mm.then_inc(S["window_turned"], 1)

    def gram_product(pe, c):
        pe.wait_ge(S["window_copied"], c + 1)
        for h in range(2):
            mm = pe.matmul(psPX[:, h * HALF * TAPS0:(h + 1) * HALF * TAPS0], T["xT"][0:WINH, h, :],
                           T["band"][0:WINH, :], start=True, stop=True)
        mm.then_inc(S["gram_applied"], 1)

    def layer0(pe, c, i):
        if i == 0:
            pe.wait_ge(S["patch_copied"], 2 * (c + 1))
        if not isinstance(c, int) or 8 * c + i >= 2:
            pe.wait_ge(S["l0_ready"], 8 * c + i - 1)
        q, slot = i // 2, i % 2
        pe.matmul(psL[i % 2][:, :], T["w60"][:, slot, :],
                  p60T[:, 4 * q:4 * q + 4, :].rearrange("r a p -> r (a p)"),
                  start=True, stop=True).then_inc(S["l0_done"], 1)

    def square(act, e):
        layer, _, bank, par, number, _ = e
        n = tiles(layer) * C
        act.wait_ge(S["conv_done"], number)
        act.wait_ge(S["summed"], number - 2)
        act.activation(T["sq"][:, par, 0:n], psY[bank][:, 0:n], ACT.Square).then_inc(S["squared"], 1)

    def gelu(act, e, carry=None):
        layer, half, _, _, number, column = e
        n = tiles(layer) * P
        act.wait_ge(S["turned"], number)
        if half == 0 and layer < 4:
            buf = lbuf[layer]
            act.wait_ge(S["h_ready"], number - 1)
            act.activation(buf[:, 0:1], buf[:, buf.shape[1] - 1:buf.shape[1]], ACT.Copy)\
                .then_inc(S[f"carried{layer}"], 1)
            act.wait_ge(S[f"carried{layer}"], carry)
        if layer == 4:
            dst = T["l4"][:, bass.ds(column, n)]
        else:
            dst = lbuf[layer][:, 1 + 512 * half:1 + 512 * half + n]
        act.activation(dst, psT[:, 0:n], ACT.Gelu, bias=T["cols"][:, 8 + layer:9 + layer],
                       scale=T["cols"][:, layer:layer + 1]).then_inc(S["h_ready"], 1)

    def gelu0(act, c, i):
        if i == 0:
            if not (isinstance(c, int) and c == 0):
                act.wait_ge(S["l0_ready"], 8 * c)
            act.wait_ge(S["l0_done"], 8 * c + 1)
            act.activation(T["l0"][:, 0:2], T["l0"][:, CHUNK:CHUNK + 2], ACT.Copy).then_inc(S["carried0"], 1)
            act.wait_ge(S["carried0"], c + 1)
        act.wait_ge(S["l0_done"], 8 * c + i + 1)
        q, slot = i // 2, i % 2
        act.activation(view(T["l0"][:, :], [[2, 4], [POS, P]], 2 + 8 * q + slot),
                       psL[i % 2][:, :].rearrange("c (a p) -> c a p", a=4), ACT.Gelu,
                       bias=T["cols"][:, 8:9], scale=T["cols"][:, 0:1]).then_inc(S["l0_ready"], 1)

    def stats(dve, e):
        layer, _, _, par, number, _ = e
        n = tiles(layer)
        dve.wait_ge(S["squared"], number)
        dve.reduce_sum(T["ss"][:, par, 0:n], T["sq"][:, par, 0:n * C].rearrange("p (t c) -> p t c", c=C), axis=AX.X)\
            .then_inc(S["summed"], 1)
        dve.wait_ge(S["summed"], number)
        dve.tensor_scalar(T["var"][:, par, 0:n], T["ss"][:, par, 0:n], 1.0 / C, EPS, ALU.mult, ALU.add)\
            .then_inc(S["var_ready"], 1)

    def normalise(dve, e):
        layer, _, bank, par, number, _ = e
        n = tiles(layer)
        dve.wait_ge(S["rstd_ready"], number)
        dve.wait_ge(S["turned"], number - 2)
        dve.tensor_tensor(T["yn"][:, par, 0:n * C].rearrange("p (t c) -> p t c", c=C),
                          psY[bank][:, 0:n * C].rearrange("p (t c) -> p t c", c=C),
                          bcast(T["rstd"][:, par, 0:n], C), ALU.mult).then_inc(S["normed"], 1)

    def copy_patches(dve, c, half):
        dve.wait_ge(S["patch_turned"], 2 * c + half + 1)
        if not (isinstance(c, int) and c == 0):
            dve.wait_ge(S["l0_done"], 8 * c)
        dve.tensor_copy(p60T[:, 8 * half:8 * half + 8, :].rearrange("r a p -> r (a p)"), psPb[0:2 * ROWS, :])\
            .then_inc(S["patch_copied"], 1)

    def copy_windows(dve, c):
        dve.wait_ge(S["window_turned"], c + 1)
        dve.tensor_copy(T["xT"][0:WINH, :, :].rearrange("r a p -> r (a p)"), psPX[0:WINH, 0:2 * P])\
            .then_inc(S["window_copied"], 1)

    def patch_stats(dve, c):
        dve.wait_ge(S["gram_applied"], c + 1)
        dve.tensor_tensor(T["zz"][:, :, :], psPX[:, 0:POS * TAPS0].rearrange("p (a k) -> p a k", k=TAPS0),
                          patches, ALU.mult).then_inc(S["zz_done"], 1)
        dve.wait_ge(S["zz_done"], c + 2)
        dve.reduce_sum(T["zs"][:, :], T["zz"][:, :, :], axis=AX.X).then_inc(S["zsum"], 1)
        dve.wait_ge(S["zsum"], c + 1)
        dve.tensor_scalar(T["zvar"][:, :], T["zs"][:, :], 1.0 / C, EPS, ALU.mult, ALU.add)\
            .then_inc(S["zvar_ready"], 1)

    def split_patches(dve, c, part):
        def at(n):
            return p60[:, :, n * TAPS0:(n + 1) * TAPS0]
        high, middle, low = ([n for n, (a, _) in enumerate(SPLIT) if a == want] for want in range(3))
        if part == 0:
            dve.wait_ge(S["zrstd_ready"], 4 * (c + 1))
            dve.tensor_tensor(T["scaled"][:, :, :], patches, bcast(T["zrstd"][:, :], TAPS0), ALU.mult)\
                .then_inc(S["scaled_ready"], 1)
            dve.wait_ge(S["scaled_ready"], 5 * c + 1)
            if not (isinstance(c, int) and c == 0):
                dve.wait_ge(S["patch_turned"], 2 * c)
            dve.tensor_copy(at(high[0]), T["scaled"][:, :, :]).then_inc(S["scaled_ready"], 1)
            dve.wait_ge(S["scaled_ready"], 5 * c + 2)
            dve.tensor_tensor(T["rest"][:, :, :], T["scaled"][:, :, :], at(high[0]), ALU.subtract)\
                .then_inc(S["scaled_ready"], 1)
            dve.wait_ge(S["scaled_ready"], 5 * c + 3)
            dve.tensor_copy(at(middle[0]), T["rest"][:, :, :]).then_inc(S["scaled_ready"], 1)
        else:
            dve.wait_ge(S["scaled_ready"], 5 * c + 4)
            dve.tensor_tensor(at(low[0]), T["rest"][:, :, :], at(middle[0]), ALU.subtract)
            for n in high[1:]:
                dve.tensor_copy(at(n), at(high[0]))
            dve.tensor_copy(at(middle[1]), at(middle[0])).then_inc(S["scaled_ready"], 1)
            dve.wait_ge(S["scaled_ready"], 5 * c + 5)
            dve.nop().then_inc(S["patch_ready"], 1)

    def root(pool, e):
        layer, _, _, par, number, _ = e
        n = tiles(layer)
        pool.wait_ge(S["var_ready"], number)
        pool.wait_ge(S["normed"], number - 2)
        pool.tensor_tensor(T["rstd"][:, par, 0:n], T["var"][:, par, 0:n], T["minus_half"][:, 0:n], ALU.pow)\
            .then_inc(S["rstd_ready"], 1)

    def patch_root(pool, c, part):
        pool.wait_ge(S["zvar_ready"], c + 1)
        s = slice(part * POS // 4, (part + 1) * POS // 4)
        pool.tensor_tensor(T["zrstd"][:, s], T["zvar"][:, s], T["minus_half"][:, 0:POS // 4], ALU.pow)\
            .then_inc(S["zrstd_ready"], 1)

    with nc.Block() as block:
        @block.sync
        def _(sp):
            def load(c):
                sp.wait_ge(S["scaled_ready"], 5 * c - 4)
                sp.dma_start(xs[:, :], x_chunk(io, c)).then_inc(S["x_loaded"], 16)
            load(1)
            load(2)
            with sp.Fori(0, CHUNKS) as j:
                load(j + 3)
            sp.wait_ge(S["x_loaded"], 16 * (CHUNKS + 3))

        @block.tensor
        def _(pe):
            pe.wait_ge(S["w60_loaded"], 16 * 2 * PARTS)
            pe.wait_ge(S["band_loaded"], 16 * HALF)
            for c in range(2):
                window_transposes(pe, c)
                gram_product(pe, c)
                if c == 0:
                    patch_transposes(pe, 0, 0)
                    patch_transposes(pe, 0, 1)
                    for i in range(8):
                        layer0(pe, 0, i)
            with pe.Fori(0, CHUNKS) as j:
                for g in range(NG):
                    conv(pe, j, g)
                    transposes(pe, event(j if g >= LAG else j - 1, (g - LAG) % NG))
                    if g == 1:
                        patch_transposes(pe, j + 1, 0)
                    if g == 2:
                        patch_transposes(pe, j + 1, 1)
                    if g == 3:
                        window_transposes(pe, j + 2)
                    if g == 4:
                        gram_product(pe, j + 2)
                    for i in L0_AFTER.get(g, ()):
                        layer0(pe, j + 1, i)
            transposes(pe, event(CHUNKS - 1, 6))
            transposes(pe, event(CHUNKS - 1, 7))
            for n, e in enumerate(TAIL):
                pe.wait_ge(S["h_ready"], END + n)
                products(pe, e)
                transposes(pe, e)

        @block.scalar
        def _(act):
            for i in range(8):
                gelu0(act, 0, i)
            with act.Fori(0, CHUNKS) as j:
                for g in range(NG):
                    square(act, event(j, g))
                    back = 0 if g >= LAG else 1
                    gelu(act, event(j - back, (g - LAG) % NG), j - back + (2 if (g - LAG) % NG == 6 else 1))
                    for i in L0_AFTER.get(g, ()):
                        gelu0(act, j + 1, i)
            gelu(act, event(CHUNKS - 1, 6), CHUNKS + 1)
            gelu(act, event(CHUNKS - 1, 7))
            for e in TAIL:
                square(act, e)
                gelu(act, e, CHUNKS + 1)

        @block.vector
        def _(dve):
            for name, n in (("normed", NG), ("turned", NG - LAG), ("h_ready", NG - LAG), ("summed", NG),
                            ("squared", NG), ("var_ready", NG), ("rstd_ready", NG), ("conv_done", NG), ("zz_done", 1)):
                dve.sem_inc(S[name], n)
            for c in range(2):
                copy_windows(dve, c)
                patch_stats(dve, c)
                split_patches(dve, c, 0)
                split_patches(dve, c, 1)
                if c == 0:
                    copy_patches(dve, 0, 0)
                    copy_patches(dve, 0, 1)
            with dve.Fori(0, CHUNKS) as j:
                for g in range(NG):
                    stats(dve, event(j, g))
                    if g == 1:
                        copy_patches(dve, j + 1, 0)
                    if g == 2:
                        copy_patches(dve, j + 1, 1)
                    if g == 3:
                        copy_windows(dve, j + 2)
                    normalise(dve, event(j, g))
                    if g == 4:
                        patch_stats(dve, j + 2)
                    if g == 6:
                        split_patches(dve, j + 2, 0)
                    if g == 7:
                        split_patches(dve, j + 2, 1)
            for e in TAIL:
                stats(dve, e)
                normalise(dve, e)

        @block.gpsimd
        def _(pool):
            for c in range(2):
                for part in range(4):
                    patch_root(pool, c, part)
            with pool.Fori(0, CHUNKS) as j:
                for g in range(NG):
                    root(pool, event(j, g))
                    if g == 4:
                        patch_root(pool, j + 2, 0)
                        patch_root(pool, j + 2, 1)
                    if g == 5:
                        patch_root(pool, j + 2, 2)
                        patch_root(pool, j + 2, 3)
            for e in TAIL:
                root(pool, e)


D = 192
D1, D2 = 128, D - 128
LEN = 374
TOK = 125
TPB = 3
SEQ = TOK * TPB
TILES = B * TPB
N_EXPERT, HID = 4, 768
HC = HID // P
SOFT_E, SLOT, SOFT_H = 64, 16, 384
SLOTS = SOFT_E * SLOT
SC = SLOTS // P
SHC = SOFT_H // P


class Link:

    def __init__(self, eng, sem, per_round=0, round_=0):
        self.eng, self.sem, self.base, self.n = eng, sem, round_ * per_round, 0

    def __call__(self, ins):
        self.n += 1
        ins.then_inc(self.sem, 1)
        self.eng.wait_ge(self.sem, self.base + self.n)


def layers56(nc, T, S):
    psY, psT = [T["psY"][0], T["psY"][1]], T["psT"]

    def run(layer, groups, src, src_at, dst, sem):
        gap = 2 * SEQ
        s = {k: S[f"{k}{layer}"] for k in ("in", "conv", "sq", "sum", "var", "rstd", "norm", "turn", "out")}
        with nc.Block() as block:
            @block.tensor
            def _(pe):
                def turn(g):
                    pe.wait_ge(s["norm"], g + 1)
                    if g >= 1:
                        pe.wait_ge(s["out"], g)
                    for t in range(TPB):
                        mm = pe.transpose(psT[:, t * TOK:(t + 1) * TOK], T["yn"][0:TOK, g % 2, t * C:(t + 1) * C],
                                          T["ident"][0:TOK, 0:TOK])
                    mm.then_inc(s["turn"], 1)
                for g in range(groups):
                    pe.wait_ge(s["in"], g + 1)
                    if g >= 2:
                        pe.wait_ge(s["norm"], g - 1)
                    for t in range(TPB):
                        for k in range(2):
                            at = 2 * TOK * t + k
                            mm = pe.matmul(psY[g % 2][0:TOK, t * C:(t + 1) * C],
                                           T["stage"][:, g % 2, at:at + 2 * TOK - 1:2],
                                           T["wt"][:, 12 + 2 * (layer - 5) + k, :], start=(k == 0), stop=(k == 1))
                    mm.then_inc(s["conv"], 1)
                    if g >= 1:
                        turn(g - 1)
                turn(groups - 1)

            @block.scalar
            def _(act):
                def gelu(g):
                    act.wait_ge(s["turn"], g + 1)
                    act.activation(T[dst][:, g * SEQ:(g + 1) * SEQ], psT[:, 0:SEQ], ACT.Gelu,
                                   bias=T["cols"][:, 8 + layer:9 + layer],
                                   scale=T["cols"][:, layer:layer + 1]).then_inc(s["out"], 1)
                for g in range(groups):
                    act.wait_ge(s["conv"], g + 1)
                    if g >= 2:
                        act.wait_ge(s["sum"], g - 1)
                    act.activation(T["sq"][0:TOK, g % 2, 0:TPB * C], psY[g % 2][0:TOK, 0:TPB * C], ACT.Square)\
                        .then_inc(s["sq"], 1)
                    if g >= 1:
                        gelu(g - 1)
                gelu(groups - 1)

            @block.vector
            def _(dve):
                def place(g):
                    if g >= 2:
                        dve.wait_ge(s["conv"], g - 1)
                    dve.tensor_copy(T["stage"][:, g % 2, 0:gap], T[src][:, src_at + g * gap:src_at + (g + 1) * gap])\
                        .then_inc(s["in"], 1)
                place(0)
                for g in range(groups):
                    if g + 1 < groups:
                        place(g + 1)
                    dve.wait_ge(s["sq"], g + 1)
                    dve.reduce_sum(T["ss"][0:TOK, g % 2, 0:TPB],
                                   T["sq"][0:TOK, g % 2, 0:TPB * C].rearrange("p (t c) -> p t c", c=C), axis=AX.X)\
                        .then_inc(s["sum"], 1)
                    dve.wait_ge(s["sum"], g + 1)
                    dve.tensor_scalar(T["var"][0:TOK, g % 2, 0:TPB], T["ss"][0:TOK, g % 2, 0:TPB], 1.0 / C, EPS,
                                      ALU.mult, ALU.add).then_inc(s["var"], 1)
                    dve.wait_ge(s["rstd"], g + 1)
                    if g >= 2:
                        dve.wait_ge(s["turn"], g - 1)
                    dve.tensor_tensor(T["yn"][0:TOK, g % 2, 0:TPB * C].rearrange("p (t c) -> p t c", c=C),
                                      psY[g % 2][0:TOK, 0:TPB * C].rearrange("p (t c) -> p t c", c=C),
                                      bcast(T["rstd"][0:TOK, g % 2, 0:TPB], C), ALU.mult).then_inc(s["norm"], 1)

            @block.gpsimd
            def _(pool):
                for g in range(groups):
                    pool.wait_ge(s["var"], g + 1)
                    if g >= 2:
                        pool.wait_ge(s["norm"], g - 1)
                    pool.tensor_tensor(T["rstd"][0:TOK, g % 2, 0:TPB], T["var"][0:TOK, g % 2, 0:TPB],
                                       T["minus_half"][0:TOK, 0:TPB], ALU.pow).then_inc(s["rstd"], 1)

    run(5, 2 * B, "l4", 513, "l5", "l5_ready")
    run(6, B, "l5", 0, "l6", "l6_ready")


def norm_stats(dve, T, S, link, k, get, width):
    for t in range(TPB):
        ins = dve.bn_stats(T["bn"][0:TOK, t, :], get(t))
    link(ins)
    for t in range(TPB):
        ins = dve.bn_aggr(T["mv"][0:TOK, t, :], T["bn"][0:TOK, t, :])
    link(ins)
    dve.tensor_scalar(T["nvar"][0:TOK, 0:TPB], T["mv"][0:TOK, :, 1], EPS, None, ALU.add).then_inc(S["nvar"], 1)
    dve.wait_ge(S["nroot"], k + 1)


def norm_root(pool, T, S, k):
    pool.wait_ge(S["nvar"], k + 1)
    pool.tensor_tensor(T["nrstd"][0:TOK, 0:TPB], T["nvar"][0:TOK, 0:TPB], T["minus_half"][0:TOK, 0:TPB], ALU.pow)\
        .then_inc(S["nroot"], 1)


def norm_apply(dve, T, get, out):
    for t in range(TPB):
        ins = dve.tensor_scalar(out(t), get(t), T["mv"][0:TOK, t, 0:1], T["nrstd"][0:TOK, t:t + 1],
                                ALU.subtract, ALU.mult)
    return ins


def htile(T, b, t):
    return T["h"][0:TOK, TPB * b + t, :]


def tokens(nc, T, S):
    pA, pB, pC, pD = T["ps"][0], T["ps"][1], T["ps"][2], T["ps"][3]
    nTok, nCh = T["tA"], T["tB"]
    with nc.Block() as block:
        @block.tensor
        def _(pe):
            for b in range(B):
                if b >= 1:
                    pe.wait_ge(S["tok_normed"], b)
                for t in range(TPB):
                    mm = pe.transpose(pA[0:TOK, t * C:(t + 1) * C],
                                      T["l6"][:, b * SEQ + t * TOK:b * SEQ + (t + 1) * TOK], T["ident"][:, :])
                mm.then_inc(S["tok_turned"], 1)
                pe.wait_ge(S["tok_normed"], b + 1)
                if b >= 1:
                    pe.wait_ge(S["tok_affine"], b)
                for t in range(TPB):
                    mm = pe.transpose(pB[:, t * TOK:(t + 1) * TOK], nTok[0:TOK, t * C:(t + 1) * C],
                                      T["ident"][0:TOK, 0:TOK])
                mm.then_inc(S["tok_back"], 1)
                pe.wait_ge(S["tok_affine"], b + 1)
                if b >= 1:
                    pe.wait_ge(S["tok_out"], b)
                for t in range(TPB):
                    mm = pe.matmul((pC[0:TOK, t * D:(t + 1) * D] if t < 2 else pD[0:TOK, 0:D]),
                                   nCh[:, t * TOK:(t + 1) * TOK], T["proj_w"][:, :], start=True, stop=True)
                mm.then_inc(S["tok_projected"], 1)

        @block.vector
        def _(dve):
            for b in range(B):
                link = Link(dve, S["tok_link"], 2, b)
                dve.wait_ge(S["tok_turned"], b + 1)
                get = lambda t: pA[0:TOK, t * C:(t + 1) * C]
                norm_stats(dve, T, S, link, b, get, C)
                norm_apply(dve, T, get, lambda t: nTok[0:TOK, t * C:(t + 1) * C]).then_inc(S["tok_normed"], 1)
                dve.wait_ge(S["tok_projected"], b + 1)
                for t in range(TPB):
                    ins = dve.tensor_tensor(htile(T, b, t), pC[0:TOK, t * D:(t + 1) * D] if t < 2 else pD[0:TOK, 0:D],
                                            T["rows"][0:TOK, 0, :], ALU.add)
                ins.then_inc(S["tok_out"], 1)

        @block.gpsimd
        def _(pool):
            for b in range(B):
                norm_root(pool, T, S, b)

        @block.scalar
        def _(act):
            for b in range(B):
                act.wait_ge(S["tok_back"], b + 1)
                act.activation(nCh[:, 0:SEQ], pB[:, 0:SEQ], ACT.Identity, bias=T["cols"][:, 15:16],
                               scale=T["cols"][:, 7:8]).then_inc(S["tok_affine"], 1)


def ssm_tables(nc, T, S):
    v = T["sv"]
    names = ("dt are r th k y cos sin nr ni dr di q0 q1 q2 qr qi cm sm c2 s2 tmp ay").split()
    col = {n: v[:, i:i + 1] for i, n in enumerate(names)}
    logA, Aim, logdt = (T["cols"][:, 16 + i:17 + i] for i in range(3))
    TWO_PI = 6.283185307179586
    C1 = 6.28125
    C2 = 0.0019340515136718750
    C3 = TWO_PI - C1 - C2
    MAGIC = 12582912.0
    steps = LEN
    with nc.Block() as block:
        @block.scalar
        def _(act):
            act.activation(col["dt"], logdt, ACT.Exp)
            act.activation(col["are"], logA, ACT.Exp).then_inc(S["ssm_exp"], 1)
            act.wait_ge(S["ssm_r"], 1)
            act.activation(col["r"], col["nr"], ACT.Exp, scale=-1.0).then_inc(S["ssm_exp"], 1)
            act.wait_ge(S["ssm_angle"], 1)
            act.activation(col["sin"], col["y"], ACT.Sin)
            act.activation(col["cos"], col["ay"], ACT.Sin).then_inc(S["ssm_exp"], 1)

        @block.vector
        def _(dve):
            link = Link(dve, S["ssm_link"])
            tt = lambda o, a, b_, op: link(dve.tensor_tensor(o, a, b_, op))
            ts = lambda o, a, s1, s2, op0, op1=ALU.bypass: link(dve.tensor_scalar(o, a, s1, s2, op0, op1))
            stt = lambda o, a, s, b_, op0, op1: link(dve.scalar_tensor_tensor(out=o, in0=a, scalar=s, in1=b_, op0=op0, op1=op1))
            dve.wait_ge(S["ssm_exp"], 1)
            dve.tensor_tensor(col["nr"], col["are"], col["dt"], ALU.mult).then_inc(S["ssm_r"], 1)
            tt(col["th"], Aim, col["dt"], ALU.mult)
            ts(col["k"], col["th"], 1.0 / TWO_PI, None, ALU.mult)
            ts(col["k"], col["k"], MAGIC, None, ALU.add)
            ts(col["k"], col["k"], MAGIC, None, ALU.subtract)
            stt(col["y"], col["k"], -C1, col["th"], ALU.mult, ALU.add)
            stt(col["y"], col["k"], -C2, col["y"], ALU.mult, ALU.add)
            stt(col["y"], col["k"], -C3, col["y"], ALU.mult, ALU.add)
            ts(col["y"], col["y"], 3.1415925, -3.1415925, ALU.min, ALU.max)
            ts(col["tmp"], col["y"], -1.0, None, ALU.mult)
            tt(col["ay"], col["y"], col["tmp"], ALU.max)
            dve.tensor_scalar(col["ay"], col["ay"], -1.0, TWO_PI / 4, ALU.mult, ALU.add).then_inc(S["ssm_angle"], 1)
            dve.wait_ge(S["ssm_exp"], 3)
            tt(col["nr"], col["r"], col["cos"], ALU.mult)
            ts(col["nr"], col["nr"], -1.0, None, ALU.add)
            tt(col["ni"], col["r"], col["sin"], ALU.mult)
            ts(col["dr"], col["are"], -1.0, 1e-8, ALU.mult, ALU.add)
            tt(col["q0"], col["dr"], col["dr"], ALU.mult)
            tt(col["q1"], Aim, Aim, ALU.mult)
            tt(col["q0"], col["q0"], col["q1"], ALU.add)
            link(dve.reciprocal(col["q0"], col["q0"]))
            tt(col["qr"], col["ni"], Aim, ALU.mult)
            stt(col["qr"], col["nr"], col["dr"], col["qr"], ALU.mult, ALU.add)
            tt(col["qr"], col["qr"], col["q0"], ALU.mult)
            tt(col["qi"], col["nr"], Aim, ALU.mult)
            stt(col["qi"], col["ni"], col["dr"], col["qi"], ALU.mult, ALU.subtract)
            tt(col["qi"], col["qi"], col["q0"], ALU.mult)
            Cr, Ci, Wr, Wi = T["CT"][:, 0, :], T["CT"][:, 1, :], T["Cq"][:, 0, :], T["Cq"][:, 1, :]
            ts(Wr, Ci, col["qi"], None, ALU.mult)
            stt(Wr, Cr, col["qr"], Wr, ALU.mult, ALU.subtract)
            ts(Wi, Cr, col["qi"], -1.0, ALU.mult, ALU.mult)
            ts(T["Ctmp"][:, :], Ci, col["qr"], None, ALU.mult)
            tt(Wi, Wi, T["Ctmp"][:, :], ALU.subtract)
            cos, sin = T["cosT"], T["sinT"]
            link(dve.memset(cos[:, 0:1], 1.0))
            link(dve.memset(sin[:, 0:1], 0.0))
            ts(col["cm"], col["cos"], 1.0, None, ALU.mult)
            ts(col["sm"], col["sin"], 1.0, None, ALU.mult)
            m = 1
            while m < steps:
                n = min(m, steps - m)
                ts(T["rot"][:, 0:n], sin[:, 0:n], col["sm"], None, ALU.mult)
                stt(cos[:, m:m + n], cos[:, 0:n], col["cm"], T["rot"][:, 0:n], ALU.mult, ALU.subtract)
                ts(T["rot"][:, 0:n], cos[:, 0:n], col["sm"], None, ALU.mult)
                stt(sin[:, m:m + n], sin[:, 0:n], col["cm"], T["rot"][:, 0:n], ALU.mult, ALU.add)
                tt(col["c2"], col["cm"], col["cm"], ALU.mult)
                tt(col["s2"], col["sm"], col["sm"], ALU.mult)
                ts(col["sm"], col["sm"], col["cm"], 2.0, ALU.mult, ALU.mult)
                tt(col["cm"], col["c2"], col["s2"], ALU.subtract)
                m *= 2


def state_space(nc, T, S):
    pA, pB, pR, pI = T["ps"][0], T["ps"][1], T["ps"][2], T["ps"][3]
    pO = [T["ps"][4], T["ps"][5]]
    u, uA, uB = T["u"], T["uA"], T["uB"]
    cos, sin = T["cosT"][:, 0:LEN], T["sinT"][:, 0:LEN]
    decay = view(T["sv"][:, 2:3], [[0, LEN]])
    m1, m2, vr, vi, gr, gi, xr, xi = (T["seq"][:, i, 0:LEN] for i in range(8))
    with nc.Block() as block:
        @block.tensor
        def _(pe):
            for b in range(B):
                pe.wait_ge(S["u_ready"], b + 1)
                if b >= 1:
                    pe.wait_ge(S["uT_ready"], 2 * b)
                for t in range(TPB):
                    pe.transpose(pA[:, t * TOK:(t + 1) * TOK], u[0:TOK, b % 2, t, 0:D1], T["ident"][0:TOK, 0:TOK])
                    mm = pe.transpose(pB[0:D2, t * TOK:(t + 1) * TOK], u[0:TOK, b % 2, t, D1:D],
                                      T["ident"][0:TOK, 0:TOK])
                mm.then_inc(S["u_turned"], 1)
                pe.wait_ge(S["uT_ready"], 2 * (b + 1))
                if b >= 1:
                    pe.wait_ge(S["ssm_in"], b)
                for part, dst in ((0, pR), (1, pI)):
                    pe.matmul(dst[:, 0:LEN], T["BTa"][:, part, :], uA[:, 0:LEN], start=True, stop=False)
                    mm = pe.matmul(dst[:, 0:LEN], T["BTb"][:, part, :], uB[:, 0:LEN], start=False, stop=True)
                mm.then_inc(S["Bu_ready"], 1)
                pe.wait_ge(S["x_ready"], b + 1)
                if b >= 1:
                    pe.wait_ge(S["ssm_out"], b)
                for t in range(TPB):
                    n = min(TOK, LEN - t * TOK)
                    o = pO[t // 2][0:n, (t % 2) * D:(t % 2 + 1) * D]
                    pe.matmul(o, xr[:, t * TOK:t * TOK + n], T["Cq"][:, 0, :], start=True, stop=False)
                    mm = pe.matmul(o, xi[:, t * TOK:t * TOK + n], T["Cq"][:, 1, :], start=False, stop=True)
                mm.then_inc(S["y_ready"], 1)

        @block.scalar
        def _(act):
            for b in range(B):
                act.wait_ge(S["u_turned"], b + 1)
                if b >= 1:
                    act.wait_ge(S["Bu_ready"], b)
                act.activation(uA[:, 0:SEQ], pA[:, 0:SEQ], ACT.Copy).then_inc(S["uT_ready"], 1)
                act.activation(uB[:, 0:SEQ], pB[0:D2, 0:SEQ], ACT.Copy).then_inc(S["uT_ready"], 1)

        @block.gpsimd
        def _(pool):
            for b in range(B):
                norm_root(pool, T, S, B + b)

        @block.vector
        def _(dve):
            def norm(b):
                link = Link(dve, S["ssm_nlink"], 2, b)
                norm_stats(dve, T, S, link, B + b, lambda t: htile(T, b, t), D)
                norm_apply(dve, T, lambda t: htile(T, b, t), lambda t: u[0:TOK, b % 2, t, :]).then_inc(S["u_ready"], 1)
            norm(0)
            for b in range(B):
                if b + 1 < B:
                    norm(b + 1)
                dve.wait_ge(S["Bu_ready"], b + 1)
                link = Link(dve, S["ssm_slink"], 9, b)
                R, I = pR[:, 0:LEN], pI[:, 0:LEN]
                tt = lambda o, a, b_, op: dve.tensor_tensor(o, a, b_, op)
                tt(m1, R, cos, ALU.mult)
                link(tt(m2, I, sin, ALU.mult))
                link(tt(vr, m1, m2, ALU.add))
                tt(m1, I, cos, ALU.mult)
                ins = tt(m2, R, sin, ALU.mult)
                link(ins)
                dve.nop().then_inc(S["ssm_in"], 1)
                link(tt(vi, m1, m2, ALU.subtract))
                dve.tensor_tensor_scan(gr, decay, vr, 0.0, ALU.mult, ALU.add)
                link(dve.tensor_tensor_scan(gi, decay, vi, 0.0, ALU.mult, ALU.add))
                tt(m1, gr, cos, ALU.mult)
                link(tt(m2, gi, sin, ALU.mult))
                if b >= 1:
                    dve.wait_ge(S["y_ready"], b)
                link(tt(xr, m1, m2, ALU.subtract))
                tt(m1, gi, cos, ALU.mult)
                link(tt(m2, gr, sin, ALU.mult))
                link(tt(xi, m1, m2, ALU.add))
                dve.nop().then_inc(S["x_ready"], 1)
                ub = u[0:TOK, b % 2, :, :]
                hb = T["h"][0:TOK, TPB * b:TPB * (b + 1), :]
                Drow = view(T["rows"][0:TOK, 1, :], [[0, TPB], [1, D]])
                tt(T["uD"][0:TOK, :, :], ub, Drow, ALU.mult).then_inc(S["ssm_blink"], 1)
                dve.wait_ge(S["ssm_blink"], 2 * b + 1)
                tt(hb, hb, T["uD"][0:TOK, :, :], ALU.add).then_inc(S["ssm_blink"], 1)
                dve.wait_ge(S["ssm_blink"], 2 * b + 2)
                dve.wait_ge(S["y_ready"], b + 1)
                for t in range(TPB):
                    n = min(TOK, LEN - t * TOK)
                    ins = tt(htile(T, b, t)[0:n], htile(T, b, t)[0:n], pO[t // 2][0:n, (t % 2) * D:(t % 2 + 1) * D],
                             ALU.add)
                ins.then_inc(S["ssm_out"], 1)


def turn_tiles(pe, T, src, b, pA, pB):
    for t in range(TPB):
        pe.transpose(pA[:, t * TOK:(t + 1) * TOK], src[0:TOK, b % 2, t, 0:D1], T["ident"][0:TOK, 0:TOK])
        mm = pe.transpose(pB[0:D2, t * TOK:(t + 1) * TOK], src[0:TOK, b % 2, t, D1:D], T["ident"][0:TOK, 0:TOK])
    return mm


def routed_ffn(nc, T, S):
    ps = T["ps"]
    pA, pB, pG, pH, pO = ps[0], ps[1], ps[2], [ps[3], ps[4]], [ps[5], ps[6]]
    v, vA, vB, G = T["u"], T["vA"], T["vB"], T["G"]
    CH = N_EXPERT * HC
    OUTS = N_EXPERT + 1
    with nc.Block() as block:
        @block.tensor
        def _(pe):
            def turn(b):
                pe.wait_ge(S["v_ready"], b + 1)
                if b >= 1:
                    pe.wait_ge(S["vT_ready"], 2 * b)
                turn_tiles(pe, T, v, b, pA, pB).then_inc(S["v_turned"], 1)

            def up(b, e):
                for c in range(HC):
                    k = b * CH + e * HC + c
                    if k >= 2:
                        pe.wait_ge(S["hid_ready"], k - 1)
                    w = slice(e * HID + c * P, e * HID + (c + 1) * P)
                    pe.matmul(pH[k % 2][:, 0:SEQ], T["w1a"][:, w], vA[:, b % 2, :], start=True, stop=False)
                    pe.matmul(pH[k % 2][:, 0:SEQ], T["w1b"][:, w], vB[:, b % 2, :], start=False, stop=True)\
                        .then_inc(S["hid_done"], 1)

            def out(b, e):
                k = b * OUTS + e
                if k >= 1:
                    pe.wait_ge(S["picked"], k)
                if e == N_EXPERT:
                    pe.wait_ge(S["maskT_ready"], b + 1)
                else:
                    pe.wait_ge(S["hid_ready"], b * CH + (e + 1) * HC)
                for t in range(TPB):
                    o = pO[t // 2][0:TOK, (t % 2) * D:(t % 2 + 1) * D]
                    s = slice(t * TOK, (t + 1) * TOK)
                    if e == N_EXPERT:
                        mm = pe.matmul(o, T["maskT"][:, s], T["b2"][:, :], start=True, stop=True)
                    else:
                        for c in range(HC):
                            mm = pe.matmul(o, G[:, (e % 2) * HC + c, s], T["w2"][:, e * HC + c, :],
                                           start=(c == 0), stop=(c == HC - 1))
                mm.then_inc(S["out_done"], 1)
            turn(0)
            for b in range(B):
                pe.wait_ge(S["vT_ready"], 2 * (b + 1))
                if b >= 1:
                    pe.wait_ge(S["maskT_ready"], b)
                for t in range(TPB):
                    s = slice(t * TOK, (t + 1) * TOK)
                    o = pG[0:TOK, t * N_EXPERT:(t + 1) * N_EXPERT]
                    pe.matmul(o, vA[:, b % 2, s], T["gate_wa"][:, :], start=True, stop=False)
                    mm = pe.matmul(o, vB[:, b % 2, s], T["gate_wb"][:, :], start=False, stop=True)
                mm.then_inc(S["scores_ready"], 1)
                for e in range(N_EXPERT):
                    up(b, e)
                    if e == 1:
                        pe.wait_ge(S["mask_ready"], b + 1)
                        for t in range(TPB):
                            mm = pe.transpose(pG[0:N_EXPERT, t * TOK:(t + 1) * TOK], T["mask"][0:TOK, b % 2, t, :],
                                              T["ident"][0:TOK, 0:TOK])
                        mm.then_inc(S["mask_turned"], 1)
                    if e >= 1:
                        out(b, e - 1)
                    if e == 2 and b + 1 < B:
                        turn(b + 1)
                out(b, N_EXPERT - 1)
                out(b, N_EXPERT)

        @block.scalar
        def _(act):
            def copy(b):
                act.wait_ge(S["v_turned"], b + 1)
                if b >= 2:
                    act.wait_ge(S["hid_done"], CH * (b - 1))
                act.activation(vA[:, b % 2, :], pA[:, 0:SEQ], ACT.Copy).then_inc(S["vT_ready"], 1)
                act.activation(vB[:, b % 2, :], pB[0:D2, 0:SEQ], ACT.Copy).then_inc(S["vT_ready"], 1)
            copy(0)
            for b in range(B):
                act.wait_ge(S["z_ready"], b + 1)
                act.activation(T["ez"][0:TOK, :, :], T["z"][0:TOK, :, :], ACT.Exp).then_inc(S["ez_ready"], 1)
                for e in range(N_EXPERT):
                    for c in range(HC):
                        k = b * CH + e * HC + c
                        act.wait_ge(S["hid_done"], k + 1)
                        if k >= 2 * HC:
                            kb, ke = divmod(k // HC - 2, N_EXPERT)
                            act.wait_ge(S["out_done"], kb * OUTS + ke + 1)
                        act.activation(G[:, (e % 2) * HC + c, :], pH[k % 2][:, 0:SEQ], ACT.Gelu,
                                       bias=T["b1"][:, e * HC + c:e * HC + c + 1]).then_inc(S["hid_ready"], 1)
                    if e == 2 and b + 1 < B:
                        copy(b + 1)

        @block.gpsimd
        def _(pool):
            for b in range(B):
                norm_root(pool, T, S, 2 * B + b)

        @block.vector
        def _(dve):
            def norm(b):
                link = Link(dve, S["ffn_nlink"], 2, b)
                norm_stats(dve, T, S, link, 2 * B + b, lambda t: htile(T, b, t), D)
                if b >= 2:
                    dve.wait_ge(S["v_turned"], b - 1)
                norm_apply(dve, T, lambda t: htile(T, b, t), lambda t: v[0:TOK, b % 2, t, :]).then_inc(S["v_ready"], 1)

            def gate(b):
                z, ez, m = T["z"][0:TOK, :, :], T["ez"][0:TOK, :, :], T["mask"][0:TOK, b % 2, :, :]
                top, left = T["top"][0:TOK, :], T["left"][0:TOK, :]
                link = Link(dve, S["gate_link"], 13, b)
                dve.wait_ge(S["scores_ready"], b + 1)
                shift = view(T["gate_row"][0:TOK, 2 * N_EXPERT:3 * N_EXPERT], [[0, TPB], [1, N_EXPERT]])
                link(dve.tensor_tensor(z, pG[0:TOK, 0:TPB * N_EXPERT].rearrange("p (t e) -> p t e", e=N_EXPERT),
                                       shift, ALU.add))
                link(dve.tensor_reduce(top, z, AX.X, ALU.max))
                dve.tensor_tensor(z, z, bcast(top, N_EXPERT), ALU.subtract).then_inc(S["z_ready"], 1)
                dve.wait_ge(S["ez_ready"], b + 1)
                link(dve.reduce_sum(top, ez, axis=AX.X))
                link(dve.reciprocal(top, top))
                link(dve.tensor_tensor(ez, ez, bcast(top, N_EXPERT), ALU.mult))
                link(dve.tensor_reduce(top, ez, AX.X, ALU.max))
                link(dve.tensor_tensor(m, ez, bcast(top, N_EXPERT), ALU.is_ge))
                link(dve.tensor_scalar(left, m[:, :, 0], -1.0, 1.0, ALU.mult, ALU.add))
                for e in range(1, N_EXPERT):
                    link(dve.tensor_tensor(m[:, :, e], m[:, :, e], left, ALU.mult))
                    if e + 1 < N_EXPERT:
                        link(dve.tensor_tensor(left, left, m[:, :, e], ALU.subtract))
                dve.nop().then_inc(S["mask_ready"], 1)
                dve.wait_ge(S["mask_turned"], b + 1)
                if b >= 1:
                    dve.wait_ge(S["out_done"], OUTS * b)
                dve.tensor_copy(T["maskT"][:, :], pG[0:N_EXPERT, 0:SEQ]).then_inc(S["maskT_ready"], 1)

            dve.wait_ge(S["rows_loaded"], 16 * 2)
            dve.tensor_tensor(T["gate_row"][0:TOK, 2 * N_EXPERT:3 * N_EXPERT], T["gate_row"][0:TOK, 0:N_EXPERT],
                              T["gate_row"][0:TOK, N_EXPERT:2 * N_EXPERT], ALU.subtract).then_inc(S["shift_ready"], 1)
            dve.wait_ge(S["shift_ready"], 1)
            norm(0)
            for b in range(B):
                gate(b)
                if b + 1 < B:
                    norm(b + 1)
                for e in range(OUTS):
                    k = b * OUTS + e
                    dve.wait_ge(S["out_done"], k + 1)
                    if k >= 1:
                        dve.wait_ge(S["picked"], k)
                    for t in range(TPB):
                        o = pO[t // 2][0:TOK, (t % 2) * D:(t % 2 + 1) * D]
                        h = htile(T, b, t)
                        if e == N_EXPERT:
                            ins = dve.tensor_tensor(h, h, o, ALU.add)
                        else:
                            ins = dve.scalar_tensor_tensor(out=h, in0=o, scalar=T["mask"][0:TOK, b % 2, t, e:e + 1],
                                                           in1=h, op0=ALU.mult, op1=ALU.add)
                    ins.then_inc(S["picked"], 1)
                    dve.wait_ge(S["picked"], k + 1)


def two_way_scan(nc, T, S):
    ps = T["ps"]
    pA, pB, pX, pC, pO = ps[0], ps[1], [ps[2], ps[3]], [ps[4], ps[5], ps[6]], [ps[7], ps[1]]
    a, xh, nA, nB, xA, xB = T["u"], T["xh"], T["nA"], T["nB"], T["xA"], T["xB"]
    cols = lambda i, m: T["mcol"][:, 3 * i + m:3 * i + m + 1]
    BIAS, LOGIT, B_, C_, D_, BB, DB = range(7)
    zA, zB = T["zA"], T["zB"]
    with nc.Block() as block:
        @block.tensor
        def _(pe):
            for b in range(B):
                pe.wait_ge(S["xh_ready"], b + 1)
                if b >= 1:
                    pe.wait_ge(S["two_out"], b)
                turn_tiles(pe, T, xh, 0, pA, pB).then_inc(S["xh_turned"], 1)
                pe.wait_ge(S["n_ready"], 2 * (b + 1))
                for i in range(4):
                    k = 4 * b + i
                    if k >= 2:
                        pe.wait_ge(S["proj_read"], k - 1)
                    o = pX[k % 2][:, 0:LEN]
                    pe.matmul(o, T["Wia"][:, i, :], nA[:, 0:LEN], start=True, stop=False)
                    pe.matmul(o, T["Wib"][:, i, :], nB[:, 0:LEN], start=False, stop=True).then_inc(S["proj_done"], 1)
                pe.wait_ge(S["proj_read"], 4 * b + 2)
                for m in range(3):
                    if b >= 1:
                        pe.wait_ge(S["conv_read"], 6 * (b - 1) + 2 * (m + 1))
                    o = pC[m][:, 0:LEN]
                    for k in range(3):
                        pe.matmul(o, T["Wca"][:, k, m * P:(m + 1) * P], xA[:, k:k + LEN], start=(k == 0), stop=False)
                    pe.matmul(o, T["Wcb"][:, m * P:(m + 1) * P], xB[:, 0:LEN], start=False, stop=False)
                    pe.matmul(o, T["Wcc"][0:D2, m * P:(m + 1) * P], xB[0:D2, 2:2 + LEN], start=False, stop=True)\
                        .then_inc(S["conv2_done"], 1)
                pe.wait_ge(S["y2_ready"], b + 1)
                for t in range(TPB):
                    n = min(TOK, LEN - t * TOK)
                    o = pO[t // 2][0:n, (t % 2) * D:(t % 2 + 1) * D]
                    pe.matmul(o, T["yA"][:, t * TOK:t * TOK + n], T["Woa"][:, :], start=True, stop=False)
                    mm = pe.matmul(o, T["yB"][:, t * TOK:t * TOK + n], T["Wob"][:, :], start=False, stop=True)
                mm.then_inc(S["two_done"], 1)

        @block.scalar
        def _(act):
            for b in range(B):
                act.wait_ge(S["xh_turned"], b + 1)
                if b >= 1:
                    act.wait_ge(S["proj_done"], 4 * b)
                act.activation(nA[:, 0:SEQ], pA[:, 0:SEQ], ACT.Identity, bias=T["lncol"][:, 2:3],
                               scale=T["lncol"][:, 0:1]).then_inc(S["n_ready"], 1)
                act.activation(nB[:, 0:SEQ], pB[0:D2, 0:SEQ], ACT.Identity, bias=T["lncol"][0:D2, 3:4],
                               scale=T["lncol"][0:D2, 1:2]).then_inc(S["n_ready"], 1)
                if b >= 1:
                    act.wait_ge(S["conv2_done"], 3 * b)
                    act.wait_ge(S["y2_ready"], b)
                bi = lambda i, lo=0, hi=P: T["lncol"][lo:hi, 4 + i:5 + i]
                for i in range(4):
                    k = 4 * b + i
                    act.wait_ge(S["proj_done"], k + 1)
                    src = pX[k % 2]
                    if i == 0:
                        ins = act.activation(xA[:, 1:1 + LEN], src[:, 0:LEN], ACT.Identity, bias=bi(i))
                    elif i == 1:
                        act.activation(xB[0:D2, 1:1 + LEN], src[0:D2, 0:LEN], ACT.Identity, bias=bi(i, 0, D2))
                        ins = act.activation(xB[D2:P, 0:LEN], src[D2:P, 0:LEN], ACT.Identity, bias=bi(i, D2, P))
                    else:
                        ins = act.activation((zA if i == 2 else zB)[:, 0:LEN], src[:, 0:LEN], ACT.Silu, bias=bi(i))
                    ins.then_inc(S["proj_read"], 1)
                for m in range(3):
                    act.wait_ge(S["conv2_done"], 3 * b + m + 1)
                    act.activation(T["bu"][:, m, 0:LEN], pC[m][:, 0:LEN], ACT.Identity, bias=cols(BB, m), scale=cols(B_, m))\
                        .then_inc(S["conv_read"], 1)
                    act.activation(T["du"][:, m, 0:LEN], pC[m][:, 0:LEN], ACT.Identity, bias=cols(DB, m), scale=cols(D_, m))\
                        .then_inc(S["conv_read"], 1)

        @block.gpsimd
        def _(pool):
            for b in range(B):
                norm_root(pool, T, S, 3 * B + 2 * b)
                norm_root(pool, T, S, 3 * B + 2 * b + 1)

        @block.vector
        def _(dve):
            def norm(b):
                link = Link(dve, S["two_nlink"], 5, b)
                norm_stats(dve, T, S, link, 3 * B + 2 * b, lambda t: htile(T, b, t), D)
                at = lambda t: a[0:TOK, b % 2, t, :]
                link(norm_apply(dve, T, lambda t: htile(T, b, t), at))
                norm_stats(dve, T, S, link, 3 * B + 2 * b + 1, at, D)
                if b >= 1:
                    dve.wait_ge(S["xh_turned"], b)
                norm_apply(dve, T, at, lambda t: xh[0:TOK, 0, t, :]).then_inc(S["xh_ready"], 1)
            norm(0)
            for b in range(B):
                if b + 1 < B:
                    norm(b + 1)
                link = Link(dve, S["two_link"], 10, b)
                s, bu, du = T["scan"], T["bu"], T["du"]
                flip = lambda ap: view(ap, [[-1, LEN]], LEN - 1)
                for m, rows, back in ((0, slice(0, P), False), (1, slice(0, P), True),
                                      (2, slice(0, D2), False), (2, slice(D2, P), True)):
                    dve.wait_ge(S["conv_read"], 6 * b + 2 * m + 1)
                    src, dst = bu[rows, m, 0:LEN], s[rows, m, 0:LEN]
                    if back:
                        src, dst = flip(src), flip(dst)
                    ins = dve.tensor_tensor_scan(dst, view(T["mcol"][rows, 3 * LOGIT + m:3 * LOGIT + m + 1], [[0, LEN]]),
                                                 src, 0.0, ALU.mult, ALU.add)
                    link(ins)
                dve.wait_ge(S["conv_read"], 6 * b + 6)
                for m in range(3):
                    ins = dve.scalar_tensor_tensor(out=s[:, m, 0:LEN], in0=s[:, m, 0:LEN], scalar=cols(C_, m),
                                                   in1=du[:, m, 0:LEN], op0=ALU.mult, op1=ALU.add)
                link(ins)
                link(dve.tensor_tensor(s[:, 0, 0:LEN], s[:, 0, 0:LEN], s[:, 1, 0:LEN], ALU.add))
                dve.wait_ge(S["proj_read"], 4 * b + 4)
                if b >= 1:
                    dve.wait_ge(S["two_done"], b)
                dve.tensor_tensor(T["yA"][:, 0:LEN], s[:, 0, 0:LEN], zA[:, 0:LEN], ALU.mult)
                link(dve.tensor_tensor(T["yB"][:, 0:LEN], s[:, 2, 0:LEN], zB[:, 0:LEN], ALU.mult))
                dve.nop().then_inc(S["y2_ready"], 1)
                hb = T["h"][0:TOK, TPB * b:TPB * (b + 1), :]
                link(dve.tensor_tensor(hb, hb, a[0:TOK, b % 2, :, :], ALU.add))
                link(dve.tensor_tensor(hb, hb, view(T["rows"][0:TOK, 2, :], [[0, TPB], [1, D]]), ALU.add))
                dve.wait_ge(S["two_done"], b + 1)
                for t in range(TPB):
                    n = min(TOK, LEN - t * TOK)
                    ins = dve.tensor_tensor(htile(T, b, t)[0:n], htile(T, b, t)[0:n],
                                            pO[t // 2][0:n, (t % 2) * D:(t % 2 + 1) * D], ALU.add)
                link(ins)
                dve.nop().then_inc(S["two_out"], 1)


def soft_prepare(nc, T, S, io):
    with nc.Block() as block:
        @block.sync
        def _(sp):
            sp.dma_start(T["phA"][:, :], io["phiA"]).then_inc(S["phi_loaded"], 16)
            sp.dma_start(T["phB"][:, :], io["phiB"]).then_inc(S["phi_loaded"], 16)

        @block.vector
        def _(dve):
            link = Link(dve, S["phi_link"])
            dve.wait_ge(S["phi_loaded"], 32)
            for n, (name, rows) in enumerate((("phA", P), ("phB", D2))):
                phi, sq, s = T[name], T["phq"], T["phs"]
                link(dve.tensor_tensor(sq[0:rows, :], phi[:, :], phi[:, :], ALU.mult))
                link(dve.reduce_sum(s[0:rows, 0:SLOT], sq[0:rows, :].rearrange("d (n p) -> d p n", p=SLOT), axis=AX.X))
                dve.tensor_scalar(s[0:rows, 0:SLOT], s[0:rows, 0:SLOT], 1e-6, None, ALU.add).then_inc(S["phi_sum"], 1)
                dve.wait_ge(S["phi_root"], n + 1)
                link(dve.tensor_tensor(phi[:, :].rearrange("d (n p) -> d n p", p=SLOT),
                                       phi[:, :].rearrange("d (n p) -> d n p", p=SLOT),
                                       view(s[0:rows, SLOT:2 * SLOT], [[0, SOFT_E], [1, SLOT]]), ALU.mult))

        @block.gpsimd
        def _(pool):
            pool.memset(T["phs"][:, 2 * SLOT:3 * SLOT], -0.5).then_inc(S["phi_half"], 1)
            pool.wait_ge(S["phi_half"], 1)
            for n, rows in enumerate((P, D2)):
                pool.wait_ge(S["phi_sum"], n + 1)
                s = T["phs"]
                pool.tensor_tensor(s[0:rows, SLOT:2 * SLOT], s[0:rows, 0:SLOT], s[0:rows, 2 * SLOT:3 * SLOT], ALU.pow)\
                    .then_inc(S["phi_root"], 1)


def dispatch(nc, T, S, io):
    ps = T["ps"]
    pL = [(ps[0], ps[1]), (ps[2], ps[3])]
    pT, pE, pC = [ps[4], ps[5]], ps[6], ps[7]
    q, qA, qB, L, EC, EDT, ED, ECT = (T[n] for n in ("q", "qA", "qB", "L", "EC", "EDT", "ED", "ECT"))
    HALVES = SLOTS // 512
    rows = lambda t: min(TOK, LEN - t * TOK)
    with nc.Block() as block:
        @block.tensor
        def _(pe):
            def turn(b):
                pe.wait_ge(S["q_ready"], b + 1)
                k = TPB * b + 1
                if b >= 1:
                    pe.wait_ge(S["lg_read"], TPB * b)
                for t in range(TPB):
                    s = slice(t * TOK, (t + 1) * TOK)
                    pe.transpose(pL[k % 2][0][:, s], q[0:TOK, b % 3, t, 0:D1], T["ident"][0:TOK, 0:TOK])
                    mm = pe.transpose(pL[k % 2][1][0:D2, s], q[0:TOK, b % 3, t, D1:D], T["ident"][0:TOK, 0:TOK])
                mm.then_inc(S["q_turned"], 1)

            def logits(b, i):
                t, half = i // HALVES, i % HALVES
                k = TPB * b + t
                if i == 0:
                    pe.wait_ge(S["qT_ready"], 2 * (b + 1))
                if half == 0 and k >= 2:
                    pe.wait_ge(S["lg_read"], k - 1)
                s, w = slice(t * TOK, (t + 1) * TOK), slice(512 * half, 512 * (half + 1))
                o = pL[k % 2][half][0:TOK, :]
                pe.matmul(o, qA[:, b % 2, s], T["phA"][:, w], start=True, stop=False)
                mm = pe.matmul(o, qB[:, b % 2, s], T["phB"][:, w], start=False, stop=True)
                if half == HALVES - 1:
                    mm.then_inc(S["lg_done"], 1)

            def logits_turned(b, c):
                k = SC * b + c
                if c == 0:
                    pe.wait_ge(S["lg_read"], TPB * (b + 1))
                    if b >= 1:
                        pe.wait_ge(S["xs_read"], SC // 2 * b)
                if k >= 2:
                    pe.wait_ge(S["edt_ready"], k - 1)
                for t in range(TPB):
                    mm = pe.transpose(pT[k % 2][:, t * TOK:t * TOK + TOK], L[0:TOK, b % 2, t, c * P:(c + 1) * P],
                                      T["ident"][0:TOK, 0:TOK])
                mm.then_inc(S["lt_done"], 1)

            def slot_weights_turned(b, c):
                k = SC * b + c
                pe.wait_ge(S["edt_ready"], k + 1)
                if c == 0 and b >= 1:
                    pe.wait_ge(S["ht_read"], SC * b)
                if k >= 1:
                    pe.wait_ge(S["ed_read"], k)
                for t in range(TPB):
                    mm = pe.transpose(pE[0:rows(t), t * P:(t + 1) * P], EDT[:, k % 2, t * TOK:t * TOK + rows(t)],
                                      T["ident"][:, :])
                mm.then_inc(S["ed_turned"], 1)

            def token_weights_turned(b, c):
                k = SC * b + c
                if k >= 1:
                    pe.wait_ge(S["ect_read"], k)
                for t in range(TPB):
                    mm = pe.transpose(pC[:, t * TOK:(t + 1) * TOK], EC[0:TOK, b % 2, t, c * P:(c + 1) * P],
                                      T["ident"][0:TOK, 0:TOK])
                mm.then_inc(S["ect_turned"], 1)

            def slot_inputs(b, p):
                k = SC // 2 * b + p
                if p == 0:
                    pe.wait_ge(S["ed_read"], SC * (b + 1))
                if p >= 2:
                    pe.wait_ge(S["xs_read"], k - 1)
                for cc in range(2):
                    c = 2 * p + cc
                    for t in range(TPB):
                        mm = pe.matmul(pT[p % 2][:, cc * D:(cc + 1) * D], ED[0:rows(t), t, c * P:(c + 1) * P],
                                       q[0:rows(t), b % 3, t, :], start=(t == 0), stop=(t == TPB - 1))
                mm.then_inc(S["xs_done"], 1)

            def slot_inputs_turned(b, p):
                k = SC // 2 * b + p
                pe.wait_ge(S["hat_ready"], k + 1)
                if k >= 1:
                    pe.wait_ge(S["ht_read"], 2 * k)
                for cc in range(2):
                    pe.transpose(pE[:, cc * P:(cc + 1) * P], T["xs2"][:, p % 2, cc, 0:D1], T["ident"][:, :])
                    mm = pe.transpose(pE[0:D2, (2 + cc) * P:(3 + cc) * P], T["xs2"][:, p % 2, cc, D1:D], T["ident"][:, :])
                mm.then_inc(S["ht_done"], 1)

            turn(0)
            for i in range(TPB * HALVES):
                logits(0, i)
            for b in range(B):
                if b + 1 < B:
                    turn(b + 1)
                for c in range(SC):
                    logits_turned(b, c)
                    if c >= 1:
                        slot_weights_turned(b, c - 1)
                    token_weights_turned(b, c)
                    if b + 1 < B and 1 <= c <= TPB * HALVES:
                        logits(b + 1, c - 1)
                slot_weights_turned(b, SC - 1)
                for p in range(SC // 2):
                    slot_inputs(b, p)
                    if p >= 1:
                        slot_inputs_turned(b, p - 1)
                slot_inputs_turned(b, SC // 2 - 1)

        @block.scalar
        def _(act):
            def copy_q(b):
                k = TPB * b + 1
                act.wait_ge(S["q_turned"], b + 1)
                act.activation(qA[:, b % 2, :], pL[k % 2][0][:, 0:SEQ], ACT.Copy).then_inc(S["qT_ready"], 1)
                act.activation(qB[:, b % 2, :], pL[k % 2][1][0:D2, 0:SEQ], ACT.Copy).then_inc(S["qT_ready"], 1)

            def read_logits(b, t):
                k = TPB * b + t
                act.wait_ge(S["lg_max"], k + 1)
                if t == 0 and b >= 2:
                    act.wait_ge(S["ect_turned"], SC * (b - 1))
                for half in range(HALVES):
                    w = slice(512 * half, 512 * (half + 1))
                    act.activation(EC[0:TOK, b % 2, t, w], pL[k % 2][half][0:TOK, :], ACT.Exp,
                                   bias=T["lgm"][0:TOK, k % 2, 2:3],
                                   accum_out=T["zc2"][0:TOK, k, half:half + 1])
                for half in range(HALVES):
                    w = slice(512 * half, 512 * (half + 1))
                    ins = act.activation(L[0:TOK, b % 2, t, w], pL[k % 2][half][0:TOK, :], ACT.Copy)
                ins.then_inc(S["lg_read"], 1)

            copy_q(0)
            for t in range(TPB):
                read_logits(0, t)
            for b in range(B):
                if b + 1 < B:
                    copy_q(b + 1)
                for c in range(SC):
                    k = SC * b + c
                    act.wait_ge(S["lt_max"], k + 1)
                    if k >= 2:
                        act.wait_ge(S["ed_turned"], k - 1)
                    act.activation(EDT[:, k % 2, 0:LEN], pT[k % 2][:, 0:LEN], ACT.Exp, bias=T["ltm"][:, k % 2:k % 2 + 1],
                                   accum_out=T["zd"][:, k:k + 1]).then_inc(S["edt_ready"], 1)
                    act.wait_ge(S["ect_turned"], k + 1)
                    if c == 0 and b >= 2:
                        act.wait_ge(S[f"ect_stored{b % 2}"], 16 * (b // 2))
                    act.activation(ECT[:, b % 2, c, :], pC[:, 0:SEQ], ACT.Copy).then_inc(S["ect_read"], 1)
                    if b + 1 < B and c in (2, 4, 6):
                        read_logits(b + 1, c // 2 - 1)
                for p in range(SC // 2):
                    k = SC // 2 * b + p
                    act.wait_ge(S["ht_done"], k + 1)
                    for name, r, at in (("H1", P, 0), ("H2", D2, 2 * P)):
                        act.activation(view(T[name][:, :], [[P, 2 * P // SLOT], [1, SLOT]], 2 * p * (P // SLOT) * P + b * SLOT),
                                       pE[0:r, at:at + 2 * P].rearrange("d (n s) -> d n s", s=SLOT), ACT.Copy)\
                            .then_inc(S["ht_read"], 1)

        @block.sync
        def _(sp):
            for b in range(B):
                sp.wait_ge(S["ect_read"], SC * (b + 1))
                sp.dma_start(io["ect"][b], ECT[:, b % 2, :, :]).then_inc(S[f"ect_stored{b % 2}"], 16)
            for half in range(2):
                sp.wait_ge(S[f"ect_stored{half}"], 16 * B // 2)

        @block.gpsimd
        def _(pool):
            norm_root(pool, T, S, 5 * B)
            norm_root(pool, T, S, 5 * B + 1)
            for b in range(B):
                if b + 2 < B:
                    norm_root(pool, T, S, 5 * B + b + 2)
                for p in range(SC // 2):
                    pool.wait_ge(S["xvar"], SC // 2 * b + p + 1)
                    pool.tensor_tensor(T["xrstd"][:, 0:2], T["xv"][:, 0:2], T["minus_half"][:, 0:2], ALU.pow)\
                        .then_inc(S["xroot"], 1)

        @block.vector
        def _(dve):
            def norm(b):
                link = Link(dve, S["soft_nlink"], 2, b)
                norm_stats(dve, T, S, link, 5 * B + b, lambda t: htile(T, b, t), D)
                norm_apply(dve, T, lambda t: htile(T, b, t), lambda t: q[0:TOK, b % 3, t, :]).then_inc(S["q_ready"], 1)

            def token_max(b, t):
                k = TPB * b + t
                link = Link(dve, S["lg_link"], 1, k)
                dve.wait_ge(S["lg_done"], k + 1)
                if k >= 2:
                    dve.wait_ge(S["lg_read"], k - 1)
                m = T["lgm"][0:TOK, k % 2, :]
                for half in range(HALVES):
                    ins = dve.tensor_reduce(m[:, half:half + 1], pL[k % 2][half][0:TOK, :], AX.X, ALU.max)
                link(ins)
                dve.tensor_reduce(m[:, 2:3], m[:, 0:2], AX.X, ALU.max, negate=True).then_inc(S["lg_max"], 1)

            norm(0)
            norm(1)
            for t in range(TPB):
                token_max(0, t)
            for b in range(B):
                def ed_read(c):
                    k = SC * b + c
                    dve.wait_ge(S["ed_turned"], k + 1)
                    if c == 0 and b >= 1:
                        dve.wait_ge(S["xs_done"], SC // 2 * b)
                    last = TPB - 1
                    dve.tensor_copy(ED[0:TOK, 0:last, c * P:(c + 1) * P],
                                    pE[0:TOK, 0:last * P].rearrange("m (t s) -> m t s", s=P))
                    dve.tensor_copy(ED[0:rows(last), last, c * P:(c + 1) * P], pE[0:rows(last), last * P:TPB * P])\
                        .then_inc(S["ed_read"], 1)
                for c in range(SC):
                    k = SC * b + c
                    dve.wait_ge(S["lt_done"], k + 1)
                    if k >= 2:
                        dve.wait_ge(S["edt_ready"], k - 1)
                    dve.tensor_reduce(T["ltm"][:, k % 2:k % 2 + 1], pT[k % 2][:, 0:LEN], AX.X, ALU.max, negate=True)\
                        .then_inc(S["lt_max"], 1)
                    if c >= 1:
                        ed_read(c - 1)
                    if b + 1 < B and c in (2, 4, 6):
                        token_max(b + 1, c // 2 - 1)
                ed_read(SC - 1)
                if b + 2 < B:
                    norm(b + 2)
                dve.reciprocal(T["rzd"][:, 0:SC], T["zd"][:, SC * b:SC * (b + 1)]).then_inc(S["rzd_ready"], 1)
                dve.wait_ge(S["rzd_ready"], b + 1)
                for p in range(SC // 2):
                    k = SC // 2 * b + p
                    link = Link(dve, S["xs_link"], 2, k)
                    dve.wait_ge(S["xs_done"], k + 1)
                    if k >= 2:
                        dve.wait_ge(S["ht_done"], k - 1)
                    x2 = T["xs2"][:, p % 2, :, :]
                    dve.tensor_tensor(x2, pT[p % 2][:, 0:2 * D].rearrange("s (c d) -> s c d", d=D),
                                      bcast(T["rzd"][:, 2 * p:2 * p + 2], D), ALU.mult).then_inc(S["xs_read"], 1)
                    dve.wait_ge(S["xs_read"], k + 1)
                    for cc in range(2):
                        ins = dve.bn_stats(T["xbn"][:, cc, :], x2[:, cc, :])
                    link(ins)
                    for cc in range(2):
                        ins = dve.bn_aggr(T["xmv"][:, cc, :], T["xbn"][:, cc, :])
                    link(ins)
                    dve.tensor_scalar(T["xv"][:, 0:2], T["xmv"][:, :, 1], EPS, None, ALU.add).then_inc(S["xvar"], 1)
                    dve.wait_ge(S["xroot"], k + 1)
                    for cc in range(2):
                        ins = dve.tensor_scalar(x2[:, cc, :], x2[:, cc, :], T["xmv"][:, cc, 0:1],
                                                T["xrstd"][:, cc:cc + 1], ALU.subtract, ALU.mult)
                    ins.then_inc(S["hat_ready"], 1)
            zc2 = T["zc2"][0:TOK, :, :]
            dve.tensor_tensor(T["rzc"][0:TOK, :], zc2[:, :, 0], zc2[:, :, 1], ALU.add).then_inc(S["rzc_sum"], 1)
            dve.wait_ge(S["rzc_sum"], 1)
            dve.reciprocal(T["rzc"][0:TOK, :], T["rzc"][0:TOK, :])


RING = 4


def experts(nc, T, S, io):
    ps = T["ps"]
    pH, pY = [ps[0], ps[1]], [ps[2], ps[3]]
    W = SOFT_H + SHC * D
    n_rows = B * SLOT

    def load(sp, n, r):
        sp.dma_start(T["w12"][:, r, :], bass.AP(io["w12"].tensor, n * P * W, [[W, P], [1, W]]))\
            .then_inc(S[f"expert_loaded{r}"], 16)
        sp.dma_start(T["w1x"][:, r, :], bass.AP(io["w1x"].tensor, n * (D2 + 1) * SOFT_H, [[SOFT_H, D2 + 1], [1, SOFT_H]]))\
            .then_inc(S[f"expert_loaded{r}"], 16)

    with nc.Block() as block:
        @block.sync
        def _(sp):
            for r in range(RING):
                load(sp, r, r)
            with sp.Fori(RING, SOFT_E - RING + 1, RING) as i:
                for r in range(RING):
                    sp.wait_ge(S["expert_out"], i + r - RING + 1)
                    load(sp, i + r, r)

        @block.tensor
        def _(pe):
            def up(n, i, r):
                pe.wait_ge(S[f"expert_loaded{r}"], 32 // RING * i + 32)
                pe.wait_ge(S["slots_ready"], 2 * n + 2)
                for c in range(SHC):
                    o = pH[r % 2][:, c * n_rows:(c + 1) * n_rows]
                    pe.matmul(o, T["w12"][:, r, c * P:(c + 1) * P], T["a1"][:, r % 2, :], start=True, stop=False)
                    mm = pe.matmul(o, T["w1x"][:, r, c * P:(c + 1) * P], T["a2"][:, r % 2, :], start=False, stop=True)
                mm.then_inc(S["expert_hid"], 1)

            def down(n, r):
                pe.wait_ge(S["expert_act"], n + 1)
                pe.wait_ge(S["expert_read"], n)
                for c in range(SHC):
                    mm = pe.matmul(pY[r % 2][:, 0:D], T["eg"][:, r % 2, c * n_rows:(c + 1) * n_rows],
                                   T["w12"][:, r, SOFT_H + c * D:SOFT_H + (c + 1) * D], start=(c == 0), stop=(c == SHC - 1))
                mm.then_inc(S["expert_out"], 1)
            with pe.Fori(0, SOFT_E - RING + 1, RING) as i:
                for r in range(RING):
                    up(i + r, i, r)
                    if r >= 1:
                        down(i + r - 1, r - 1)
                down(i + RING - 1, RING - 1)

        @block.scalar
        def _(act):
            with act.Fori(0, SOFT_E - RING + 1, RING) as i:
                for r in range(RING):
                    act.wait_ge(S["expert_hid"], i + r + 1)
                    act.activation(T["eg"][:, r % 2, :], pH[r % 2][:, 0:SHC * n_rows], ACT.Gelu)\
                        .then_inc(S["expert_act"], 1)

        @block.vector
        def _(dve):
            def slots(n, r):
                for name, src, g, rows in (("a1", "H1", "egA", P), ("a2", "H2", "egB", D2)):
                    dve.tensor_scalar(T[name][0:rows, r % 2, :], T[src][:, bass.ds(n * n_rows, n_rows)],
                                      T[g][:, 0, bass.ds(n, 1)], T[g][:, 1, bass.ds(n, 1)], ALU.mult, ALU.add)\
                        .then_inc(S["slots_ready"], 1)

            with dve.Fori(0, SOFT_E - RING + 1, RING) as i:
                dve.wait_ge(S["y_stored"], 16 * i)
                slots(i, 0)
                for r in range(RING):
                    if r + 1 < RING:
                        if r >= 1:
                            dve.wait_ge(S["expert_hid"], i + r)
                        slots(i + r + 1, r + 1)
                    dve.wait_ge(S["expert_out"], i + r + 1)
                    dve.tensor_copy(T["ye"][:, r, :], pY[r % 2][:, 0:D]).then_inc(S["expert_read"], 1)

        @block.gpsimd
        def _(pool):
            with pool.Fori(0, SOFT_E - RING + 1, RING) as i:
                for r in range(RING):
                    pool.wait_ge(S["expert_read"], i + r + 1)
                    dst = bass.AP(io["ys"].tensor, (i + r) * SLOT * D, [[SLOTS * D, B], [D, SLOT], [1, D]])
                    pool.dma_start(dst, T["ye"][:, r, :]).then_inc(S["y_stored"], 16)
            pool.wait_ge(S["y_stored"], 16 * SOFT_E)


def combine(nc, T, S, io):
    pO = T["ps"][0:2]
    with nc.Block() as block:
        @block.sync
        def _(sp):
            def load(b):
                if b >= 2:
                    sp.wait_ge(S["mixed"], TPB * (b - 1))
                src = bass.AP(io["ys"].tensor, b * SLOTS * D, [[D, P], [P * D, SC], [1, D]])
                sp.dma_start(T["yb"][:, b % 2, :, :], src).then_inc(S[f"mix_loaded{b % 2}"], 16)
                sp.dma_start(T["ectb"][:, b % 2, :, :], io["ect"][b]).then_inc(S[f"mix_loaded{b % 2}"], 16)
            load(0)
            load(1)
            for b in range(B):
                for t in range(TPB):
                    k = TPB * b + t
                    n = min(TOK, LEN - t * TOK)
                    sp.wait_ge(S["mix_out"], k + 1)
                    sp.dma_start(io["out"][b, t * TOK:t * TOK + n, :], T["o"][0:n, k % 4, :]).then_inc(S[f"stored{k % 4}"], 16)
                if b + 2 < B:
                    load(b + 2)
            for r in range(4):
                sp.wait_ge(S[f"stored{r}"], 16 * TILES // 4)

        @block.vector
        def _(dve):
            def bias(b):
                dve.wait_ge(S[f"mix_loaded{b % 2}"], 32 * (b // 2 + 1))
                dve.tensor_tensor(T["yb"][:, b % 2, :, :], T["yb"][:, b % 2, :, :], T["b2s"][:, :, :], ALU.add)\
                    .then_inc(S["yb_ready"], 1)
            bias(0)
            for b in range(B):
                if b + 1 < B:
                    bias(b + 1)
                for t in range(TPB):
                    k = TPB * b + t
                    n = min(TOK, LEN - t * TOK)
                    dve.wait_ge(S["mixed"], k + 1)
                    if k >= 4:
                        dve.wait_ge(S[f"stored{k % 4}"], 16 * (k // 4))
                    dve.scalar_tensor_tensor(out=T["o"][0:n, k % 4, :], in0=pO[k % 2][0:n, 0:D], scalar=T["rzc"][0:n, k:k + 1],
                                             in1=htile(T, b, t)[0:n], op0=ALU.mult, op1=ALU.add).then_inc(S["mix_out"], 1)

        @block.tensor
        def _(pe):
            for b in range(B):
                pe.wait_ge(S["yb_ready"], b + 1)
                for t in range(TPB):
                    k = TPB * b + t
                    n = min(TOK, LEN - t * TOK)
                    if k >= 2:
                        pe.wait_ge(S["mix_out"], k - 1)
                    for c in range(SC):
                        mm = pe.matmul(pO[k % 2][0:n, 0:D], T["ectb"][:, b % 2, c, t * TOK:t * TOK + n],
                                       T["yb"][:, b % 2, c, :], start=(c == 0), stop=(c == SC - 1))
                    mm.then_inc(S["mixed"], 1)


def program(nc, io):
    with ExitStack() as ctx:
        def sb(name, shape, dt=F32, on=ctx):
            T[name] = on.enter_context(nc.sbuf_tensor(f"t{len(made)}_" + name, shape, dt))
            made.append(name)

        T, S, made = {}, {}, []
        psum = [ctx.enter_context(nc.psum_tensor(f"bank{i}", [P, 512], F32)) for i in range(8)]
        T["ps"] = psum
        T["psY"], T["psT"], T["psL"], T["psPX"] = psum[0:3], psum[3], psum[4:6], psum[6]
        for name in ("nvar nroot tok_link tok_turned tok_normed tok_back tok_affine tok_projected tok_out "
                     "ssm_exp ssm_r ssm_angle ssm_link u_ready u_turned uT_ready ssm_in Bu_ready x_ready "
                     "ssm_out y_ready ssm_nlink ssm_slink ssm_blink rows_loaded weights_loaded small_loaded v_ready "
                     "v_turned vT_ready hid_ready hid_done picked maskT_ready out_done scores_ready mask_ready "
                     "mask_turned z_ready ez_ready ffn_nlink gate_link shift_ready xh_ready xh_turned two_out "
                     "n_ready proj_read proj_done conv_read conv2_done y2_ready two_done two_nlink two_link "
                     "sig phi_loaded phi_link phi_sum phi_root phi_half q_ready lg_read q_turned qT_ready "
                     "lg_done xs_read edt_ready lt_done ht_read ed_read ed_turned ect_read ect_turned xs_done "
                     "hat_ready ht_done lg_max lt_max ect_stored0 ect_stored1 xvar xroot soft_nlink lg_link rzd_ready "
                     "xs_link rzc_sum expert_out slots_ready expert_hid expert_act expert_read y_stored "
                     "soft_loaded mixed mix_out stored0 stored1 stored2 stored3 yb_ready mix_loaded0 mix_loaded1 expert_loaded0 "
                     "expert_loaded1 expert_loaded2 expert_loaded3").split():
            S[name] = ctx.enter_context(nc.semaphore(name))
        early_names = ("wt_loaded w0_loaded gram_ready band_loaded w0_split w60_loaded ident_zero identb_ready "
                       "pool_zero dve w0_centred wt_centred w0c_ready w0c_copied gram_done normed l0_ready "
                       "h_ready conv_done turned patch_ready zz_done patch_copied patch_turned window_turned "
                       "window_copied gram_applied l0_done summed squared carried0 carried1 carried2 carried3 "
                       "var_ready rstd_ready zsum zvar_ready zrstd_ready scaled_ready x_loaded cols_loaded "
                       "ident_ready").split()
        for name in early_names:
            S[name] = nc.alloc_semaphore(name=name)
        late_names = [f"{name}{layer}" for layer in (5, 6)
                      for name in ("in", "conv", "sq", "sum", "var", "rstd", "norm", "turn", "out")]

        sb("ident", [P, P])
        sb("minus_half", [P, 8])
        sb("bn", [P, TPB, 6])
        sb("mv", [P, TPB, 2])
        sb("nvar", [P, 4])
        sb("nrstd", [P, 4])
        sb("h", [P, TILES, D])
        with ExitStack() as weights:
            def sw(name, shape, dt=F32):
                sb(name, shape, dt, weights)
            sw("cols", [P, 19])
            sw("rows", [TOK, 3, D])
            sw("gate_row", [TOK, 3 * N_EXPERT])
            sw("proj_w", [P, D])
            sw("CT", [P, 2, D])
            sw("BTa", [P, 2, P])
            sw("BTb", [D2, 2, P])
            sw("gate_wa", [P, N_EXPERT])
            sw("gate_wb", [D2, N_EXPERT])
            sw("b1", [P, N_EXPERT * HC])
            sw("b2", [N_EXPERT, D])
            sw("Wia", [P, 4, P])
            sw("Wib", [D2, 4, P])
            sw("Wca", [P, 3, 3 * P])
            sw("Wcb", [P, 3 * P])
            sw("Wcc", [D2, 3 * P])
            sw("Woa", [P, D])
            sw("Wob", [P, D])
            sw("mcol", [P, 21])
            sw("lncol", [P, 8])
            with ExitStack() as conv:
                def sc(name, shape, dt=F32):
                    sb(name, shape, dt, conv)
                sc("wt", [P, 16, C])
                sc("l4", [P, CHUNK // 16 * (CHUNKS + 2)])
                sc("sq", [P, 2, 512])
                sc("yn", [P, 2, 512])
                sc("ss", [P, 2, 4])
                sc("var", [P, 2, 4])
                sc("rstd", [P, 2, 4])
                with ExitStack() as early:
                    def se(name, shape, dt=F32):
                        sb(name, shape, dt, early)
                    se("identb", [P, P], BF16)
                    se("wmean", [P, 16])
                    se("w0T", [TAPS0, C])
                    se("w0mean", [TAPS0, 1])
                    se("w0parts", [TAPS0, 3, C], BF16)
                    se("w0rest", [TAPS0, C])
                    se("w0c", [P, TAPS0])
                    se("gram", [TAPS0, TAPS0])
                    se("band", [WINH, HALF * TAPS0])
                    se("w60", [2 * ROWS, 2, C], BF16)
                    se("xs", [P, WIN])
                    se("xT", [WINH, 2, P])
                    se("zz", [P, POS, TAPS0])
                    se("zs", [P, POS])
                    se("zvar", [P, POS])
                    se("zrstd", [P, POS])
                    se("scaled", [P, POS, TAPS0])
                    se("rest", [P, POS, TAPS0])
                    se("p60", [P, POS, ROWS], BF16)
                    se("p60T", [2 * ROWS, PAIRS, P], BF16)
                    se("l0", [P, 2 + CHUNK])
                    se("l1", [P, 1 + CHUNK // 2])
                    se("l2", [P, 1 + CHUNK // 4])
                    se("l3", [P, 1 + CHUNK // 8])
                    setup(nc, T, S, io)
                    stream(nc, T, S, io)
                nc.all_engine_barrier()
                nc.clear_and_free_semaphores([S[name] for name in early_names])
                nc.all_engine_barrier()
                for name in late_names:
                    S[name] = nc.alloc_semaphore(name=name)
                with ExitStack() as late:
                    sb("l5", [P, 2 * B * SEQ], on=late)
                    sb("l6", [P, B * SEQ], on=late)
                    sb("stage", [P, 2, 2 * SEQ], on=late)
                    sb("tA", [P, TPB * C], on=late)
                    sb("tB", [P, SEQ], on=late)
                    layers56(nc, T, S)
                    tokens(nc, T, S)
            with ExitStack() as attn:
                def sa(name, shape, dt=F32):
                    sb(name, shape, dt, attn)
                sa("sv", [P, 24])
                sa("Cq", [P, 2, D])
                sa("Ctmp", [P, D])
                sa("cosT", [P, LEN])
                sa("sinT", [P, LEN])
                sa("rot", [P, LEN])
                sa("u", [TOK, 2, TPB, D])
                sa("uD", [TOK, TPB, D])
                sa("uA", [P, SEQ])
                sa("uB", [D2, SEQ])
                sa("seq", [P, 8, LEN])
                ssm_tables(nc, T, S)
                state_space(nc, T, S)
            with ExitStack() as ffn:
                def sf(name, shape, dt=F32):
                    sb(name, shape, dt, ffn)
                sf("w1a", [P, N_EXPERT * HID])
                sf("w1b", [D2, N_EXPERT * HID])
                sf("w2", [P, N_EXPERT * HC, D])
                sf("u", [TOK, 2, TPB, D])
                sf("vA", [P, 2, SEQ])
                sf("vB", [D2, 2, SEQ])
                sf("G", [P, 2 * HC, SEQ])
                sf("z", [P, TPB, N_EXPERT])
                sf("ez", [P, TPB, N_EXPERT])
                sf("mask", [P, 2, TPB, N_EXPERT])
                sf("top", [P, TPB])
                sf("left", [P, TPB])
                sf("maskT", [N_EXPERT, SEQ])
                with nc.Block() as block:
                    @block.sync
                    def _(sp):
                        for name in ("w1a", "w1b", "w2"):
                            sp.dma_start(T[name][:], io[name]).then_inc(S["weights_loaded"], 16)
                        sp.wait_ge(S["weights_loaded"], 3 * 16)
                routed_ffn(nc, T, S)
            with ExitStack() as two:
                def s2(name, shape, dt=F32):
                    sb(name, shape, dt, two)
                s2("u", [TOK, 2, TPB, D])
                s2("xh", [TOK, 2, TPB, D])
                s2("nA", [P, SEQ])
                s2("nB", [D2, SEQ])
                s2("xA", [P, LEN + 2])
                s2("xB", [P, LEN + 2])
                s2("zA", [P, LEN])
                s2("zB", [P, LEN])
                s2("yA", [P, LEN])
                s2("yB", [P, LEN])
                s2("bu", [P, 3, LEN])
                s2("du", [P, 3, LEN])
                s2("scan", [P, 3, LEN])
                two_way_prepare(nc, T, S)
                two_way_scan(nc, T, S)
        with ExitStack() as soft:
            sb("H1", [P, SOFT_E * P], on=soft)
            sb("H2", [D2, SOFT_E * P], on=soft)
            sb("zc2", [TOK, TILES, 2], on=soft)
            sb("rzc", [TOK, TILES], on=soft)
            with ExitStack() as disp:
                def sd(name, shape, dt=F32):
                    sb(name, shape, dt, disp)
                sd("phA", [P, SLOTS])
                sd("phB", [D2, SLOTS])
                with ExitStack() as prep:
                    sb("phq", [P, SLOTS], on=prep)
                    sb("phs", [P, 3 * SLOT], on=prep)
                    soft_prepare(nc, T, S, io)
                sd("q", [TOK, 3, TPB, D])
                sd("qA", [P, 2, SEQ])
                sd("qB", [D2, 2, SEQ])
                sd("L", [TOK, 2, TPB, SLOTS])
                sd("EC", [TOK, 2, TPB, SLOTS])
                sd("EDT", [P, 2, LEN])
                sd("ED", [TOK, TPB, SLOTS])
                sd("ECT", [P, 2, SC, SEQ])
                sd("lgm", [TOK, 2, 3])
                sd("ltm", [P, 2])
                sd("zd", [P, SC * B])
                sd("rzd", [P, SC])
                sd("xs2", [P, 2, 2, D])
                sd("xbn", [P, 2, 6])
                sd("xmv", [P, 2, 2])
                sd("xv", [P, 2])
                sd("xrstd", [P, 2])
                dispatch(nc, T, S, io)
            def sx(name, shape, dt=F32):
                sb(name, shape, dt, soft)
            sx("w12", [P, RING, SOFT_H + SHC * D])
            sx("w1x", [D2 + 1, RING, SOFT_H])
            sx("a1", [P, 2, P])
            sx("a2", [D2 + 1, 2, P])
            sx("eg", [P, 2, SOFT_H])
            sx("ye", [P, RING, D])
            sx("egA", [P, 2, SOFT_E])
            sx("egB", [D2, 2, SOFT_E])
            sx("b2s", [P, SC, D])
            with nc.Block() as block:
                @block.sync
                def _(sp):
                    sp.dma_start(T["egA"][:, :, :], io["egA"]).then_inc(S["soft_loaded"], 16)
                    sp.dma_start(T["egB"][:, :, :], io["egB"]).then_inc(S["soft_loaded"], 16)
                    for m in range(P // SLOT):
                        src = bass.AP(io["soft_b2"].tensor, m * D, [[0, SLOT], [P // SLOT * D, SC], [1, D]])
                        sp.dma_start(T["b2s"][m * SLOT:(m + 1) * SLOT, :, :], src).then_inc(S["soft_loaded"], 16)
                    sp.wait_ge(S["soft_loaded"], 16 * (2 + P // SLOT))

                @block.gpsimd
                def _(pool):
                    pool.memset(T["a2"][:, :, :], 1.0)
            experts(nc, T, S, io)
            sx("yb", [P, 2, SC, D])
            sx("ectb", [P, 2, SC, SEQ])
            sx("o", [TOK, 4, D])
            combine(nc, T, S, io)


def two_way_prepare(nc, T, S):
    cols = lambda i: T["mcol"][:, 3 * i:3 * i + 3]
    with nc.Block() as block:
        @block.scalar
        def _(act):
            act.activation(cols(1), cols(1), ACT.Exp, scale=-1.0).then_inc(S["sig"], 1)

        @block.gpsimd
        def _(pool):
            pool.memset(T["xA"][:, :], 0.0)
            pool.memset(T["xB"][:, :], 0.0)

        @block.vector
        def _(dve):
            dve.wait_ge(S["sig"], 1)
            dve.tensor_scalar(cols(1), cols(1), 1.0, None, ALU.add).then_inc(S["sig"], 1)
            dve.wait_ge(S["sig"], 2)
            dve.reciprocal(cols(1), cols(1))
            dve.tensor_tensor(cols(5), cols(0), cols(2), ALU.mult)
            dve.tensor_tensor(cols(6), cols(0), cols(4), ALU.mult)


def kernel(**inputs):
    import numpy as np
    import concourse.bacc as bacc
    from concourse.bass_utils import run_bass_kernel_spmd as launch

    a = {k: np.asarray(v) for k, v in inputs.items()}
    x = np.concatenate([a["x"].reshape(-1), np.zeros(((CHUNKS + 3) * STEP + WIN - a["x"].size,), a["x"].dtype)])
    conv_w = np.concatenate([a[f"L0_tok_conv_w{l}"].transpose(1, 2, 0) for l in range(1, 7)], axis=1)
    at, ff, tw = (lambda n, p=p: a[p + n] for p in ("L0_attn_", "L0_ffn_", "L1_attn_"))
    cols = np.stack([a[f"L0_tok_ln_g{l}"] for l in range(7)] + [a["L0_tok_fln_g"]]
                    + [a[f"L0_tok_ln_b{l}"] for l in range(7)] + [a["L0_tok_fln_b"]]
                    + [at("log_A_real"), at("A_imag"), at("log_dt")], axis=1)
    arrays = {"x": x, "conv_w": conv_w, "conv_w0": a["L0_tok_conv_w0"][:, 0, :].T, "cols": cols}
    arrays["proj_w"] = a["L0_tok_proj_w"]
    arrays["rows"] = np.stack([a["L0_tok_proj_b"], at("D"), tw("bo")])
    arrays["gate_row"] = np.concatenate([ff("gate_b"), ff("gate_center")])
    arrays["CT"] = np.stack([at("C_re").T, at("C_im").T], axis=1)
    BT = np.stack([at("B_re").T, at("B_im").T], axis=1)
    arrays["BTa"], arrays["BTb"] = BT[:D1], BT[D1:]
    arrays["gate_wa"], arrays["gate_wb"] = ff("gate_w")[:D1], ff("gate_w")[D1:]
    arrays["b1"] = ff("b1").reshape(N_EXPERT * HC, P).T
    arrays["b2"] = ff("b2")
    w1 = ff("w1").transpose(1, 0, 2).reshape(D, N_EXPERT * HID)
    arrays["w1a"], arrays["w1b"] = w1[:D1], w1[D1:]
    arrays["w2"] = ff("w2").reshape(N_EXPERT * HC, P, D).transpose(1, 0, 2)

    def halves(v):
        return v[..., :D1], np.concatenate([v[..., D1:], v[..., D1:]], axis=-1)
    Wi, bi = tw("Wi"), tw("bi")
    W = np.stack(halves(Wi[:, :D]) + halves(Wi[:, D:]), axis=1)
    arrays["Wia"], arrays["Wib"] = W[:D1], W[D1:]
    g, g2 = halves(tw("ln_g"))
    b, b2 = halves(tw("ln_b"))
    arrays["lncol"] = np.stack((g, g2, b, b2) + halves(bi[:D]) + halves(bi[D:]), axis=1)

    def mixed(f, b):
        return np.concatenate([f[..., :D1], b[..., :D1], f[..., D1:], b[..., D1:]], axis=-1)
    Wc = mixed(tw("Wf_conv").transpose(1, 2, 0), tw("Wb_conv").transpose(1, 2, 0)[:, ::-1])
    arrays["Wca"] = Wc[:D1]
    arrays["Wcb"] = np.concatenate([Wc[D1:, 0], Wc[D1:, 1]])
    arrays["Wcc"] = Wc[D1:, 2]
    arrays["Woa"], arrays["Wob"] = tw("Wo")[:D1], np.concatenate([tw("Wo")[D1:], tw("Wo")[D1:]])
    arrays["mcol"] = np.concatenate([mixed(tw(f), tw(b)).reshape(3, P).T for f, b in
                                     (("bf_conv", "bb_conv"), ("af", "ab"), ("bf", "bb"), ("cf", "cb"), ("df", "db"))],
                                    axis=1)
    so = lambda n: a["L1_ffn_" + n]
    phi = so("phi").transpose(2, 0, 1).reshape(D, SLOTS)
    arrays["phiA"], arrays["phiB"] = phi[:D1], phi[D1:]
    arrays["w12"] = np.concatenate([so("w1")[:, :D1], so("w2").reshape(SOFT_E, SHC, P, D).transpose(0, 2, 1, 3)
                                    .reshape(SOFT_E, P, SHC * D)], axis=2)
    arrays["w1x"] = np.concatenate([so("w1")[:, D1:], so("b1")[:, None]], axis=1)
    eg = np.stack([so("ln_g").T, so("ln_b").T], axis=1)
    arrays["egA"], arrays["egB"] = eg[:D1], eg[D1:]
    arrays["soft_b2"] = so("b2")
    arrays = {k: np.ascontiguousarray(v) for k, v in arrays.items()}
    nc = bacc.Bacc("TRN2", target_bir_lowering=False, num_devices=1)
    io = {k: nc.dram_tensor("in_" + k, v.shape, mybir.dt.from_np(v.dtype), kind="ExternalInput").ap()
          for k, v in arrays.items()}
    io["out"] = nc.dram_tensor("out", [B, LEN, D], F32, kind="ExternalOutput").ap()
    io["ect"] = nc.dram_tensor("ect", [B, P, SC, SEQ], F32, kind="Internal").ap()
    io["ys"] = nc.dram_tensor("ys", [B, SLOTS, D], F32, kind="Internal").ap()
    program(nc, io)
    r = launch(nc, [{"in_" + k: v for k, v in arrays.items()}], core_ids=[0])
    return r.results[0]["out"]
```

```python
import concourse.bass as bass
from concourse import mybir
from contextlib import ExitStack

F32 = mybir.dt.float32
BF16 = mybir.dt.bfloat16
ALU = mybir.AluOpType
ACT = mybir.ActivationFunctionType
AX = mybir.AxisListType

P = 128
B = 8
SAMPLES = 120000
C = 128
TAPS0, STRIDE0 = 10, 5
EPS = 1e-5

CHUNK = 4096
POS = CHUNK // P
WIN = STRIDE0 * (POS - 1) + TAPS0
HALF = POS // 2
WINH = STRIDE0 * (HALF - 1) + TAPS0
STEP = CHUNK * STRIDE0
CHUNKS = -(-B * SAMPLES // STEP)
PAIRS = POS // 2
PARTS = 6
ROWS = PARTS * TAPS0
SPLIT = [(0, 0), (0, 1), (1, 0), (0, 2), (2, 0), (1, 1)]


def view(ap, dims, offset=0):
    return bass.AP(ap.tensor, ap.offset + offset, [list(ap.ap[0])] + [list(d) for d in dims])


def bcast(ap, n):
    return bass.AP(ap.tensor, ap.offset, [list(d) for d in ap.ap] + [[0, n]])


GROUPS = [(1, 0), (1, 1), (1, 2), (1, 3), (4, 0), (3, 0), (2, 0), (2, 1)]
NG = len(GROUPS)
BANKS = 4
LAG = 2
L0_MIDDLE = {5: (3,), 6: (5,), 7: (7,)}
L0_BEHIND = {4: (2,), 5: (4,), 6: (6,)}
L0_END = {3: (0, 1)}
INPUT_OF = {1: 0, 2: 1, 3: 2, 4: 3}


def setup(nc, T, S, io):
    with nc.Block() as block:
        @block.sync
        def _(sp):
            sp.dma_start(T["wt"][:, :, :], io["conv_w"]).then_inc(S["wt_loaded"], 16)
            sp.dma_start(T["w0T"][:, :], io["conv_w0"]).then_inc(S["w0_loaded"], 16)
            sp.dma_start(T["cols"][:, :], io["cols"]).then_inc(S["cols_loaded"], 16)
            sp.dma_start(T["xs"][:, :], x_chunk(io, 0)).then_inc(S["x_loaded"], 16)
            for name in ("proj_w", "CT", "BTa", "BTb", "gate_wa", "gate_wb", "b1", "b2", "Wia", "Wib", "Wca", "Wcb",
                         "Wcc", "Woa", "Wob", "lncol"):
                sp.dma_start(T[name][:], io[name]).then_inc(S["small_loaded"], 16)
            sp.dma_start(T["mcol"][:, 0:15], io["mcol"]).then_inc(S["small_loaded"], 16)
            for name, n in (("rows", 3 * D), ("gate_row", 2 * N_EXPERT)):
                src = bass.AP(io[name].tensor, 0, [[0, TOK], [1, n]])
                sp.dma_start(view(T[name][:], [[1, n]]), src).then_inc(S["rows_loaded"], 16)
            sp.wait_ge(S["gram_ready"], 1)
            for r in range(HALF):
                sp.dma_start(T["band"][STRIDE0 * r:STRIDE0 * r + TAPS0, TAPS0 * r:TAPS0 * (r + 1)],
                             T["gram"][:, :]).then_inc(S["band_loaded"], 16)
            sp.wait_ge(S["w0_split"], 1)
            for slot in range(2):
                for n, (_, part) in enumerate(SPLIT):
                    r = slot * ROWS + n * TAPS0
                    sp.dma_start(T["w60"][r:r + TAPS0, slot, :], T["w0parts"][:, part, :])\
                        .then_inc(S["w60_loaded"], 16)
            sp.wait_ge(S["cols_loaded"], 16)
            sp.wait_ge(S["small_loaded"], 16 * 17)
            sp.wait_ge(S["rows_loaded"], 16 * 2)

        @block.gpsimd
        def _(pool):
            pool.memset(T["ident"][:, :], 0.0).then_inc(S["ident_zero"], 1)
            pool.wait_ge(S["ident_zero"], 1)
            pool.affine_select(out=T["ident"][:, :], in_=T["ident"][:, :], compare_op=ALU.not_equal,
                               fill=1.0, base=0, pattern=[[-1, P]], channel_multiplier=1)\
                .then_inc(S["ident_ready"], 1)
            pool.memset(T["minus_half"][:, :], -0.5)
            pool.memset(T["h"][:, :, :], 0.0)
            pool.memset(T["band"][:, :], 0.0)
            pool.memset(T["w60"][:, :, :], 0.0)
            for name in ("l0", "l1", "l2", "l3"):
                pool.memset(T[name][:, :], 0.0)
            pool.memset(T["yn"][:, :, :], 0.0).then_inc(S["pool_zero"], 1)

        @block.vector
        def _(dve):
            dve.wait_ge(S["pool_zero"], 1)
            dve.wait_ge(S["w0_loaded"], 16)
            dve.reduce_sum(T["w0mean"][:, :], T["w0T"][:, :], axis=AX.X).then_inc(S["dve"], 1)
            dve.wait_ge(S["dve"], 1)
            dve.tensor_scalar(T["w0mean"][:, :], T["w0mean"][:, :], 1.0 / C, None, ALU.mult).then_inc(S["dve"], 1)
            dve.wait_ge(S["dve"], 2)
            dve.tensor_scalar(T["w0T"][:, :], T["w0T"][:, :], T["w0mean"][:, 0:1], None, ALU.subtract)\
                .then_inc(S["w0_centred"], 1)
            dve.wait_ge(S["w0_centred"], 1)
            dve.tensor_copy(T["w0parts"][:, 0, :], T["w0T"][:, :]).then_inc(S["dve"], 1)
            dve.wait_ge(S["dve"], 3)
            dve.tensor_tensor(T["w0rest"][:, :], T["w0T"][:, :], T["w0parts"][:, 0, :], ALU.subtract)\
                .then_inc(S["dve"], 1)
            dve.wait_ge(S["dve"], 4)
            dve.tensor_copy(T["w0parts"][:, 1, :], T["w0rest"][:, :]).then_inc(S["dve"], 1)
            dve.wait_ge(S["dve"], 5)
            dve.tensor_tensor(T["w0parts"][:, 2, :], T["w0rest"][:, :], T["w0parts"][:, 1, :], ALU.subtract)\
                .then_inc(S["w0_split"], 1)
            dve.wait_ge(S["wt_loaded"], 16)
            dve.reduce_sum(T["wmean"][:, :], T["wt"][:, :, :], axis=AX.X).then_inc(S["dve"], 1)
            dve.wait_ge(S["dve"], 6)
            dve.tensor_scalar(T["wmean"][:, :], T["wmean"][:, :], 1.0 / C, None, ALU.mult).then_inc(S["dve"], 1)
            dve.wait_ge(S["dve"], 7)
            dve.tensor_tensor(T["wt"][:, :, :], T["wt"][:, :, :], bcast(T["wmean"][:, :], C), ALU.subtract)\
                .then_inc(S["wt_centred"], 1)
            dve.wait_ge(S["w0c_ready"], 1)
            dve.tensor_copy(T["w0c"][:, :], T["psT"][:, 0:TAPS0]).then_inc(S["w0c_copied"], 1)
            dve.wait_ge(S["gram_done"], 1)
            dve.tensor_copy(T["gram"][:, :], T["psT"][0:TAPS0, 16:16 + TAPS0]).then_inc(S["gram_ready"], 1)

        @block.tensor
        def _(pe):
            pe.wait_ge(S["ident_ready"], 1)
            pe.wait_ge(S["w0_centred"], 1)
            pe.transpose(T["psT"][:, 0:TAPS0], T["w0T"][:, :], T["ident"][0:TAPS0, 0:TAPS0])\
                .then_inc(S["w0c_ready"], 1)
            pe.wait_ge(S["w0c_copied"], 1)
            pe.matmul(T["psT"][0:TAPS0, 16:16 + TAPS0], T["w0c"][:, :], T["w0c"][:, :], start=True, stop=True)\
                .then_inc(S["gram_done"], 1)
        @block.scalar
        def _(act):
            act.wait_ge(S["ident_ready"], 1)
            act.activation(T["identb"][:, :], T["ident"][:, :], ACT.Copy).then_inc(S["identb_ready"], 1)


def x_chunk(io, c):
    return bass.AP(io["x"].tensor, io["x"].offset + c * STEP, [[STEP // P, P], [1, WIN]])


def stream(nc, T, S, io):
    lbuf = {0: T["l0"], 1: T["l1"], 2: T["l2"], 3: T["l3"]}
    psY, psT, psL, psPX = T["psY"], T["psT"], T["psL"], T["psPX"]
    psPb = psPX[:, :].bitcast(BF16)
    xs, p60, p60T = T["xs"], T["p60"], T["p60T"]
    patches = view(xs[:, :], [[STRIDE0, POS], [1, TAPS0]])

    def count(j, g):
        return (j + 1) * NG + g + 1

    def event(j, g):
        return GROUPS[g] + (g % BANKS, g % 2, count(j, g), 256 * j)

    END = (CHUNKS + 1) * NG
    TAIL = [(4, 0, 0, 0, END + 1, 256 * CHUNKS), (3, 0, 1, 1, END + 2, 0), (4, 0, 0, 0, END + 3, 256 * (CHUNKS + 1))]

    def tiles(layer):
        return 2 if layer == 4 else 4

    NEEDS = {4: (5, 1), 5: (7, 1), 6: (1, 0), 7: (3, 0)}

    def conv(pe, j, g):
        layer = GROUPS[g][0]
        pe.wait_ge(S["normed"], count(j, g) - BANKS)
        if layer == 1:
            if g == 0:
                pe.wait_ge(S["l0_ready"], 8 * (j + 1))
        else:
            need, back = NEEDS[g]
            pe.wait_ge(S["h_ready"], count(j - back, need))
        products(pe, event(j, g), lambda: layer0s(pe, j + 1, L0_MIDDLE.get(g, ())))

    def layer0s(pe, c, tiles):
        for i in tiles:
            layer0(pe, c, i)

    def products(pe, e, in_the_middle=None):
        layer, half, bank, _, _, _ = e
        src = lbuf[INPUT_OF[layer]]
        for t in range(tiles(layer)):
            if t == 2 and in_the_middle:
                in_the_middle()
            for k in range(3):
                at = 2 * (512 * half + P * t) + k
                mm = pe.matmul(psY[bank][:, t * C:(t + 1) * C], src[:, at:at + 2 * P - 1:2],
                               T["wt"][:, 3 * (layer - 1) + k, :], start=(k == 0), stop=(k == 2))
        mm.then_inc(S["conv_done"], 1)

    def transposes(pe, e):
        layer, _, _, par, number, _ = e
        pe.wait_ge(S["normed"], number)
        pe.wait_ge(S["h_ready"], number - 1)
        for t in range(tiles(layer)):
            mm = pe.transpose(psT[:, t * P:(t + 1) * P], T["yn"][:, par, t * C:(t + 1) * C], T["ident"][:, :])
        mm.then_inc(S["turned"], 1)

    def patch_transposes(pe, c, half):
        pe.wait_ge(S["patch_ready"], c + 1)
        if half == 0:
            pe.wait_ge(S["zz_done"], c + 3)
        else:
            pe.wait_ge(S["patch_copied"], 2 * c + 1)
        for n in range(8):
            q = 8 * half + n
            mm = pe.transpose(psPb[0:2 * ROWS, n * P:(n + 1) * P],
                              p60[:, 2 * q:2 * q + 2, :].rearrange("p a r -> p (a r)"), T["identb"][:, :])
        mm.then_inc(S["patch_turned"], 1)

    def window_transposes(pe, c):
        pe.wait_ge(S["x_loaded"], 16 * (c + 1))
        if not (isinstance(c, int) and c < 2):
            pe.wait_ge(S["patch_copied"], 2 * (c - 1))
        for h in range(2):
            at = h * STRIDE0 * HALF
            mm = pe.transpose(psPX[0:WINH, h * P:(h + 1) * P], xs[:, at:at + WINH], T["ident"][:, :])
        mm.then_inc(S["window_turned"], 1)

    def gram_product(pe, c):
        pe.wait_ge(S["window_copied"], c + 1)
        for h in range(2):
            mm = pe.matmul(psPX[:, h * HALF * TAPS0:(h + 1) * HALF * TAPS0], T["xT"][0:WINH, h, :],
                           T["band"][0:WINH, :], start=True, stop=True)
        mm.then_inc(S["gram_applied"], 1)

    def layer0(pe, c, i):
        if i % 4 == 0:
            pe.wait_ge(S["patch_copied"], 2 * c + i // 4 + 1)
        if not isinstance(c, int) or 8 * c + i >= 2:
            pe.wait_ge(S["l0_ready"], 8 * c + i - 1)
        q, slot = i // 2, i % 2
        pe.matmul(psL[i % 2][:, :], T["w60"][:, slot, :],
                  p60T[:, 4 * q:4 * q + 4, :].rearrange("r a p -> r (a p)"),
                  start=True, stop=True).then_inc(S["l0_done"], 1)

    def square(act, e):
        layer, _, bank, par, number, _ = e
        n = tiles(layer) * C
        act.wait_ge(S["conv_done"], number)
        act.wait_ge(S["summed"], number - 2)
        act.activation(T["sq"][:, par, 0:n], psY[bank][:, 0:n], ACT.Square).then_inc(S["squared"], 1)

    def gelu(act, e, carry=None):
        layer, half, _, _, number, column = e
        n = tiles(layer) * P
        act.wait_ge(S["turned"], number)
        if half == 0 and layer < 4:
            buf = lbuf[layer]
            act.wait_ge(S["h_ready"], number - 1)
            act.activation(buf[:, 0:1], buf[:, buf.shape[1] - 1:buf.shape[1]], ACT.Copy)\
                .then_inc(S[f"carried{layer}"], 1)
            act.wait_ge(S[f"carried{layer}"], carry)
        if layer == 4:
            dst = T["l4"][:, bass.ds(column, n)]
        else:
            dst = lbuf[layer][:, 1 + 512 * half:1 + 512 * half + n]
        act.activation(dst, psT[:, 0:n], ACT.Gelu, bias=T["cols"][:, 8 + layer:9 + layer],
                       scale=T["cols"][:, layer:layer + 1]).then_inc(S["h_ready"], 1)

    def gelu0(act, c, i):
        if i == 0:
            if not (isinstance(c, int) and c == 0):
                act.wait_ge(S["l0_ready"], 8 * c)
            act.wait_ge(S["l0_done"], 8 * c + 1)
            act.activation(T["l0"][:, 0:2], T["l0"][:, CHUNK:CHUNK + 2], ACT.Copy).then_inc(S["carried0"], 1)
            act.wait_ge(S["carried0"], c + 1)
        act.wait_ge(S["l0_done"], 8 * c + i + 1)
        q, slot = i // 2, i % 2
        act.activation(view(T["l0"][:, :], [[2, 4], [POS, P]], 2 + 8 * q + slot),
                       psL[i % 2][:, :].rearrange("c (a p) -> c a p", a=4), ACT.Gelu,
                       bias=T["cols"][:, 8:9], scale=T["cols"][:, 0:1]).then_inc(S["l0_ready"], 1)

    def stats(dve, e):
        layer, _, _, par, number, _ = e
        n = tiles(layer)
        dve.wait_ge(S["squared"], number)
        dve.reduce_sum(T["ss"][:, par, 0:n], T["sq"][:, par, 0:n * C].rearrange("p (t c) -> p t c", c=C), axis=AX.X)\
            .then_inc(S["summed"], 1)
        dve.wait_ge(S["summed"], number)
        dve.tensor_scalar(T["var"][:, par, 0:n], T["ss"][:, par, 0:n], 1.0 / C, EPS, ALU.mult, ALU.add)\
            .then_inc(S["var_ready"], 1)

    def normalise(dve, e):
        layer, _, bank, par, number, _ = e
        n = tiles(layer)
        dve.wait_ge(S["rstd_ready"], number)
        dve.wait_ge(S["turned"], number - 2)
        dve.tensor_tensor(T["yn"][:, par, 0:n * C].rearrange("p (t c) -> p t c", c=C),
                          psY[bank][:, 0:n * C].rearrange("p (t c) -> p t c", c=C),
                          bcast(T["rstd"][:, par, 0:n], C), ALU.mult).then_inc(S["normed"], 1)

    def copy_patches(dve, c, half):
        dve.wait_ge(S["patch_turned"], 2 * c + half + 1)
        if not (isinstance(c, int) and c == 0):
            dve.wait_ge(S["l0_done"], 8 * c)
        dve.tensor_copy(p60T[:, 8 * half:8 * half + 8, :].rearrange("r a p -> r (a p)"), psPb[0:2 * ROWS, :])\
            .then_inc(S["patch_copied"], 1)

    def copy_windows(dve, c):
        dve.wait_ge(S["window_turned"], c + 1)
        dve.tensor_copy(T["xT"][0:WINH, :, :].rearrange("r a p -> r (a p)"), psPX[0:WINH, 0:2 * P])\
            .then_inc(S["window_copied"], 1)

    def patch_squares(dve, c):
        dve.wait_ge(S["gram_applied"], c + 1)
        dve.tensor_tensor(T["zz"][:, :, :], psPX[:, 0:POS * TAPS0].rearrange("p (a k) -> p a k", k=TAPS0),
                          patches, ALU.mult).then_inc(S["zz_done"], 1)

    def patch_stats(dve, c):
        dve.wait_ge(S["zz_done"], c + 2)
        dve.reduce_sum(T["zs"][:, :], T["zz"][:, :, :], axis=AX.X).then_inc(S["zsum"], 1)
        dve.wait_ge(S["zsum"], c + 1)
        dve.tensor_scalar(T["zvar"][:, :], T["zs"][:, :], 1.0 / C, EPS, ALU.mult, ALU.add)\
            .then_inc(S["zvar_ready"], 1)

    def split_patches(dve, c, part):
        def at(n):
            return p60[:, :, n * TAPS0:(n + 1) * TAPS0]
        high, middle, low = ([n for n, (a, _) in enumerate(SPLIT) if a == want] for want in range(3))
        if part == 0:
            dve.wait_ge(S["zrstd_ready"], 4 * (c + 1))
            dve.tensor_tensor(T["scaled"][:, :, :], patches, bcast(T["zrstd"][:, :], TAPS0), ALU.mult)\
                .then_inc(S["scaled_ready"], 1)
            dve.wait_ge(S["scaled_ready"], 5 * c + 1)
            if not (isinstance(c, int) and c == 0):
                dve.wait_ge(S["patch_turned"], 2 * c)
            dve.tensor_copy(at(high[0]), T["scaled"][:, :, :]).then_inc(S["scaled_ready"], 1)
            dve.wait_ge(S["scaled_ready"], 5 * c + 2)
            dve.tensor_tensor(T["rest"][:, :, :], T["scaled"][:, :, :], at(high[0]), ALU.subtract)\
                .then_inc(S["scaled_ready"], 1)
            dve.wait_ge(S["scaled_ready"], 5 * c + 3)
            dve.tensor_copy(at(middle[0]), T["rest"][:, :, :]).then_inc(S["scaled_ready"], 1)
        else:
            dve.wait_ge(S["scaled_ready"], 5 * c + 4)
            dve.tensor_tensor(at(low[0]), T["rest"][:, :, :], at(middle[0]), ALU.subtract)
            for n in high[1:]:
                dve.tensor_copy(at(n), at(high[0]))
            dve.tensor_copy(at(middle[1]), at(middle[0])).then_inc(S["scaled_ready"], 1)
            dve.wait_ge(S["scaled_ready"], 5 * c + 5)
            dve.nop().then_inc(S["patch_ready"], 1)

    def root(pool, e):
        layer, _, _, par, number, _ = e
        n = tiles(layer)
        pool.wait_ge(S["var_ready"], number)
        pool.wait_ge(S["normed"], number - 2)
        pool.tensor_tensor(T["rstd"][:, par, 0:n], T["var"][:, par, 0:n], T["minus_half"][:, 0:n], ALU.pow)\
            .then_inc(S["rstd_ready"], 1)

    def patch_root(pool, c, part):
        pool.wait_ge(S["zvar_ready"], c + 1)
        s = slice(part * POS // 4, (part + 1) * POS // 4)
        pool.tensor_tensor(T["zrstd"][:, s], T["zvar"][:, s], T["minus_half"][:, 0:POS // 4], ALU.pow)\
            .then_inc(S["zrstd_ready"], 1)

    with nc.Block() as block:
        @block.sync
        def _(sp):
            def load(c):
                sp.wait_ge(S["scaled_ready"], 5 * c - 4)
                sp.dma_start(xs[:, :], x_chunk(io, c)).then_inc(S["x_loaded"], 16)
            load(1)
            load(2)
            with sp.Fori(0, CHUNKS) as j:
                load(j + 3)
            sp.wait_ge(S["x_loaded"], 16 * (CHUNKS + 3))

        @block.tensor
        def _(pe):
            pe.wait_ge(S["w60_loaded"], 16 * 2 * PARTS)
            pe.wait_ge(S["band_loaded"], 16 * HALF)
            for c in range(2):
                window_transposes(pe, c)
                gram_product(pe, c)
            patch_transposes(pe, 0, 0)
            patch_transposes(pe, 0, 1)
            layer0s(pe, 0, range(8))
            with pe.Fori(0, CHUNKS) as j:
                for g in range(NG):
                    conv(pe, j, g)
                    layer0s(pe, j + 1, L0_BEHIND.get(g, ()))
                    transposes(pe, event(j if g >= LAG else j - 1, (g - LAG) % NG))
                    if g == 0:
                        window_transposes(pe, j + 2)
                    if g == 1:
                        gram_product(pe, j + 2)
                    if g == 2:
                        patch_transposes(pe, j + 1, 0)
                    if g == 3:
                        patch_transposes(pe, j + 1, 1)
                    layer0s(pe, j + 1, L0_END.get(g, ()))
            transposes(pe, event(CHUNKS - 1, 6))
            transposes(pe, event(CHUNKS - 1, 7))
            for n, e in enumerate(TAIL):
                pe.wait_ge(S["h_ready"], END + n)
                products(pe, e)
                transposes(pe, e)

        @block.scalar
        def _(act):
            for i in range(8):
                gelu0(act, 0, i)
            with act.Fori(0, CHUNKS) as j:
                for g in range(NG):
                    for i in L0_MIDDLE.get(g, ()):
                        gelu0(act, j + 1, i)
                    square(act, event(j, g))
                    for i in L0_BEHIND.get(g, ()):
                        gelu0(act, j + 1, i)
                    back = 0 if g >= LAG else 1
                    gelu(act, event(j - back, (g - LAG) % NG), j - back + (2 if (g - LAG) % NG == 6 else 1))
                    for i in L0_END.get(g, ()):
                        gelu0(act, j + 1, i)
            gelu(act, event(CHUNKS - 1, 6), CHUNKS + 1)
            gelu(act, event(CHUNKS - 1, 7))
            for e in TAIL:
                square(act, e)
                gelu(act, e, CHUNKS + 1)

        @block.vector
        def _(dve):
            for name, n in (("normed", NG), ("turned", NG - LAG), ("h_ready", NG - LAG), ("summed", NG),
                            ("squared", NG), ("var_ready", NG), ("rstd_ready", NG), ("conv_done", NG), ("zz_done", 1)):
                dve.sem_inc(S[name], n)
            for c in range(2):
                copy_windows(dve, c)
                patch_squares(dve, c)
                patch_stats(dve, c)
                if c == 1:
                    copy_patches(dve, 0, 0)
                    copy_patches(dve, 0, 1)
                split_patches(dve, c, 0)
                split_patches(dve, c, 1)
            with dve.Fori(0, CHUNKS) as j:
                for g in range(NG):
                    if g == 0:
                        copy_windows(dve, j + 2)
                    stats(dve, event(j, g))
                    if g == 1:
                        patch_squares(dve, j + 2)
                    if g == 2:
                        copy_patches(dve, j + 1, 0)
                    if g == 3:
                        copy_patches(dve, j + 1, 1)
                    normalise(dve, event(j, g))
                    if g == 1:
                        patch_stats(dve, j + 2)
                    if g == 6:
                        split_patches(dve, j + 2, 0)
                    if g == 7:
                        split_patches(dve, j + 2, 1)
            for e in TAIL:
                stats(dve, e)
                normalise(dve, e)

        @block.gpsimd
        def _(pool):
            for c in range(2):
                for part in range(4):
                    patch_root(pool, c, part)
            with pool.Fori(0, CHUNKS) as j:
                for g in range(NG):
                    root(pool, event(j, g))
                    if 2 <= g <= 5:
                        patch_root(pool, j + 2, g - 2)
            for e in TAIL:
                root(pool, e)


D = 192
D1, D2 = 128, D - 128
LEN = 374
TOK = 125
TPB = 3
SEQ = TOK * TPB
TILES = B * TPB
N_EXPERT, HID = 4, 768
HC = HID // P
SOFT_E, SLOT, SOFT_H = 64, 16, 384
SLOTS = SOFT_E * SLOT
SC = SLOTS // P
SHC = SOFT_H // P


class Link:

    def __init__(self, eng, sem, per_round=0, round_=0):
        self.eng, self.sem, self.base, self.n = eng, sem, round_ * per_round, 0

    def __call__(self, ins):
        self.n += 1
        ins.then_inc(self.sem, 1)
        self.eng.wait_ge(self.sem, self.base + self.n)


def layers56(nc, T, S):
    psY, psT = [T["psY"][0], T["psY"][1]], T["psT"]

    def run(layer, groups, src, src_at, dst, sem):
        gap = 2 * SEQ
        s = {k: S[f"{k}{layer}"] for k in ("in", "conv", "sq", "sum", "var", "rstd", "norm", "turn", "out")}
        with nc.Block() as block:
            @block.tensor
            def _(pe):
                def turn(g):
                    pe.wait_ge(s["norm"], g + 1)
                    if g >= 1:
                        pe.wait_ge(s["out"], g)
                    for t in range(TPB):
                        mm = pe.transpose(psT[:, t * TOK:(t + 1) * TOK], T["yn"][0:TOK, g % 2, t * C:(t + 1) * C],
                                          T["ident"][0:TOK, 0:TOK])
                    mm.then_inc(s["turn"], 1)
                for g in range(groups):
                    pe.wait_ge(s["in"], g + 1)
                    if g >= 2:
                        pe.wait_ge(s["norm"], g - 1)
                    for t in range(TPB):
                        for k in range(2):
                            at = 2 * TOK * t + k
                            mm = pe.matmul(psY[g % 2][0:TOK, t * C:(t + 1) * C],
                                           T["stage"][:, g % 2, at:at + 2 * TOK - 1:2],
                                           T["wt"][:, 12 + 2 * (layer - 5) + k, :], start=(k == 0), stop=(k == 1))
                    mm.then_inc(s["conv"], 1)
                    if g >= 1:
                        turn(g - 1)
                turn(groups - 1)

            @block.scalar
            def _(act):
                def gelu(g):
                    act.wait_ge(s["turn"], g + 1)
                    act.activation(T[dst][:, g * SEQ:(g + 1) * SEQ], psT[:, 0:SEQ], ACT.Gelu,
                                   bias=T["cols"][:, 8 + layer:9 + layer],
                                   scale=T["cols"][:, layer:layer + 1]).then_inc(s["out"], 1)
                for g in range(groups):
                    act.wait_ge(s["conv"], g + 1)
                    if g >= 2:
                        act.wait_ge(s["sum"], g - 1)
                    act.activation(T["sq"][0:TOK, g % 2, 0:TPB * C], psY[g % 2][0:TOK, 0:TPB * C], ACT.Square)\
                        .then_inc(s["sq"], 1)
                    if g >= 1:
                        gelu(g - 1)
                gelu(groups - 1)

            @block.vector
            def _(dve):
                def place(g):
                    if g >= 2:
                        dve.wait_ge(s["conv"], g - 1)
                    dve.tensor_copy(T["stage"][:, g % 2, 0:gap], T[src][:, src_at + g * gap:src_at + (g + 1) * gap])\
                        .then_inc(s["in"], 1)
                place(0)
                for g in range(groups):
                    if g + 1 < groups:
                        place(g + 1)
                    dve.wait_ge(s["sq"], g + 1)
                    dve.reduce_sum(T["ss"][0:TOK, g % 2, 0:TPB],
                                   T["sq"][0:TOK, g % 2, 0:TPB * C].rearrange("p (t c) -> p t c", c=C), axis=AX.X)\
                        .then_inc(s["sum"], 1)
                    dve.wait_ge(s["sum"], g + 1)
                    dve.tensor_scalar(T["var"][0:TOK, g % 2, 0:TPB], T["ss"][0:TOK, g % 2, 0:TPB], 1.0 / C, EPS,
                                      ALU.mult, ALU.add).then_inc(s["var"], 1)
                    dve.wait_ge(s["rstd"], g + 1)
                    if g >= 2:
                        dve.wait_ge(s["turn"], g - 1)
                    dve.tensor_tensor(T["yn"][0:TOK, g % 2, 0:TPB * C].rearrange("p (t c) -> p t c", c=C),
                                      psY[g % 2][0:TOK, 0:TPB * C].rearrange("p (t c) -> p t c", c=C),
                                      bcast(T["rstd"][0:TOK, g % 2, 0:TPB], C), ALU.mult).then_inc(s["norm"], 1)

            @block.gpsimd
            def _(pool):
                for g in range(groups):
                    pool.wait_ge(s["var"], g + 1)
                    if g >= 2:
                        pool.wait_ge(s["norm"], g - 1)
                    pool.tensor_tensor(T["rstd"][0:TOK, g % 2, 0:TPB], T["var"][0:TOK, g % 2, 0:TPB],
                                       T["minus_half"][0:TOK, 0:TPB], ALU.pow).then_inc(s["rstd"], 1)

    run(5, 2 * B, "l4", 513, "l5", "l5_ready")
    run(6, B, "l5", 0, "l6", "l6_ready")


def norm_stats(dve, T, S, link, k, get, width):
    for t in range(TPB):
        ins = dve.bn_stats(T["bn"][0:TOK, t, :], get(t))
    link(ins)
    for t in range(TPB):
        ins = dve.bn_aggr(T["mv"][0:TOK, t, :], T["bn"][0:TOK, t, :])
    link(ins)
    dve.tensor_scalar(T["nvar"][0:TOK, 0:TPB], T["mv"][0:TOK, :, 1], EPS, None, ALU.add).then_inc(S["nvar"], 1)
    dve.wait_ge(S["nroot"], k + 1)


def norm_root(pool, T, S, k):
    pool.wait_ge(S["nvar"], k + 1)
    pool.tensor_tensor(T["nrstd"][0:TOK, 0:TPB], T["nvar"][0:TOK, 0:TPB], T["minus_half"][0:TOK, 0:TPB], ALU.pow)\
        .then_inc(S["nroot"], 1)


def norm_apply(dve, T, get, out):
    for t in range(TPB):
        ins = dve.tensor_scalar(out(t), get(t), T["mv"][0:TOK, t, 0:1], T["nrstd"][0:TOK, t:t + 1],
                                ALU.subtract, ALU.mult)
    return ins


def htile(T, b, t):
    return T["h"][0:TOK, TPB * b + t, :]


def tokens(nc, T, S):
    pA, pB, pC, pD = T["ps"][0], T["ps"][1], T["ps"][2], T["ps"][3]
    nTok, nCh = T["tA"], T["tB"]
    with nc.Block() as block:
        @block.tensor
        def _(pe):
            for b in range(B):
                if b >= 1:
                    pe.wait_ge(S["tok_normed"], b)
                for t in range(TPB):
                    mm = pe.transpose(pA[0:TOK, t * C:(t + 1) * C],
                                      T["l6"][:, b * SEQ + t * TOK:b * SEQ + (t + 1) * TOK], T["ident"][:, :])
                mm.then_inc(S["tok_turned"], 1)
                pe.wait_ge(S["tok_normed"], b + 1)
                if b >= 1:
                    pe.wait_ge(S["tok_affine"], b)
                for t in range(TPB):
                    mm = pe.transpose(pB[:, t * TOK:(t + 1) * TOK], nTok[0:TOK, t * C:(t + 1) * C],
                                      T["ident"][0:TOK, 0:TOK])
                mm.then_inc(S["tok_back"], 1)
                pe.wait_ge(S["tok_affine"], b + 1)
                if b >= 1:
                    pe.wait_ge(S["tok_out"], b)
                for t in range(TPB):
                    mm = pe.matmul((pC[0:TOK, t * D:(t + 1) * D] if t < 2 else pD[0:TOK, 0:D]),
                                   nCh[:, t * TOK:(t + 1) * TOK], T["proj_w"][:, :], start=True, stop=True)
                mm.then_inc(S["tok_projected"], 1)

        @block.vector
        def _(dve):
            for b in range(B):
                link = Link(dve, S["tok_link"], 2, b)
                dve.wait_ge(S["tok_turned"], b + 1)
                get = lambda t: pA[0:TOK, t * C:(t + 1) * C]
                norm_stats(dve, T, S, link, b, get, C)
                norm_apply(dve, T, get, lambda t: nTok[0:TOK, t * C:(t + 1) * C]).then_inc(S["tok_normed"], 1)
                dve.wait_ge(S["tok_projected"], b + 1)
                for t in range(TPB):
                    ins = dve.tensor_tensor(htile(T, b, t), pC[0:TOK, t * D:(t + 1) * D] if t < 2 else pD[0:TOK, 0:D],
                                            T["rows"][0:TOK, 0, :], ALU.add)
                ins.then_inc(S["tok_out"], 1)

        @block.gpsimd
        def _(pool):
            for b in range(B):
                norm_root(pool, T, S, b)

        @block.scalar
        def _(act):
            for b in range(B):
                act.wait_ge(S["tok_back"], b + 1)
                act.activation(nCh[:, 0:SEQ], pB[:, 0:SEQ], ACT.Identity, bias=T["cols"][:, 15:16],
                               scale=T["cols"][:, 7:8]).then_inc(S["tok_affine"], 1)


def ssm_tables(nc, T, S):
    v = T["sv"]
    names = ("dt are r th k y cos sin nr ni dr di q0 q1 q2 qr qi cm sm c2 s2 tmp ay").split()
    col = {n: v[:, i:i + 1] for i, n in enumerate(names)}
    logA, Aim, logdt = (T["cols"][:, 16 + i:17 + i] for i in range(3))
    TWO_PI = 6.283185307179586
    C1 = 6.28125
    C2 = 0.0019340515136718750
    C3 = TWO_PI - C1 - C2
    MAGIC = 12582912.0
    steps = LEN
    with nc.Block() as block:
        @block.scalar
        def _(act):
            act.activation(col["dt"], logdt, ACT.Exp)
            act.activation(col["are"], logA, ACT.Exp).then_inc(S["ssm_exp"], 1)
            act.wait_ge(S["ssm_r"], 1)
            act.activation(col["r"], col["nr"], ACT.Exp, scale=-1.0).then_inc(S["ssm_exp"], 1)
            act.wait_ge(S["ssm_angle"], 1)
            act.activation(col["sin"], col["y"], ACT.Sin)
            act.activation(col["cos"], col["ay"], ACT.Sin).then_inc(S["ssm_exp"], 1)

        @block.vector
        def _(dve):
            link = Link(dve, S["ssm_link"])
            tt = lambda o, a, b_, op: link(dve.tensor_tensor(o, a, b_, op))
            ts = lambda o, a, s1, s2, op0, op1=ALU.bypass: link(dve.tensor_scalar(o, a, s1, s2, op0, op1))
            stt = lambda o, a, s, b_, op0, op1: link(dve.scalar_tensor_tensor(out=o, in0=a, scalar=s, in1=b_, op0=op0, op1=op1))
            dve.wait_ge(S["ssm_exp"], 1)
            dve.tensor_tensor(col["nr"], col["are"], col["dt"], ALU.mult).then_inc(S["ssm_r"], 1)
            tt(col["th"], Aim, col["dt"], ALU.mult)
            ts(col["k"], col["th"], 1.0 / TWO_PI, None, ALU.mult)
            ts(col["k"], col["k"], MAGIC, None, ALU.add)
            ts(col["k"], col["k"], MAGIC, None, ALU.subtract)
            stt(col["y"], col["k"], -C1, col["th"], ALU.mult, ALU.add)
            stt(col["y"], col["k"], -C2, col["y"], ALU.mult, ALU.add)
            stt(col["y"], col["k"], -C3, col["y"], ALU.mult, ALU.add)
            ts(col["y"], col["y"], 3.1415925, -3.1415925, ALU.min, ALU.max)
            ts(col["tmp"], col["y"], -1.0, None, ALU.mult)
            tt(col["ay"], col["y"], col["tmp"], ALU.max)
            dve.tensor_scalar(col["ay"], col["ay"], -1.0, TWO_PI / 4, ALU.mult, ALU.add).then_inc(S["ssm_angle"], 1)
            dve.wait_ge(S["ssm_exp"], 3)
            tt(col["nr"], col["r"], col["cos"], ALU.mult)
            ts(col["nr"], col["nr"], -1.0, None, ALU.add)
            tt(col["ni"], col["r"], col["sin"], ALU.mult)
            ts(col["dr"], col["are"], -1.0, 1e-8, ALU.mult, ALU.add)
            tt(col["q0"], col["dr"], col["dr"], ALU.mult)
            tt(col["q1"], Aim, Aim, ALU.mult)
            tt(col["q0"], col["q0"], col["q1"], ALU.add)
            link(dve.reciprocal(col["q0"], col["q0"]))
            tt(col["qr"], col["ni"], Aim, ALU.mult)
            stt(col["qr"], col["nr"], col["dr"], col["qr"], ALU.mult, ALU.add)
            tt(col["qr"], col["qr"], col["q0"], ALU.mult)
            tt(col["qi"], col["nr"], Aim, ALU.mult)
            stt(col["qi"], col["ni"], col["dr"], col["qi"], ALU.mult, ALU.subtract)
            tt(col["qi"], col["qi"], col["q0"], ALU.mult)
            Cr, Ci, Wr, Wi = T["CT"][:, 0, :], T["CT"][:, 1, :], T["Cq"][:, 0, :], T["Cq"][:, 1, :]
            ts(Wr, Ci, col["qi"], None, ALU.mult)
            stt(Wr, Cr, col["qr"], Wr, ALU.mult, ALU.subtract)
            ts(Wi, Cr, col["qi"], -1.0, ALU.mult, ALU.mult)
            ts(T["Ctmp"][:, :], Ci, col["qr"], None, ALU.mult)
            tt(Wi, Wi, T["Ctmp"][:, :], ALU.subtract)
            cos, sin = T["cosT"], T["sinT"]
            link(dve.memset(cos[:, 0:1], 1.0))
            link(dve.memset(sin[:, 0:1], 0.0))
            ts(col["cm"], col["cos"], 1.0, None, ALU.mult)
            ts(col["sm"], col["sin"], 1.0, None, ALU.mult)
            m = 1
            while m < steps:
                n = min(m, steps - m)
                ts(T["rot"][:, 0:n], sin[:, 0:n], col["sm"], None, ALU.mult)
                stt(cos[:, m:m + n], cos[:, 0:n], col["cm"], T["rot"][:, 0:n], ALU.mult, ALU.subtract)
                ts(T["rot"][:, 0:n], cos[:, 0:n], col["sm"], None, ALU.mult)
                stt(sin[:, m:m + n], sin[:, 0:n], col["cm"], T["rot"][:, 0:n], ALU.mult, ALU.add)
                tt(col["c2"], col["cm"], col["cm"], ALU.mult)
                tt(col["s2"], col["sm"], col["sm"], ALU.mult)
                ts(col["sm"], col["sm"], col["cm"], 2.0, ALU.mult, ALU.mult)
                tt(col["cm"], col["c2"], col["s2"], ALU.subtract)
                m *= 2


def state_space(nc, T, S):
    pA, pB, pR, pI = T["ps"][0], T["ps"][1], T["ps"][2], T["ps"][3]
    pO = [T["ps"][4], T["ps"][5]]
    u, uA, uB = T["u"], T["uA"], T["uB"]
    cos, sin = T["cosT"][:, 0:LEN], T["sinT"][:, 0:LEN]
    decay = view(T["sv"][:, 2:3], [[0, LEN]])
    m1, m2, vr, vi, gr, gi, xr, xi = (T["seq"][:, i, 0:LEN] for i in range(8))
    with nc.Block() as block:
        @block.tensor
        def _(pe):
            for b in range(B):
                pe.wait_ge(S["u_ready"], b + 1)
                if b >= 1:
                    pe.wait_ge(S["uT_ready"], 2 * b)
                for t in range(TPB):
                    pe.transpose(pA[:, t * TOK:(t + 1) * TOK], u[0:TOK, b % 2, t, 0:D1], T["ident"][0:TOK, 0:TOK])
                    mm = pe.transpose(pB[0:D2, t * TOK:(t + 1) * TOK], u[0:TOK, b % 2, t, D1:D],
                                      T["ident"][0:TOK, 0:TOK])
                mm.then_inc(S["u_turned"], 1)
                pe.wait_ge(S["uT_ready"], 2 * (b + 1))
                if b >= 1:
                    pe.wait_ge(S["ssm_in"], b)
                for part, dst in ((0, pR), (1, pI)):
                    pe.matmul(dst[:, 0:LEN], T["BTa"][:, part, :], uA[:, 0:LEN], start=True, stop=False)
                    mm = pe.matmul(dst[:, 0:LEN], T["BTb"][:, part, :], uB[:, 0:LEN], start=False, stop=True)
                mm.then_inc(S["Bu_ready"], 1)
                pe.wait_ge(S["x_ready"], b + 1)
                if b >= 1:
                    pe.wait_ge(S["ssm_out"], b)
                for t in range(TPB):
                    n = min(TOK, LEN - t * TOK)
                    o = pO[t // 2][0:n, (t % 2) * D:(t % 2 + 1) * D]
                    pe.matmul(o, xr[:, t * TOK:t * TOK + n], T["Cq"][:, 0, :], start=True, stop=False)
                    mm = pe.matmul(o, xi[:, t * TOK:t * TOK + n], T["Cq"][:, 1, :], start=False, stop=True)
                mm.then_inc(S["y_ready"], 1)

        @block.scalar
        def _(act):
            for b in range(B):
                act.wait_ge(S["u_turned"], b + 1)
                if b >= 1:
                    act.wait_ge(S["Bu_ready"], b)
                act.activation(uA[:, 0:SEQ], pA[:, 0:SEQ], ACT.Copy).then_inc(S["uT_ready"], 1)
                act.activation(uB[:, 0:SEQ], pB[0:D2, 0:SEQ], ACT.Copy).then_inc(S["uT_ready"], 1)

        @block.gpsimd
        def _(pool):
            for b in range(B):
                norm_root(pool, T, S, B + b)

        @block.vector
        def _(dve):
            def norm(b):
                link = Link(dve, S["ssm_nlink"], 2, b)
                norm_stats(dve, T, S, link, B + b, lambda t: htile(T, b, t), D)
                norm_apply(dve, T, lambda t: htile(T, b, t), lambda t: u[0:TOK, b % 2, t, :]).then_inc(S["u_ready"], 1)
            norm(0)
            for b in range(B):
                if b + 1 < B:
                    norm(b + 1)
                dve.wait_ge(S["Bu_ready"], b + 1)
                link = Link(dve, S["ssm_slink"], 9, b)
                R, I = pR[:, 0:LEN], pI[:, 0:LEN]
                tt = lambda o, a, b_, op: dve.tensor_tensor(o, a, b_, op)
                tt(m1, R, cos, ALU.mult)
                link(tt(m2, I, sin, ALU.mult))
                link(tt(vr, m1, m2, ALU.add))
                tt(m1, I, cos, ALU.mult)
                ins = tt(m2, R, sin, ALU.mult)
                link(ins)
                dve.nop().then_inc(S["ssm_in"], 1)
                link(tt(vi, m1, m2, ALU.subtract))
                dve.tensor_tensor_scan(gr, decay, vr, 0.0, ALU.mult, ALU.add)
                link(dve.tensor_tensor_scan(gi, decay, vi, 0.0, ALU.mult, ALU.add))
                tt(m1, gr, cos, ALU.mult)
                link(tt(m2, gi, sin, ALU.mult))
                if b >= 1:
                    dve.wait_ge(S["y_ready"], b)
                link(tt(xr, m1, m2, ALU.subtract))
                tt(m1, gi, cos, ALU.mult)
                link(tt(m2, gr, sin, ALU.mult))
                link(tt(xi, m1, m2, ALU.add))
                dve.nop().then_inc(S["x_ready"], 1)
                ub = u[0:TOK, b % 2, :, :]
                hb = T["h"][0:TOK, TPB * b:TPB * (b + 1), :]
                Drow = view(T["rows"][0:TOK, 1, :], [[0, TPB], [1, D]])
                tt(T["uD"][0:TOK, :, :], ub, Drow, ALU.mult).then_inc(S["ssm_blink"], 1)
                dve.wait_ge(S["ssm_blink"], 2 * b + 1)
                tt(hb, hb, T["uD"][0:TOK, :, :], ALU.add).then_inc(S["ssm_blink"], 1)
                dve.wait_ge(S["ssm_blink"], 2 * b + 2)
                dve.wait_ge(S["y_ready"], b + 1)
                for t in range(TPB):
                    n = min(TOK, LEN - t * TOK)
                    ins = tt(htile(T, b, t)[0:n], htile(T, b, t)[0:n], pO[t // 2][0:n, (t % 2) * D:(t % 2 + 1) * D],
                             ALU.add)
                ins.then_inc(S["ssm_out"], 1)


def turn_tiles(pe, T, src, b, pA, pB):
    for t in range(TPB):
        pe.transpose(pA[:, t * TOK:(t + 1) * TOK], src[0:TOK, b % 2, t, 0:D1], T["ident"][0:TOK, 0:TOK])
        mm = pe.transpose(pB[0:D2, t * TOK:(t + 1) * TOK], src[0:TOK, b % 2, t, D1:D], T["ident"][0:TOK, 0:TOK])
    return mm


def routed_ffn(nc, T, S):
    ps = T["ps"]
    pA, pB, pG, pH, pO = ps[0], ps[1], ps[2], [ps[3], ps[4]], [ps[5], ps[6]]
    v, vA, vB, G = T["u"], T["vA"], T["vB"], T["G"]
    CH = N_EXPERT * HC
    OUTS = N_EXPERT + 1
    with nc.Block() as block:
        @block.tensor
        def _(pe):
            def turn(b):
                pe.wait_ge(S["v_ready"], b + 1)
                if b >= 1:
                    pe.wait_ge(S["vT_ready"], 2 * b)
                turn_tiles(pe, T, v, b, pA, pB).then_inc(S["v_turned"], 1)

            def up(b, e):
                for c in range(HC):
                    k = b * CH + e * HC + c
                    if k >= 2:
                        pe.wait_ge(S["hid_ready"], k - 1)
                    w = slice(e * HID + c * P, e * HID + (c + 1) * P)
                    pe.matmul(pH[k % 2][:, 0:SEQ], T["w1a"][:, w], vA[:, b % 2, :], start=True, stop=False)
                    pe.matmul(pH[k % 2][:, 0:SEQ], T["w1b"][:, w], vB[:, b % 2, :], start=False, stop=True)\
                        .then_inc(S["hid_done"], 1)

            def out(b, e):
                k = b * OUTS + e
                if k >= 1:
                    pe.wait_ge(S["picked"], k)
                if e == N_EXPERT:
                    pe.wait_ge(S["maskT_ready"], b + 1)
                else:
                    pe.wait_ge(S["hid_ready"], b * CH + (e + 1) * HC)
                for t in range(TPB):
                    o = pO[t // 2][0:TOK, (t % 2) * D:(t % 2 + 1) * D]
                    s = slice(t * TOK, (t + 1) * TOK)
                    if e == N_EXPERT:
                        mm = pe.matmul(o, T["maskT"][:, s], T["b2"][:, :], start=True, stop=True)
                    else:
                        for c in range(HC):
                            mm = pe.matmul(o, G[:, (e % 2) * HC + c, s], T["w2"][:, e * HC + c, :],
                                           start=(c == 0), stop=(c == HC - 1))
                mm.then_inc(S["out_done"], 1)
            turn(0)
            for b in range(B):
                pe.wait_ge(S["vT_ready"], 2 * (b + 1))
                if b >= 1:
                    pe.wait_ge(S["maskT_ready"], b)
                for t in range(TPB):
                    s = slice(t * TOK, (t + 1) * TOK)
                    o = pG[0:TOK, t * N_EXPERT:(t + 1) * N_EXPERT]
                    pe.matmul(o, vA[:, b % 2, s], T["gate_wa"][:, :], start=True, stop=False)
                    mm = pe.matmul(o, vB[:, b % 2, s], T["gate_wb"][:, :], start=False, stop=True)
                mm.then_inc(S["scores_ready"], 1)
                for e in range(N_EXPERT):
                    up(b, e)
                    if e == 1:
                        pe.wait_ge(S["mask_ready"], b + 1)
                        for t in range(TPB):
                            mm = pe.transpose(pG[0:N_EXPERT, t * TOK:(t + 1) * TOK], T["mask"][0:TOK, b % 2, t, :],
                                              T["ident"][0:TOK, 0:TOK])
                        mm.then_inc(S["mask_turned"], 1)
                    if e >= 1:
                        out(b, e - 1)
                    if e == 2 and b + 1 < B:
                        turn(b + 1)
                out(b, N_EXPERT - 1)
                out(b, N_EXPERT)

        @block.scalar
        def _(act):
            def copy(b):
                act.wait_ge(S["v_turned"], b + 1)
                if b >= 2:
                    act.wait_ge(S["hid_done"], CH * (b - 1))
                act.activation(vA[:, b % 2, :], pA[:, 0:SEQ], ACT.Copy).then_inc(S["vT_ready"], 1)
                act.activation(vB[:, b % 2, :], pB[0:D2, 0:SEQ], ACT.Copy).then_inc(S["vT_ready"], 1)
            copy(0)
            for b in range(B):
                act.wait_ge(S["z_ready"], b + 1)
                act.activation(T["ez"][0:TOK, :, :], T["z"][0:TOK, :, :], ACT.Exp).then_inc(S["ez_ready"], 1)
                for e in range(N_EXPERT):
                    for c in range(HC):
                        k = b * CH + e * HC + c
                        act.wait_ge(S["hid_done"], k + 1)
                        if k >= 2 * HC:
                            kb, ke = divmod(k // HC - 2, N_EXPERT)
                            act.wait_ge(S["out_done"], kb * OUTS + ke + 1)
                        act.activation(G[:, (e % 2) * HC + c, :], pH[k % 2][:, 0:SEQ], ACT.Gelu,
                                       bias=T["b1"][:, e * HC + c:e * HC + c + 1]).then_inc(S["hid_ready"], 1)
                    if e == 2 and b + 1 < B:
                        copy(b + 1)

        @block.gpsimd
        def _(pool):
            for b in range(B):
                norm_root(pool, T, S, 2 * B + b)

        @block.vector
        def _(dve):
            def norm(b):
                link = Link(dve, S["ffn_nlink"], 2, b)
                norm_stats(dve, T, S, link, 2 * B + b, lambda t: htile(T, b, t), D)
                if b >= 2:
                    dve.wait_ge(S["v_turned"], b - 1)
                norm_apply(dve, T, lambda t: htile(T, b, t), lambda t: v[0:TOK, b % 2, t, :]).then_inc(S["v_ready"], 1)

            def gate(b):
                z, ez, m = T["z"][0:TOK, :, :], T["ez"][0:TOK, :, :], T["mask"][0:TOK, b % 2, :, :]
                top, left = T["top"][0:TOK, :], T["left"][0:TOK, :]
                link = Link(dve, S["gate_link"], 13, b)
                dve.wait_ge(S["scores_ready"], b + 1)
                shift = view(T["gate_row"][0:TOK, 2 * N_EXPERT:3 * N_EXPERT], [[0, TPB], [1, N_EXPERT]])
                link(dve.tensor_tensor(z, pG[0:TOK, 0:TPB * N_EXPERT].rearrange("p (t e) -> p t e", e=N_EXPERT),
                                       shift, ALU.add))
                link(dve.tensor_reduce(top, z, AX.X, ALU.max))
                dve.tensor_tensor(z, z, bcast(top, N_EXPERT), ALU.subtract).then_inc(S["z_ready"], 1)
                dve.wait_ge(S["ez_ready"], b + 1)
                link(dve.reduce_sum(top, ez, axis=AX.X))
                link(dve.reciprocal(top, top))
                link(dve.tensor_tensor(ez, ez, bcast(top, N_EXPERT), ALU.mult))
                link(dve.tensor_reduce(top, ez, AX.X, ALU.max))
                link(dve.tensor_tensor(m, ez, bcast(top, N_EXPERT), ALU.is_ge))
                link(dve.tensor_scalar(left, m[:, :, 0], -1.0, 1.0, ALU.mult, ALU.add))
                for e in range(1, N_EXPERT):
                    link(dve.tensor_tensor(m[:, :, e], m[:, :, e], left, ALU.mult))
                    if e + 1 < N_EXPERT:
                        link(dve.tensor_tensor(left, left, m[:, :, e], ALU.subtract))
                dve.nop().then_inc(S["mask_ready"], 1)
                dve.wait_ge(S["mask_turned"], b + 1)
                if b >= 1:
                    dve.wait_ge(S["out_done"], OUTS * b)
                dve.tensor_copy(T["maskT"][:, :], pG[0:N_EXPERT, 0:SEQ]).then_inc(S["maskT_ready"], 1)

            dve.wait_ge(S["rows_loaded"], 16 * 2)
            dve.tensor_tensor(T["gate_row"][0:TOK, 2 * N_EXPERT:3 * N_EXPERT], T["gate_row"][0:TOK, 0:N_EXPERT],
                              T["gate_row"][0:TOK, N_EXPERT:2 * N_EXPERT], ALU.subtract).then_inc(S["shift_ready"], 1)
            dve.wait_ge(S["shift_ready"], 1)
            norm(0)
            for b in range(B):
                gate(b)
                if b + 1 < B:
                    norm(b + 1)
                for e in range(OUTS):
                    k = b * OUTS + e
                    dve.wait_ge(S["out_done"], k + 1)
                    if k >= 1:
                        dve.wait_ge(S["picked"], k)
                    for t in range(TPB):
                        o = pO[t // 2][0:TOK, (t % 2) * D:(t % 2 + 1) * D]
                        h = htile(T, b, t)
                        if e == N_EXPERT:
                            ins = dve.tensor_tensor(h, h, o, ALU.add)
                        else:
                            ins = dve.scalar_tensor_tensor(out=h, in0=o, scalar=T["mask"][0:TOK, b % 2, t, e:e + 1],
                                                           in1=h, op0=ALU.mult, op1=ALU.add)
                    ins.then_inc(S["picked"], 1)
                    dve.wait_ge(S["picked"], k + 1)


def two_way_scan(nc, T, S):
    ps = T["ps"]
    pA, pB, pX, pC, pO = ps[0], ps[1], [ps[2], ps[3]], [ps[4], ps[5], ps[6]], [ps[7], ps[1]]
    a, xh, nA, nB, xA, xB = T["u"], T["xh"], T["nA"], T["nB"], T["xA"], T["xB"]
    cols = lambda i, m: T["mcol"][:, 3 * i + m:3 * i + m + 1]
    BIAS, LOGIT, B_, C_, D_, BB, DB = range(7)
    zA, zB = T["zA"], T["zB"]
    with nc.Block() as block:
        @block.tensor
        def _(pe):
            for b in range(B):
                pe.wait_ge(S["xh_ready"], b + 1)
                if b >= 1:
                    pe.wait_ge(S["two_out"], b)
                turn_tiles(pe, T, xh, 0, pA, pB).then_inc(S["xh_turned"], 1)
                pe.wait_ge(S["n_ready"], 2 * (b + 1))
                for i in range(4):
                    k = 4 * b + i
                    if k >= 2:
                        pe.wait_ge(S["proj_read"], k - 1)
                    o = pX[k % 2][:, 0:LEN]
                    pe.matmul(o, T["Wia"][:, i, :], nA[:, 0:LEN], start=True, stop=False)
                    pe.matmul(o, T["Wib"][:, i, :], nB[:, 0:LEN], start=False, stop=True).then_inc(S["proj_done"], 1)
                pe.wait_ge(S["proj_read"], 4 * b + 2)
                for m in range(3):
                    if b >= 1:
                        pe.wait_ge(S["conv_read"], 6 * (b - 1) + 2 * (m + 1))
                    o = pC[m][:, 0:LEN]
                    for k in range(3):
                        pe.matmul(o, T["Wca"][:, k, m * P:(m + 1) * P], xA[:, k:k + LEN], start=(k == 0), stop=False)
                    pe.matmul(o, T["Wcb"][:, m * P:(m + 1) * P], xB[:, 0:LEN], start=False, stop=False)
                    pe.matmul(o, T["Wcc"][0:D2, m * P:(m + 1) * P], xB[0:D2, 2:2 + LEN], start=False, stop=True)\
                        .then_inc(S["conv2_done"], 1)
                pe.wait_ge(S["y2_ready"], b + 1)
                for t in range(TPB):
                    n = min(TOK, LEN - t * TOK)
                    o = pO[t // 2][0:n, (t % 2) * D:(t % 2 + 1) * D]
                    pe.matmul(o, T["yA"][:, t * TOK:t * TOK + n], T["Woa"][:, :], start=True, stop=False)
                    mm = pe.matmul(o, T["yB"][:, t * TOK:t * TOK + n], T["Wob"][:, :], start=False, stop=True)
                mm.then_inc(S["two_done"], 1)

        @block.scalar
        def _(act):
            for b in range(B):
                act.wait_ge(S["xh_turned"], b + 1)
                if b >= 1:
                    act.wait_ge(S["proj_done"], 4 * b)
                act.activation(nA[:, 0:SEQ], pA[:, 0:SEQ], ACT.Identity, bias=T["lncol"][:, 2:3],
                               scale=T["lncol"][:, 0:1]).then_inc(S["n_ready"], 1)
                act.activation(nB[:, 0:SEQ], pB[0:D2, 0:SEQ], ACT.Identity, bias=T["lncol"][0:D2, 3:4],
                               scale=T["lncol"][0:D2, 1:2]).then_inc(S["n_ready"], 1)
                if b >= 1:
                    act.wait_ge(S["conv2_done"], 3 * b)
                    act.wait_ge(S["y2_ready"], b)
                bi = lambda i, lo=0, hi=P: T["lncol"][lo:hi, 4 + i:5 + i]
                for i in range(4):
                    k = 4 * b + i
                    act.wait_ge(S["proj_done"], k + 1)
                    src = pX[k % 2]
                    if i == 0:
                        ins = act.activation(xA[:, 1:1 + LEN], src[:, 0:LEN], ACT.Identity, bias=bi(i))
                    elif i == 1:
                        act.activation(xB[0:D2, 1:1 + LEN], src[0:D2, 0:LEN], ACT.Identity, bias=bi(i, 0, D2))
                        ins = act.activation(xB[D2:P, 0:LEN], src[D2:P, 0:LEN], ACT.Identity, bias=bi(i, D2, P))
                    else:
                        ins = act.activation((zA if i == 2 else zB)[:, 0:LEN], src[:, 0:LEN], ACT.Silu, bias=bi(i))
                    ins.then_inc(S["proj_read"], 1)
                for m in range(3):
                    act.wait_ge(S["conv2_done"], 3 * b + m + 1)
                    act.activation(T["bu"][:, m, 0:LEN], pC[m][:, 0:LEN], ACT.Identity, bias=cols(BB, m), scale=cols(B_, m))\
                        .then_inc(S["conv_read"], 1)
                    act.activation(T["du"][:, m, 0:LEN], pC[m][:, 0:LEN], ACT.Identity, bias=cols(DB, m), scale=cols(D_, m))\
                        .then_inc(S["conv_read"], 1)

        @block.gpsimd
        def _(pool):
            for b in range(B):
                norm_root(pool, T, S, 3 * B + 2 * b)
                norm_root(pool, T, S, 3 * B + 2 * b + 1)

        @block.vector
        def _(dve):
            def norm(b):
                link = Link(dve, S["two_nlink"], 5, b)
                norm_stats(dve, T, S, link, 3 * B + 2 * b, lambda t: htile(T, b, t), D)
                at = lambda t: a[0:TOK, b % 2, t, :]
                link(norm_apply(dve, T, lambda t: htile(T, b, t), at))
                norm_stats(dve, T, S, link, 3 * B + 2 * b + 1, at, D)
                if b >= 1:
                    dve.wait_ge(S["xh_turned"], b)
                norm_apply(dve, T, at, lambda t: xh[0:TOK, 0, t, :]).then_inc(S["xh_ready"], 1)
            norm(0)
            for b in range(B):
                if b + 1 < B:
                    norm(b + 1)
                link = Link(dve, S["two_link"], 10, b)
                s, bu, du = T["scan"], T["bu"], T["du"]
                flip = lambda ap: view(ap, [[-1, LEN]], LEN - 1)
                for m, rows, back in ((0, slice(0, P), False), (1, slice(0, P), True),
                                      (2, slice(0, D2), False), (2, slice(D2, P), True)):
                    dve.wait_ge(S["conv_read"], 6 * b + 2 * m + 1)
                    src, dst = bu[rows, m, 0:LEN], s[rows, m, 0:LEN]
                    if back:
                        src, dst = flip(src), flip(dst)
                    ins = dve.tensor_tensor_scan(dst, view(T["mcol"][rows, 3 * LOGIT + m:3 * LOGIT + m + 1], [[0, LEN]]),
                                                 src, 0.0, ALU.mult, ALU.add)
                    link(ins)
                dve.wait_ge(S["conv_read"], 6 * b + 6)
                for m in range(3):
                    ins = dve.scalar_tensor_tensor(out=s[:, m, 0:LEN], in0=s[:, m, 0:LEN], scalar=cols(C_, m),
                                                   in1=du[:, m, 0:LEN], op0=ALU.mult, op1=ALU.add)
                link(ins)
                link(dve.tensor_tensor(s[:, 0, 0:LEN], s[:, 0, 0:LEN], s[:, 1, 0:LEN], ALU.add))
                dve.wait_ge(S["proj_read"], 4 * b + 4)
                if b >= 1:
                    dve.wait_ge(S["two_done"], b)
                dve.tensor_tensor(T["yA"][:, 0:LEN], s[:, 0, 0:LEN], zA[:, 0:LEN], ALU.mult)
                link(dve.tensor_tensor(T["yB"][:, 0:LEN], s[:, 2, 0:LEN], zB[:, 0:LEN], ALU.mult))
                dve.nop().then_inc(S["y2_ready"], 1)
                hb = T["h"][0:TOK, TPB * b:TPB * (b + 1), :]
                link(dve.tensor_tensor(hb, hb, a[0:TOK, b % 2, :, :], ALU.add))
                link(dve.tensor_tensor(hb, hb, view(T["rows"][0:TOK, 2, :], [[0, TPB], [1, D]]), ALU.add))
                dve.wait_ge(S["two_done"], b + 1)
                for t in range(TPB):
                    n = min(TOK, LEN - t * TOK)
                    ins = dve.tensor_tensor(htile(T, b, t)[0:n], htile(T, b, t)[0:n],
                                            pO[t // 2][0:n, (t % 2) * D:(t % 2 + 1) * D], ALU.add)
                link(ins)
                dve.nop().then_inc(S["two_out"], 1)


def soft_prepare(nc, T, S, io):
    with nc.Block() as block:
        @block.sync
        def _(sp):
            sp.dma_start(T["phA"][:, :], io["phiA"]).then_inc(S["phi_loaded"], 16)
            sp.dma_start(T["phB"][:, :], io["phiB"]).then_inc(S["phi_loaded"], 16)

        @block.vector
        def _(dve):
            link = Link(dve, S["phi_link"])
            dve.wait_ge(S["phi_loaded"], 32)
            for n, (name, rows) in enumerate((("phA", P), ("phB", D2))):
                phi, sq, s = T[name], T["phq"], T["phs"]
                link(dve.tensor_tensor(sq[0:rows, :], phi[:, :], phi[:, :], ALU.mult))
                link(dve.reduce_sum(s[0:rows, 0:SLOT], sq[0:rows, :].rearrange("d (n p) -> d p n", p=SLOT), axis=AX.X))
                dve.tensor_scalar(s[0:rows, 0:SLOT], s[0:rows, 0:SLOT], 1e-6, None, ALU.add).then_inc(S["phi_sum"], 1)
                dve.wait_ge(S["phi_root"], n + 1)
                link(dve.tensor_tensor(phi[:, :].rearrange("d (n p) -> d n p", p=SLOT),
                                       phi[:, :].rearrange("d (n p) -> d n p", p=SLOT),
                                       view(s[0:rows, SLOT:2 * SLOT], [[0, SOFT_E], [1, SLOT]]), ALU.mult))

        @block.gpsimd
        def _(pool):
            pool.memset(T["phs"][:, 2 * SLOT:3 * SLOT], -0.5).then_inc(S["phi_half"], 1)
            pool.wait_ge(S["phi_half"], 1)
            for n, rows in enumerate((P, D2)):
                pool.wait_ge(S["phi_sum"], n + 1)
                s = T["phs"]
                pool.tensor_tensor(s[0:rows, SLOT:2 * SLOT], s[0:rows, 0:SLOT], s[0:rows, 2 * SLOT:3 * SLOT], ALU.pow)\
                    .then_inc(S["phi_root"], 1)


def dispatch(nc, T, S, io):
    ps = T["ps"]
    pL = [(ps[2], ps[3]), (ps[0], ps[1])]
    pQ = pL[1]
    LOGITS_AT, TILE_AT = {3: (0, 1), 4: (2,), 5: (3,), 6: (4, 5)}, {4: 0, 6: 1, 7: 2}
    PAIRS_B, STEPS = SC // 2, SC * B
    FIRST = SC + 5

    def pair_at(k):
        after = k - FIRST
        if after >= 0 and after % SC < PAIRS_B and after // SC < B:
            return PAIRS_B * (after // SC) + after % SC

    def pairs_before(k):
        after = max(k - FIRST, 0)
        return PAIRS_B * (after // SC) + min(after % SC, PAIRS_B)
    pX = ps[0:4]
    pT, pE, pC = [ps[4], ps[5]], ps[6], ps[7]
    q, qA, qB, L, EC, EDT, ED, ECT = (T[n] for n in ("q", "qA", "qB", "L", "EC", "EDT", "ED", "ECT"))
    HALVES = SLOTS // 512
    rows = lambda t: min(TOK, LEN - t * TOK)
    with nc.Block() as block:
        @block.tensor
        def _(pe):
            def turn(b):
                pe.wait_ge(S["q_ready"], b + 1)
                if b >= 2:
                    pe.wait_ge(S["xs_read"], SC // 2 * (b - 1) - 2)
                elif b == 1:
                    pe.wait_ge(S["lg_read"], TPB)
                for t in range(TPB):
                    s = slice(t * TOK, (t + 1) * TOK)
                    pe.transpose(pQ[0][:, s], q[0:TOK, b % 3, t, 0:D1], T["ident"][0:TOK, 0:TOK])
                    mm = pe.transpose(pQ[1][0:D2, s], q[0:TOK, b % 3, t, D1:D], T["ident"][0:TOK, 0:TOK])
                mm.then_inc(S["q_turned"], 1)

            def logits(b, i):
                t, half = i // HALVES, i % HALVES
                k = TPB * b + t
                if i == 0:
                    pe.wait_ge(S["qT_ready"], 2 * (b + 1))
                if i == 0 and b >= 2:
                    pe.wait_ge(S["xs_read"], SC // 2 * (b - 1))
                if half == 0 and t >= 2:
                    pe.wait_ge(S["lg_read"], k - 1)
                s, w = slice(t * TOK, (t + 1) * TOK), slice(512 * half, 512 * (half + 1))
                o = pL[t % 2][half][0:TOK, :]
                pe.matmul(o, qA[:, b % 2, s], T["phA"][:, w], start=True, stop=False)
                mm = pe.matmul(o, qB[:, b % 2, s], T["phB"][:, w], start=False, stop=True)
                if half == HALVES - 1:
                    mm.then_inc(S["lg_done"], 1)

            def logits_turned(b, c):
                k = SC * b + c
                if c == 0:
                    pe.wait_ge(S["lg_read"], TPB * (b + 1))
                if k >= 2:
                    pe.wait_ge(S["edt_ready"], k - 1)
                for t in range(TPB):
                    mm = pe.transpose(pT[k % 2][:, t * TOK:t * TOK + TOK], L[0:TOK, b % 2, t, c * P:(c + 1) * P],
                                      T["ident"][0:TOK, 0:TOK])
                mm.then_inc(S["lt_done"], 1)

            def slot_weights_turned(k, at):
                pe.wait_ge(S["edt_ready"], k + 1)
                if pairs_before(at) >= 1:
                    pe.wait_ge(S["ht_read"], 2 * pairs_before(at))
                if k >= 1:
                    pe.wait_ge(S["ed_read"], k)
                for t in range(TPB):
                    mm = pe.transpose(pE[0:rows(t), t * P:(t + 1) * P], EDT[:, k % 3, t * TOK:t * TOK + rows(t)],
                                      T["ident"][:, :])
                mm.then_inc(S["ed_turned"], 1)

            def token_weights_turned(b, c):
                k = SC * b + c
                if k >= 1:
                    pe.wait_ge(S["ect_read"], k)
                for t in range(TPB):
                    mm = pe.transpose(pC[:, t * TOK:(t + 1) * TOK], EC[0:TOK, b % 2, t, c * P:(c + 1) * P],
                                      T["ident"][0:TOK, 0:TOK])
                mm.then_inc(S["ect_turned"], 1)

            def slot_inputs(b, p):
                if p == 0:
                    pe.wait_ge(S["ed_read"], SC * (b + 1))
                for cc in range(2):
                    c = 2 * p + cc
                    for t in range(TPB):
                        mm = pe.matmul(pX[p][:, cc * D:(cc + 1) * D], ED[0:rows(t), b % 2, t, c * P:(c + 1) * P],
                                       q[0:rows(t), b % 3, t, :], start=(t == 0), stop=(t == TPB - 1))
                mm.then_inc(S["xs_done"], 1)

            def slot_inputs_turned(k, chunks):
                p = k % PAIRS_B
                pe.wait_ge(S["hat_ready"], k + 1)
                pe.wait_ge(S["ed_read"], chunks)
                if k >= 1:
                    pe.wait_ge(S["ht_read"], 2 * k)
                for cc in range(2):
                    pe.transpose(pE[:, cc * P:(cc + 1) * P], T["xs2"][:, p, cc, 0:D1], T["ident"][:, :])
                    mm = pe.transpose(pE[0:D2, (2 + cc) * P:(3 + cc) * P], T["xs2"][:, p, cc, D1:D], T["ident"][:, :])
                mm.then_inc(S["ht_done"], 1)

            turn(0)
            for i in range(TPB * HALVES):
                logits(0, i)
            for k in range(STEPS + 2):
                b, c = k // SC, k % SC
                if k < STEPS:
                    logits_turned(b, c)
                if k >= 2:
                    slot_weights_turned(k - 2, k)
                if k < STEPS:
                    token_weights_turned(b, c)
                if b >= 1 and c in (1, 2):
                    slot_inputs(b - 1, 2 * c - 2)
                    slot_inputs(b - 1, 2 * c - 1)
                if b + 1 < B:
                    if c == 3:
                        turn(b + 1)
                    for i in LOGITS_AT.get(c, ()):
                        logits(b + 1, i)
                if pair_at(k) is not None:
                    slot_inputs_turned(pair_at(k), k - 1)
            for p in (2, 3):
                slot_inputs(B - 1, p)
            for k in range(pairs_before(STEPS + 2), PAIRS_B * B):
                slot_inputs_turned(k, STEPS)

        @block.scalar
        def _(act):
            def copy_q(b):
                act.wait_ge(S["q_turned"], b + 1)
                act.activation(qA[:, b % 2, :], pQ[0][:, 0:SEQ], ACT.Copy).then_inc(S["qT_ready"], 1)
                act.activation(qB[:, b % 2, :], pQ[1][0:D2, 0:SEQ], ACT.Copy).then_inc(S["qT_ready"], 1)

            def read_logits(b, t):
                k = TPB * b + t
                act.wait_ge(S["lg_max"], k + 1)
                if t == 0 and b >= 2:
                    act.wait_ge(S["ect_turned"], SC * (b - 1))
                for half in range(HALVES):
                    w = slice(512 * half, 512 * (half + 1))
                    act.activation(EC[0:TOK, b % 2, t, w], pL[t % 2][half][0:TOK, :], ACT.Exp,
                                   bias=T["lgm"][0:TOK, k % 2, 2:3],
                                   accum_out=T["zc2"][0:TOK, k, half:half + 1])
                for half in range(HALVES):
                    w = slice(512 * half, 512 * (half + 1))
                    ins = act.activation(L[0:TOK, b % 2, t, w], pL[t % 2][half][0:TOK, :], ACT.Copy)
                ins.then_inc(S["lg_read"], 1)

            copy_q(0)
            for t in range(TPB):
                read_logits(0, t)
            def copy_slot_inputs(k):
                b, p = k // PAIRS_B, k % PAIRS_B
                act.wait_ge(S["ht_done"], k + 1)
                for name, r, at in (("H1", P, 0), ("H2", D2, 2 * P)):
                    act.activation(view(T[name][:, :], [[P, 2 * P // SLOT], [1, SLOT]], 2 * p * (P // SLOT) * P + b * SLOT),
                                   pE[0:r, at:at + 2 * P].rearrange("d (n s) -> d n s", s=SLOT), ACT.Copy)\
                        .then_inc(S["ht_read"], 1)

            for k in range(STEPS + 2):
                b, c = k // SC, k % SC
                if k < STEPS:
                    act.wait_ge(S["lt_max"], k + 1)
                    if k >= 3:
                        act.wait_ge(S["ed_turned"], k - 2)
                    act.activation(EDT[:, k % 3, 0:LEN], pT[k % 2][:, 0:LEN], ACT.Exp, bias=T["ltm"][:, k % 2:k % 2 + 1],
                                   accum_out=T["zd"][:, k:k + 1]).then_inc(S["edt_ready"], 1)
                    act.wait_ge(S["ect_turned"], k + 1)
                    half, place = c // (SC // 2), c % (SC // 2)
                    if place == 0 and b >= 1:
                        act.wait_ge(S[f"ect_stored{half}"], 16 * b)
                    act.activation(ECT[:, half, place, :], pC[:, 0:SEQ], ACT.Copy).then_inc(S["ect_read"], 1)
                if b + 1 < B and c == 3:
                    copy_q(b + 1)
                if b + 1 < B and c in TILE_AT:
                    read_logits(b + 1, TILE_AT[c])
                if pair_at(k) is not None:
                    copy_slot_inputs(pair_at(k))
            for k in range(pairs_before(STEPS + 2), PAIRS_B * B):
                copy_slot_inputs(k)

        @block.sync
        def _(sp):
            for b in range(B):
                for half in range(2):
                    n = SC // 2
                    sp.wait_ge(S["ect_read"], SC * b + n * (half + 1))
                    sp.dma_start(io["ect"][b][:, n * half:n * (half + 1), :], ECT[:, half, :, :])\
                        .then_inc(S[f"ect_stored{half}"], 16)
            for half in range(2):
                sp.wait_ge(S[f"ect_stored{half}"], 16 * B)

        @block.gpsimd
        def _(pool):
            norm_root(pool, T, S, 5 * B)
            for b in range(B + 1):
                if b + 1 < B:
                    norm_root(pool, T, S, 5 * B + b + 1)
                if b >= 1:
                    pool.wait_ge(S["xvar"], b)
                    pool.tensor_tensor(T["xrstd"][:, :], T["xv"][:, :], T["minus_half"][:, 0:SC], ALU.pow)\
                        .then_inc(S["xroot"], 1)

        @block.vector
        def _(dve):
            def norm(b):
                link = Link(dve, S["soft_nlink"], 2, b)
                norm_stats(dve, T, S, link, 5 * B + b, lambda t: htile(T, b, t), D)
                norm_apply(dve, T, lambda t: htile(T, b, t), lambda t: q[0:TOK, b % 3, t, :]).then_inc(S["q_ready"], 1)

            def token_max(b, t):
                k = TPB * b + t
                link = Link(dve, S["lg_link"], 1, k)
                dve.wait_ge(S["lg_done"], k + 1)
                if k >= 2:
                    dve.wait_ge(S["lg_read"], k - 1)
                m = T["lgm"][0:TOK, k % 2, :]
                for half in range(HALVES):
                    ins = dve.tensor_reduce(m[:, half:half + 1], pL[t % 2][half][0:TOK, :], AX.X, ALU.max)
                link(ins)
                dve.tensor_reduce(m[:, 2:3], m[:, 0:2], AX.X, ALU.max, negate=True).then_inc(S["lg_max"], 1)

            def slot_sums(b):
                dve.reciprocal(T["rzd"][:, 0:SC], T["zd"][:, SC * b:SC * (b + 1)]).then_inc(S["rzd_ready"], 1)
                dve.wait_ge(S["rzd_ready"], b + 1)
                if b >= 1:
                    dve.wait_ge(S["ht_done"], SC // 2 * b)

            def read_slot_inputs(b, pairs):
                for p in pairs:
                    dve.wait_ge(S["xs_done"], SC // 2 * b + p + 1)
                    dve.tensor_tensor(T["xs2"][:, p, :, :], pX[p][:, 0:2 * D].rearrange("s (c d) -> s c d", d=D),
                                      bcast(T["rzd"][:, 2 * p:2 * p + 2], D), ALU.mult).then_inc(S["xs_read"], 1)

            def slot_input_stats(b):
                link = Link(dve, S["xs_link"], 2, b)
                dve.wait_ge(S["xs_read"], SC // 2 * (b + 1))
                for c in range(SC):
                    ins = dve.bn_stats(T["xbn"][:, c, :], T["xs2"][:, c // 2, c % 2, :])
                link(ins)
                for c in range(SC):
                    ins = dve.bn_aggr(T["xmv"][:, c, :], T["xbn"][:, c, :])
                link(ins)
                dve.tensor_scalar(T["xv"][:, :], T["xmv"][:, :, 1], EPS, None, ALU.add).then_inc(S["xvar"], 1)

            def normalise_slot_inputs(b, p):
                dve.wait_ge(S["xroot"], b + 1)
                for cc in range(2):
                    c = 2 * p + cc
                    ins = dve.tensor_scalar(T["xs2"][:, p, cc, :], T["xs2"][:, p, cc, :], T["xmv"][:, c, 0:1],
                                            T["xrstd"][:, c:c + 1], ALU.subtract, ALU.mult)
                ins.then_inc(S["hat_ready"], 1)

            norm(0)
            for t in range(TPB):
                token_max(0, t)
            def ed_read(k):
                b, c = k // SC, k % SC
                dve.wait_ge(S["ed_turned"], k + 1)
                if c == 0 and b >= 2:
                    dve.wait_ge(S["xs_done"], SC // 2 * (b - 1))
                last = TPB - 1
                dve.tensor_copy(ED[0:TOK, b % 2, 0:last, c * P:(c + 1) * P],
                                pE[0:TOK, 0:last * P].rearrange("m (t s) -> m t s", s=P))
                dve.tensor_copy(ED[0:rows(last), b % 2, last, c * P:(c + 1) * P], pE[0:rows(last), last * P:TPB * P])\
                    .then_inc(S["ed_read"], 1)

            for k in range(STEPS + 2):
                b, c = k // SC, k % SC
                if b + 1 < B and c in TILE_AT:
                    token_max(b + 1, TILE_AT[c])
                if k < STEPS:
                    dve.wait_ge(S["lt_done"], k + 1)
                    if k >= 2:
                        dve.wait_ge(S["edt_ready"], k - 1)
                    dve.tensor_reduce(T["ltm"][:, k % 2:k % 2 + 1], pT[k % 2][:, 0:LEN], AX.X, ALU.max, negate=True)\
                        .then_inc(S["lt_max"], 1)
                if k >= 2:
                    ed_read(k - 2)
                if c == 1 and b + 1 < B:
                    norm(b + 1)
                if b >= 1:
                    if c == 2:
                        slot_sums(b - 1)
                        read_slot_inputs(b - 1, (0, 1))
                    if c == 3:
                        read_slot_inputs(b - 1, (2, 3))
                        slot_input_stats(b - 1)
                    if 4 <= c < 4 + PAIRS_B:
                        normalise_slot_inputs(b - 1, c - 4)
            slot_sums(B - 1)
            read_slot_inputs(B - 1, range(SC // 2))
            slot_input_stats(B - 1)
            for p in range(SC // 2):
                normalise_slot_inputs(B - 1, p)
            zc2 = T["zc2"][0:TOK, :, :]
            dve.tensor_tensor(T["rzc"][0:TOK, :], zc2[:, :, 0], zc2[:, :, 1], ALU.add).then_inc(S["rzc_sum"], 1)
            dve.wait_ge(S["rzc_sum"], 1)
            dve.reciprocal(T["rzc"][0:TOK, :], T["rzc"][0:TOK, :])


RING = 4
MIX_RING = 3


def experts(nc, T, S, io):
    ps = T["ps"]
    pH, pY = [ps[0], ps[1]], [ps[2], ps[3]]
    W = SOFT_H + SHC * D
    n_rows = B * SLOT

    def load(sp, n, r):
        sp.dma_start(T["w12"][:, r, :], bass.AP(io["w12"].tensor, n * P * W, [[W, P], [1, W]]))\
            .then_inc(S[f"expert_loaded{r}"], 16)
        sp.dma_start(T["w1x"][:, r, :], bass.AP(io["w1x"].tensor, n * (D2 + 1) * SOFT_H, [[SOFT_H, D2 + 1], [1, SOFT_H]]))\
            .then_inc(S[f"expert_loaded{r}"], 16)

    with nc.Block() as block:
        @block.sync
        def _(sp):
            for r in range(RING):
                load(sp, r, r)
            def store(sp, n, r):
                sp.wait_ge(S["expert_read"], n + 3)
                dst = bass.AP(io["ys"].tensor, n * SLOT * D, [[SLOTS * D, B], [D, SLOT], [1, D]])
                sp.dma_start(dst, T["ye"][:, r, :]).then_inc(S[f"y_stored{r}"], 16)
            for b in range(MIX_RING):
                sp.dma_start(T["ectb"][:, b, :, :], io["ect"][b]).then_inc(S[f"mix_loaded{b}"], 16)
            with sp.Fori(0, SOFT_E - 2 * RING + 1, RING) as i:
                for r in range(RING):
                    sp.wait_ge(S["expert_out"], i + r + 1)
                    load(sp, i + r + RING, r)
                    store(sp, i + r, r)
            for r in range(RING):
                store(sp, SOFT_E - RING + r, r)
            for r in range(RING):
                sp.wait_ge(S[f"y_stored{r}"], 16 * SOFT_E // RING + 16)

        @block.tensor
        def _(pe):
            def up(n, r, loaded):
                pe.wait_ge(S[f"expert_loaded{r}"], loaded)
                pe.wait_ge(S["slots_ready"], 2 * n + 2)
                for c in range(SHC):
                    o = pH[r % 2][:, c * n_rows:(c + 1) * n_rows]
                    pe.matmul(o, T["w12"][:, r, c * P:(c + 1) * P], T["a1"][:, r, :], start=True, stop=False)
                    mm = pe.matmul(o, T["w1x"][:, r, c * P:(c + 1) * P], T["a2"][:, r, :], start=False, stop=True)
                mm.then_inc(S["expert_hid"], 1)

            def down(n, r):
                pe.wait_ge(S["expert_act"], n + 1)
                pe.wait_ge(S["expert_read"], n + 1)
                for c in range(SHC):
                    mm = pe.matmul(pY[r % 2][:, 0:D], T["eg"][:, r % 2, c * n_rows:(c + 1) * n_rows],
                                   T["w12"][:, r, SOFT_H + c * D:SOFT_H + (c + 1) * D], start=(c == 0), stop=(c == SHC - 1))
                mm.then_inc(S["expert_out"], 1)

            def products(i, last=False):
                for r in range(RING):
                    if not (last and r == RING - 1):
                        ahead = (r + 1) // RING
                        up(i + r + 1, (r + 1) % RING, 32 // RING * i + 32 * (1 + ahead))
                    down(i + r, r)
            up(0, 0, 32)
            with pe.Fori(0, SOFT_E - 2 * RING + 1, RING) as i:
                products(i)
            products(SOFT_E - RING, last=True)

        @block.scalar
        def _(act):
            def gelu(n, r):
                act.wait_ge(S["expert_hid"], n + RING + 1)
                act.activation(T["eg"][:, r % 2, :], pH[r % 2][:, 0:SHC * n_rows], ACT.Gelu)\
                    .then_inc(S["expert_act"], 1)

            def copy(n, r, stored):
                act.wait_ge(S["expert_out"], n + 1)
                act.wait_ge(S[f"y_stored{r}"], stored)
                act.activation(T["ye"][:, r, :], pY[r % 2][:, 0:D], ACT.Copy).then_inc(S["expert_read"], 1)

            def activations(i, last=False):
                for r in range(RING):
                    if not (last and r == RING - 1):
                        gelu(i + r + 1, (r + 1) % RING)
                    copy(i + r, r, 16 // RING * i + 16)
            gelu(0, 0)
            with act.Fori(0, SOFT_E - 2 * RING + 1, RING) as i:
                activations(i)
            activations(SOFT_E - RING, last=True)

        @block.vector
        def _(dve):
            dve.sem_inc(S["expert_hid"], RING)
            dve.sem_inc(S["expert_read"], 2)
            for r in range(RING):
                dve.sem_inc(S[f"y_stored{r}"], 16)
            with dve.Fori(0, SOFT_E - RING + 1, RING) as i:
                for r in range(RING):
                    dve.wait_ge(S["expert_hid"], i + r + 1)
                    for name, src, g, rows in (("a1", "H1", "egA", P), ("a2", "H2", "egB", D2)):
                        dve.tensor_scalar(T[name][0:rows, r, :], T[src][:, bass.ds((i + r) * n_rows, n_rows)],
                                          T[g][:, 0, bass.ds(i + r, 1)], T[g][:, 1, bass.ds(i + r, 1)], ALU.mult, ALU.add)\
                            .then_inc(S["slots_ready"], 1)


def combine(nc, T, S, io):
    pO = T["ps"][0:2]
    with nc.Block() as block:
        @block.scalar
        def _(act):
            for b in range(B):
                if b >= MIX_RING:
                    act.wait_ge(S["mixed"], TPB * (b - MIX_RING + 1))
                    act.dma_start(T["ectb"][:, b % MIX_RING, :, :], io["ect"][b])\
                        .then_inc(S[f"mix_loaded{b % MIX_RING}"], 16)
                src = bass.AP(io["ys"].tensor, b * SLOTS * D, [[D, P], [P * D, SC], [1, D]])
                act.dma_start(T["yb"][:, b % MIX_RING, :, :], src).then_inc(S[f"mix_loaded{b % MIX_RING}"], 16)

        @block.sync
        def _(sp):
            for b in range(B):
                for t in range(TPB):
                    k = TPB * b + t
                    n = min(TOK, LEN - t * TOK)
                    sp.wait_ge(S["mix_out"], k + 1)
                    sp.dma_start(io["out"][b, t * TOK:t * TOK + n, :], T["o"][0:n, k % 4, :])\
                        .then_inc(S[f"stored{k % 4}"], 16)
            for r in range(4):
                sp.wait_ge(S[f"stored{r}"], 16 * TILES // 4)

        @block.vector
        def _(dve):
            def bias(b):
                dve.wait_ge(S[f"mix_loaded{b % MIX_RING}"], 32 * (b // MIX_RING + 1))
                dve.tensor_tensor(T["yb"][:, b % MIX_RING, :, :], T["yb"][:, b % MIX_RING, :, :], T["b2s"][:, :, :], ALU.add)\
                    .then_inc(S["yb_ready"], 1)
            bias(0)
            for b in range(B):
                if b + 1 < B:
                    bias(b + 1)
                for t in range(TPB):
                    k = TPB * b + t
                    n = min(TOK, LEN - t * TOK)
                    dve.wait_ge(S["mixed"], k + 1)
                    if k >= 4:
                        dve.wait_ge(S[f"stored{k % 4}"], 16 * (k // 4))
                    dve.scalar_tensor_tensor(out=T["o"][0:n, k % 4, :], in0=pO[k % 2][0:n, 0:D], scalar=T["rzc"][0:n, k:k + 1],
                                             in1=htile(T, b, t)[0:n], op0=ALU.mult, op1=ALU.add).then_inc(S["mix_out"], 1)

        @block.tensor
        def _(pe):
            for b in range(B):
                pe.wait_ge(S["yb_ready"], b + 1)
                for t in range(TPB):
                    k = TPB * b + t
                    n = min(TOK, LEN - t * TOK)
                    if k >= 2:
                        pe.wait_ge(S["mix_out"], k - 1)
                    for c in range(SC):
                        mm = pe.matmul(pO[k % 2][0:n, 0:D], T["ectb"][:, b % MIX_RING, c, t * TOK:t * TOK + n],
                                       T["yb"][:, b % MIX_RING, c, :], start=(c == 0), stop=(c == SC - 1))
                    mm.then_inc(S["mixed"], 1)


def program(nc, io):
    with ExitStack() as ctx:
        def sb(name, shape, dt=F32, on=ctx):
            T[name] = on.enter_context(nc.sbuf_tensor(f"t{len(made)}_" + name, shape, dt))
            made.append(name)

        T, S, made = {}, {}, []
        psum = [ctx.enter_context(nc.psum_tensor(f"bank{i}", [P, 512], F32)) for i in range(8)]
        T["ps"] = psum
        T["psY"], T["psT"], T["psL"], T["psPX"] = psum[0:4], psum[4], psum[5:7], psum[7]
        for name in ("nvar nroot tok_link tok_turned tok_normed tok_back tok_affine tok_projected tok_out "
                     "ssm_exp ssm_r ssm_angle ssm_link u_ready u_turned uT_ready ssm_in Bu_ready x_ready "
                     "ssm_out y_ready ssm_nlink ssm_slink ssm_blink rows_loaded weights_loaded small_loaded v_ready "
                     "v_turned vT_ready hid_ready hid_done picked maskT_ready out_done scores_ready mask_ready "
                     "mask_turned z_ready ez_ready ffn_nlink gate_link shift_ready xh_ready xh_turned two_out "
                     "n_ready proj_read proj_done conv_read conv2_done y2_ready two_done two_nlink two_link "
                     "sig phi_loaded phi_link phi_sum phi_root phi_half q_ready lg_read q_turned qT_ready "
                     "lg_done xs_read edt_ready lt_done ht_read ed_read ed_turned ect_read ect_turned xs_done "
                     "hat_ready ht_done lg_max lt_max ect_stored0 ect_stored1 xvar xroot soft_nlink lg_link rzd_ready "
                     "xs_link rzc_sum expert_out slots_ready expert_hid expert_act expert_read y_stored0 y_stored1 y_stored2 y_stored3 "
                     "soft_loaded mixed mix_out stored0 stored1 stored2 stored3 yb_ready mix_loaded0 mix_loaded1 mix_loaded2 expert_loaded0 "
                     "expert_loaded1 expert_loaded2 expert_loaded3").split():
            S[name] = ctx.enter_context(nc.semaphore(name))
        early_names = ("wt_loaded w0_loaded gram_ready band_loaded w0_split w60_loaded ident_zero identb_ready "
                       "pool_zero dve w0_centred wt_centred w0c_ready w0c_copied gram_done normed l0_ready "
                       "h_ready conv_done turned patch_ready zz_done patch_copied patch_turned window_turned "
                       "window_copied gram_applied l0_done summed squared carried0 carried1 carried2 carried3 "
                       "var_ready rstd_ready zsum zvar_ready zrstd_ready scaled_ready x_loaded cols_loaded "
                       "ident_ready").split()
        for name in early_names:
            S[name] = nc.alloc_semaphore(name=name)
        late_names = [f"{name}{layer}" for layer in (5, 6)
                      for name in ("in", "conv", "sq", "sum", "var", "rstd", "norm", "turn", "out")]

        sb("ident", [P, P])
        sb("minus_half", [P, 8])
        sb("bn", [P, TPB, 6])
        sb("mv", [P, TPB, 2])
        sb("nvar", [P, 4])
        sb("nrstd", [P, 4])
        sb("h", [P, TILES, D])
        with ExitStack() as weights:
            def sw(name, shape, dt=F32):
                sb(name, shape, dt, weights)
            sw("cols", [P, 19])
            sw("rows", [TOK, 3, D])
            sw("gate_row", [TOK, 3 * N_EXPERT])
            sw("proj_w", [P, D])
            sw("CT", [P, 2, D])
            sw("BTa", [P, 2, P])
            sw("BTb", [D2, 2, P])
            sw("gate_wa", [P, N_EXPERT])
            sw("gate_wb", [D2, N_EXPERT])
            sw("b1", [P, N_EXPERT * HC])
            sw("b2", [N_EXPERT, D])
            sw("Wia", [P, 4, P])
            sw("Wib", [D2, 4, P])
            sw("Wca", [P, 3, 3 * P])
            sw("Wcb", [P, 3 * P])
            sw("Wcc", [D2, 3 * P])
            sw("Woa", [P, D])
            sw("Wob", [P, D])
            sw("mcol", [P, 21])
            sw("lncol", [P, 8])
            with ExitStack() as conv:
                def sc(name, shape, dt=F32):
                    sb(name, shape, dt, conv)
                sc("wt", [P, 16, C])
                sc("l4", [P, CHUNK // 16 * (CHUNKS + 2)])
                sc("sq", [P, 2, 512])
                sc("yn", [P, 2, 512])
                sc("ss", [P, 2, 4])
                sc("var", [P, 2, 4])
                sc("rstd", [P, 2, 4])
                with ExitStack() as early:
                    def se(name, shape, dt=F32):
                        sb(name, shape, dt, early)
                    se("identb", [P, P], BF16)
                    se("wmean", [P, 16])
                    se("w0T", [TAPS0, C])
                    se("w0mean", [TAPS0, 1])
                    se("w0parts", [TAPS0, 3, C], BF16)
                    se("w0rest", [TAPS0, C])
                    se("w0c", [P, TAPS0])
                    se("gram", [TAPS0, TAPS0])
                    se("band", [WINH, HALF * TAPS0])
                    se("w60", [2 * ROWS, 2, C], BF16)
                    se("xs", [P, WIN])
                    se("xT", [WINH, 2, P])
                    se("zz", [P, POS, TAPS0])
                    se("zs", [P, POS])
                    se("zvar", [P, POS])
                    se("zrstd", [P, POS])
                    se("scaled", [P, POS, TAPS0])
                    se("rest", [P, POS, TAPS0])
                    se("p60", [P, POS, ROWS], BF16)
                    se("p60T", [2 * ROWS, PAIRS, P], BF16)
                    se("l0", [P, 2 + CHUNK])
                    se("l1", [P, 1 + CHUNK // 2])
                    se("l2", [P, 1 + CHUNK // 4])
                    se("l3", [P, 1 + CHUNK // 8])
                    setup(nc, T, S, io)
                    stream(nc, T, S, io)
                nc.all_engine_barrier()
                nc.clear_and_free_semaphores([S[name] for name in early_names])
                nc.all_engine_barrier()
                for name in late_names:
                    S[name] = nc.alloc_semaphore(name=name)
                with ExitStack() as late:
                    sb("l5", [P, 2 * B * SEQ], on=late)
                    sb("l6", [P, B * SEQ], on=late)
                    sb("stage", [P, 2, 2 * SEQ], on=late)
                    sb("tA", [P, TPB * C], on=late)
                    sb("tB", [P, SEQ], on=late)
                    layers56(nc, T, S)
                    tokens(nc, T, S)
            with ExitStack() as attn:
                def sa(name, shape, dt=F32):
                    sb(name, shape, dt, attn)
                sa("sv", [P, 24])
                sa("Cq", [P, 2, D])
                sa("Ctmp", [P, D])
                sa("cosT", [P, LEN])
                sa("sinT", [P, LEN])
                sa("rot", [P, LEN])
                sa("u", [TOK, 2, TPB, D])
                sa("uD", [TOK, TPB, D])
                sa("uA", [P, SEQ])
                sa("uB", [D2, SEQ])
                sa("seq", [P, 8, LEN])
                ssm_tables(nc, T, S)
                state_space(nc, T, S)
            with ExitStack() as ffn:
                def sf(name, shape, dt=F32):
                    sb(name, shape, dt, ffn)
                sf("w1a", [P, N_EXPERT * HID])
                sf("w1b", [D2, N_EXPERT * HID])
                sf("w2", [P, N_EXPERT * HC, D])
                sf("u", [TOK, 2, TPB, D])
                sf("vA", [P, 2, SEQ])
                sf("vB", [D2, 2, SEQ])
                sf("G", [P, 2 * HC, SEQ])
                sf("z", [P, TPB, N_EXPERT])
                sf("ez", [P, TPB, N_EXPERT])
                sf("mask", [P, 2, TPB, N_EXPERT])
                sf("top", [P, TPB])
                sf("left", [P, TPB])
                sf("maskT", [N_EXPERT, SEQ])
                with nc.Block() as block:
                    @block.sync
                    def _(sp):
                        for name in ("w1a", "w1b", "w2"):
                            sp.dma_start(T[name][:], io[name]).then_inc(S["weights_loaded"], 16)
                        sp.wait_ge(S["weights_loaded"], 3 * 16)
                routed_ffn(nc, T, S)
            with ExitStack() as two:
                def s2(name, shape, dt=F32):
                    sb(name, shape, dt, two)
                s2("u", [TOK, 2, TPB, D])
                s2("xh", [TOK, 2, TPB, D])
                s2("nA", [P, SEQ])
                s2("nB", [D2, SEQ])
                s2("xA", [P, LEN + 2])
                s2("xB", [P, LEN + 2])
                s2("zA", [P, LEN])
                s2("zB", [P, LEN])
                s2("yA", [P, LEN])
                s2("yB", [P, LEN])
                s2("bu", [P, 3, LEN])
                s2("du", [P, 3, LEN])
                s2("scan", [P, 3, LEN])
                two_way_prepare(nc, T, S)
                two_way_scan(nc, T, S)
        with ExitStack() as soft:
            sb("H1", [P, SOFT_E * P], on=soft)
            sb("H2", [D2, SOFT_E * P], on=soft)
            sb("zc2", [TOK, TILES, 2], on=soft)
            sb("rzc", [TOK, TILES], on=soft)
            with ExitStack() as disp:
                def sd(name, shape, dt=F32):
                    sb(name, shape, dt, disp)
                sd("phA", [P, SLOTS])
                sd("phB", [D2, SLOTS])
                with ExitStack() as prep:
                    sb("phq", [P, SLOTS], on=prep)
                    sb("phs", [P, 3 * SLOT], on=prep)
                    soft_prepare(nc, T, S, io)
                sd("q", [TOK, 3, TPB, D])
                sd("qA", [P, 2, SEQ])
                sd("qB", [D2, 2, SEQ])
                sd("L", [TOK, 2, TPB, SLOTS])
                sd("EC", [TOK, 2, TPB, SLOTS])
                sd("EDT", [P, 3, LEN])
                sd("ED", [TOK, 2, TPB, SLOTS])
                sd("ECT", [P, 2, SC // 2, SEQ])
                sd("lgm", [TOK, 2, 3])
                sd("ltm", [P, 2])
                sd("zd", [P, SC * B])
                sd("rzd", [P, SC])
                sd("xs2", [P, SC // 2, 2, D])
                sd("xbn", [P, SC, 6])
                sd("xmv", [P, SC, 2])
                sd("xv", [P, SC])
                sd("xrstd", [P, SC])
                dispatch(nc, T, S, io)
            def sx(name, shape, dt=F32):
                sb(name, shape, dt, soft)
            sx("w12", [P, RING, SOFT_H + SHC * D])
            sx("w1x", [D2 + 1, RING, SOFT_H])
            sx("a1", [P, RING, P])
            sx("a2", [D2 + 1, RING, P])
            sx("eg", [P, 2, SOFT_H])
            sx("ye", [P, RING, D])
            sx("egA", [P, 2, SOFT_E])
            sx("egB", [D2, 2, SOFT_E])
            sx("b2s", [P, SC, D])
            with nc.Block() as block:
                @block.sync
                def _(sp):
                    sp.dma_start(T["egA"][:, :, :], io["egA"]).then_inc(S["soft_loaded"], 16)
                    sp.dma_start(T["egB"][:, :, :], io["egB"]).then_inc(S["soft_loaded"], 16)
                    for m in range(P // SLOT):
                        src = bass.AP(io["soft_b2"].tensor, m * D, [[0, SLOT], [P // SLOT * D, SC], [1, D]])
                        sp.dma_start(T["b2s"][m * SLOT:(m + 1) * SLOT, :, :], src).then_inc(S["soft_loaded"], 16)
                    sp.wait_ge(S["soft_loaded"], 16 * (2 + P // SLOT))

                @block.gpsimd
                def _(pool):
                    pool.memset(T["a2"][:, :, :], 1.0)
            sx("yb", [P, MIX_RING, SC, D])
            sx("ectb", [P, MIX_RING, SC, SEQ])
            experts(nc, T, S, io)
            sx("o", [TOK, 4, D])
            combine(nc, T, S, io)


def two_way_prepare(nc, T, S):
    cols = lambda i: T["mcol"][:, 3 * i:3 * i + 3]
    with nc.Block() as block:
        @block.scalar
        def _(act):
            act.activation(cols(1), cols(1), ACT.Exp, scale=-1.0).then_inc(S["sig"], 1)

        @block.gpsimd
        def _(pool):
            pool.memset(T["xA"][:, :], 0.0)
            pool.memset(T["xB"][:, :], 0.0)

        @block.vector
        def _(dve):
            dve.wait_ge(S["sig"], 1)
            dve.tensor_scalar(cols(1), cols(1), 1.0, None, ALU.add).then_inc(S["sig"], 1)
            dve.wait_ge(S["sig"], 2)
            dve.reciprocal(cols(1), cols(1))
            dve.tensor_tensor(cols(5), cols(0), cols(2), ALU.mult)
            dve.tensor_tensor(cols(6), cols(0), cols(4), ALU.mult)


def kernel(**inputs):
    import numpy as np
    import concourse.bacc as bacc
    from concourse.bass_utils import run_bass_kernel_spmd as launch

    a = {k: np.asarray(v) for k, v in inputs.items()}
    x = np.concatenate([a["x"].reshape(-1), np.zeros(((CHUNKS + 3) * STEP + WIN - a["x"].size,), a["x"].dtype)])
    conv_w = np.concatenate([a[f"L0_tok_conv_w{l}"].transpose(1, 2, 0) for l in range(1, 7)], axis=1)
    at, ff, tw = (lambda n, p=p: a[p + n] for p in ("L0_attn_", "L0_ffn_", "L1_attn_"))
    cols = np.stack([a[f"L0_tok_ln_g{l}"] for l in range(7)] + [a["L0_tok_fln_g"]]
                    + [a[f"L0_tok_ln_b{l}"] for l in range(7)] + [a["L0_tok_fln_b"]]
                    + [at("log_A_real"), at("A_imag"), at("log_dt")], axis=1)
    arrays = {"x": x, "conv_w": conv_w, "conv_w0": a["L0_tok_conv_w0"][:, 0, :].T, "cols": cols}
    arrays["proj_w"] = a["L0_tok_proj_w"]
    arrays["rows"] = np.stack([a["L0_tok_proj_b"], at("D"), tw("bo")])
    arrays["gate_row"] = np.concatenate([ff("gate_b"), ff("gate_center")])
    arrays["CT"] = np.stack([at("C_re").T, at("C_im").T], axis=1)
    BT = np.stack([at("B_re").T, at("B_im").T], axis=1)
    arrays["BTa"], arrays["BTb"] = BT[:D1], BT[D1:]
    arrays["gate_wa"], arrays["gate_wb"] = ff("gate_w")[:D1], ff("gate_w")[D1:]
    arrays["b1"] = ff("b1").reshape(N_EXPERT * HC, P).T
    arrays["b2"] = ff("b2")
    w1 = ff("w1").transpose(1, 0, 2).reshape(D, N_EXPERT * HID)
    arrays["w1a"], arrays["w1b"] = w1[:D1], w1[D1:]
    arrays["w2"] = ff("w2").reshape(N_EXPERT * HC, P, D).transpose(1, 0, 2)

    def halves(v):
        return v[..., :D1], np.concatenate([v[..., D1:], v[..., D1:]], axis=-1)
    Wi, bi = tw("Wi"), tw("bi")
    W = np.stack(halves(Wi[:, :D]) + halves(Wi[:, D:]), axis=1)
    arrays["Wia"], arrays["Wib"] = W[:D1], W[D1:]
    g, g2 = halves(tw("ln_g"))
    b, b2 = halves(tw("ln_b"))
    arrays["lncol"] = np.stack((g, g2, b, b2) + halves(bi[:D]) + halves(bi[D:]), axis=1)

    def mixed(f, b):
        return np.concatenate([f[..., :D1], b[..., :D1], f[..., D1:], b[..., D1:]], axis=-1)
    Wc = mixed(tw("Wf_conv").transpose(1, 2, 0), tw("Wb_conv").transpose(1, 2, 0)[:, ::-1])
    arrays["Wca"] = Wc[:D1]
    arrays["Wcb"] = np.concatenate([Wc[D1:, 0], Wc[D1:, 1]])
    arrays["Wcc"] = Wc[D1:, 2]
    arrays["Woa"], arrays["Wob"] = tw("Wo")[:D1], np.concatenate([tw("Wo")[D1:], tw("Wo")[D1:]])
    arrays["mcol"] = np.concatenate([mixed(tw(f), tw(b)).reshape(3, P).T for f, b in
                                     (("bf_conv", "bb_conv"), ("af", "ab"), ("bf", "bb"), ("cf", "cb"), ("df", "db"))],
                                    axis=1)
    so = lambda n: a["L1_ffn_" + n]
    phi = so("phi").transpose(2, 0, 1).reshape(D, SLOTS)
    arrays["phiA"], arrays["phiB"] = phi[:D1], phi[D1:]
    arrays["w12"] = np.concatenate([so("w1")[:, :D1], so("w2").reshape(SOFT_E, SHC, P, D).transpose(0, 2, 1, 3)
                                    .reshape(SOFT_E, P, SHC * D)], axis=2)
    arrays["w1x"] = np.concatenate([so("w1")[:, D1:], so("b1")[:, None]], axis=1)
    eg = np.stack([so("ln_g").T, so("ln_b").T], axis=1)
    arrays["egA"], arrays["egB"] = eg[:D1], eg[D1:]
    arrays["soft_b2"] = so("b2")
    arrays = {k: np.ascontiguousarray(v) for k, v in arrays.items()}
    nc = bacc.Bacc("TRN2", target_bir_lowering=False, num_devices=1)
    io = {k: nc.dram_tensor("in_" + k, v.shape, mybir.dt.from_np(v.dtype), kind="ExternalInput").ap()
          for k, v in arrays.items()}
    io["out"] = nc.dram_tensor("out", [B, LEN, D], F32, kind="ExternalOutput").ap()
    io["ect"] = nc.dram_tensor("ect", [B, P, SC, SEQ], F32, kind="Internal").ap()
    io["ys"] = nc.dram_tensor("ys", [B, SLOTS, D], F32, kind="Internal").ap()
    program(nc, io)
    r = launch(nc, [{"in_" + k: v for k, v in arrays.items()}], core_ids=[0])
    return r.results[0]["out"]
```

```python
import concourse.bass as bass
from concourse import mybir
from contextlib import ExitStack

F32 = mybir.dt.float32
BF16 = mybir.dt.bfloat16
I32 = mybir.dt.int32
ALU = mybir.AluOpType
ACT = mybir.ActivationFunctionType
AX = mybir.AxisListType

P = 128
B = 8
SAMPLES = 120000
C = 128
TAPS0, STRIDE0 = 10, 5
EPS = 1e-5

CHUNK = 4096
POS = CHUNK // P
WIN = STRIDE0 * (POS - 1) + TAPS0
HALF = POS // 2
WINH = STRIDE0 * (HALF - 1) + TAPS0
STEP = CHUNK * STRIDE0
CHUNKS = -(-B * SAMPLES // STEP)
PAIRS = POS // 2
PARTS = 6
ROWS = PARTS * TAPS0
SPLIT = [(0, 0), (0, 1), (1, 0), (0, 2), (2, 0), (1, 1)]


def view(ap, dims, offset=0):
    return bass.AP(ap.tensor, ap.offset + offset, [list(ap.ap[0])] + [list(d) for d in dims])


def bcast(ap, n):
    return bass.AP(ap.tensor, ap.offset, [list(d) for d in ap.ap] + [[0, n]])


GROUPS = [(1, 0), (1, 1), (1, 2), (1, 3), (4, 0), (3, 0), (2, 0), (2, 1)]
NG = len(GROUPS)
BANKS = 4
LAG = 2
L0_MIDDLE = {5: (3,), 6: (5,), 7: (7,)}
L0_BEHIND = {4: (2,), 5: (4,), 6: (6,)}
L0_END = {3: (0, 1)}
INPUT_OF = {1: 0, 2: 1, 3: 2, 4: 3}


def setup(nc, T, S, io):
    with nc.Block() as block:
        @block.sync
        def _(sp):
            sp.dma_start(T["wt"][:, :, :], io["conv_w"]).then_inc(S["wt_loaded"], 16)
            sp.dma_start(T["w0T"][:, :], io["conv_w0"]).then_inc(S["w0_loaded"], 16)
            sp.dma_start(T["cols"][:, :], io["cols"]).then_inc(S["cols_loaded"], 16)
            sp.dma_start(T["xs"][:, :], x_chunk(io, 0)).then_inc(S["x_loaded"], 16)
            sp.dma_start(T["CT"][:, :, :], io["CT"]).then_inc(S["readout_loaded"], 16)
            sp.wait_ge(S["gram_ready"], 1)
            sp.wait_ge(S["pool_zero"], 1)
            for r in range(HALF):
                sp.dma_start(T["band"][STRIDE0 * r:STRIDE0 * r + TAPS0, TAPS0 * r:TAPS0 * (r + 1)],
                             T["gram"][:, :]).then_inc(S["band_loaded"], 16)
            for name in ("proj_w", "BTa", "BTb", "gate_wa", "gate_wb", "Wia", "Wib", "Wca", "Wcb",
                         "Wcc", "Woa", "Wob", "lncol"):
                sp.dma_start(T[name][:], io[name]).then_inc(S["small_loaded"], 16)
            sp.dma_start(T["mcol"][:, 0:15], io["mcol"]).then_inc(S["small_loaded"], 16)
            for name, n in (("rows", 3 * D), ("gate_row", 2 * N_EXPERT)):
                src = bass.AP(io[name].tensor, 0, [[0, TOK], [1, n]])
                sp.dma_start(view(T[name][:], [[1, n]]), src).then_inc(S["rows_loaded"], 16)
            sp.wait_ge(S["cols_loaded"], 16)
            sp.wait_ge(S["small_loaded"], 16 * 14)
            sp.wait_ge(S["rows_loaded"], 16 * 2)

        @block.gpsimd
        def _(pool):
            pool.memset(T["ident"][:, :], 0.0).then_inc(S["ident_zero"], 1)
            pool.wait_ge(S["ident_zero"], 1)
            pool.affine_select(out=T["ident"][:, :], in_=T["ident"][:, :], compare_op=ALU.not_equal,
                               fill=1.0, base=0, pattern=[[-1, P]], channel_multiplier=1)\
                .then_inc(S["ident_ready"], 1)
            pool.memset(T["band"][:, :], 0.0)
            pool.memset(T["w60"][:, :, :], 0.0).then_inc(S["pool_zero"], 1)
            pool.memset(T["minus_half"][:, :], -0.5)
            for name in ("l0", "l1", "l2", "l3"):
                pool.memset(T[name][:, :], 0.0)
            pool.memset(T["yn"][:, :, :], 0.0)
            pool.memset(T["h"][:, :, :], 0.0)

        @block.vector
        def _(dve):
            dve.wait_ge(S["w0_loaded"], 16)
            dve.reduce_sum(T["w0mean"][:, :], T["w0T"][:, :], axis=AX.X).then_inc(S["dve"], 1)
            dve.wait_ge(S["dve"], 1)
            dve.tensor_scalar(T["w0mean"][:, :], T["w0mean"][:, :], 1.0 / C, None, ALU.mult).then_inc(S["dve"], 1)
            dve.wait_ge(S["dve"], 2)
            dve.tensor_scalar(T["w0T"][:, :], T["w0T"][:, :], T["w0mean"][:, 0:1], None, ALU.subtract)\
                .then_inc(S["w0_centred"], 1)
            dve.wait_ge(S["w0_centred"], 1)
            dve.tensor_copy(T["w0parts"][:, 0, :], T["w0T"][:, :]).then_inc(S["dve"], 1)
            dve.wait_ge(S["dve"], 3)
            dve.tensor_tensor(T["w0rest"][:, :], T["w0T"][:, :], T["w0parts"][:, 0, :], ALU.subtract)\
                .then_inc(S["dve"], 1)
            dve.wait_ge(S["dve"], 4)
            dve.tensor_copy(T["w0parts"][:, 1, :], T["w0rest"][:, :]).then_inc(S["dve"], 1)
            dve.wait_ge(S["dve"], 5)
            dve.tensor_tensor(T["w0parts"][:, 2, :], T["w0rest"][:, :], T["w0parts"][:, 1, :], ALU.subtract)\
                .then_inc(S["w0_split"], 1)
            dve.wait_ge(S["w0c_ready"], 1)
            dve.tensor_copy(T["w0c"][:, :], T["psT"][:, 0:TAPS0]).then_inc(S["w0c_copied"], 1)
            dve.wait_ge(S["gram_done"], 1)
            dve.tensor_copy(T["gram"][:, :], T["psT"][0:TAPS0, 16:16 + TAPS0]).then_inc(S["gram_ready"], 1)
            dve.wait_ge(S["readout_loaded"], 16)
            ssm_tables(dve, T, S)
            dve.wait_ge(S["wt_loaded"], 16)
            dve.reduce_sum(T["wmean"][:, :], T["wt"][:, :, :], axis=AX.X).then_inc(S["dve"], 1)
            dve.wait_ge(S["dve"], 6)
            dve.tensor_scalar(T["wmean"][:, :], T["wmean"][:, :], 1.0 / C, None, ALU.mult).then_inc(S["dve"], 1)
            dve.wait_ge(S["dve"], 7)
            dve.tensor_tensor(T["wt"][:, :, :], T["wt"][:, :, :], bcast(T["wmean"][:, :], C), ALU.subtract)\
                .then_inc(S["wt_centred"], 1)


        @block.tensor
        def _(pe):
            pe.wait_ge(S["ident_ready"], 1)
            pe.wait_ge(S["w0_centred"], 1)
            pe.transpose(T["psT"][:, 0:TAPS0], T["w0T"][:, :], T["ident"][0:TAPS0, 0:TAPS0])\
                .then_inc(S["w0c_ready"], 1)
            pe.wait_ge(S["w0c_copied"], 1)
            pe.matmul(T["psT"][0:TAPS0, 16:16 + TAPS0], T["w0c"][:, :], T["w0c"][:, :], start=True, stop=True)\
                .then_inc(S["gram_done"], 1)
        @block.scalar
        def _(act):
            act.wait_ge(S["ident_ready"], 1)
            act.activation(T["identb"][:, :], T["ident"][:, :], ACT.Copy).then_inc(S["identb_ready"], 1)
            ssm_functions(act, T, S)
            act.wait_ge(S["w0_split"], 1)
            act.wait_ge(S["pool_zero"], 1)
            for slot in range(2):
                for n, (_, part) in enumerate(SPLIT):
                    r = slot * ROWS + n * TAPS0
                    act.dma_start(T["w60"][r:r + TAPS0, slot, :], T["w0parts"][:, part, :])\
                        .then_inc(S["w60_loaded"], 16)


def x_chunk(io, c):
    return bass.AP(io["x"].tensor, io["x"].offset + c * STEP, [[STEP // P, P], [1, WIN]])


def stream(nc, T, S, io):
    lbuf = {0: T["l0"], 1: T["l1"], 2: T["l2"], 3: T["l3"]}
    psY, psT, psL, psPX = T["psY"], T["psT"], T["psL"], T["psPX"]
    psPb = psPX[:, :].bitcast(BF16)
    xs, p60, p60T = T["xs"], T["p60"], T["p60T"]
    patches = view(xs[:, :], [[STRIDE0, POS], [1, TAPS0]])

    def count(j, g):
        return (j + 1) * NG + g + 1

    def event(j, g):
        return GROUPS[g] + (g % BANKS, g % 2, count(j, g), 256 * j)

    END = (CHUNKS + 1) * NG
    TAIL = [(4, 0, 0, 0, END + 1, 256 * CHUNKS), (3, 0, 1, 1, END + 2, 0), (4, 0, 0, 0, END + 3, 256 * (CHUNKS + 1))]

    def tiles(layer):
        return 2 if layer == 4 else 4

    NEEDS = {4: (5, 1), 5: (7, 1), 6: (1, 0), 7: (3, 0)}

    def conv(pe, j, g):
        layer = GROUPS[g][0]
        pe.wait_ge(S["normed"], count(j, g) - BANKS)
        if layer == 1:
            if g == 0:
                pe.wait_ge(S["l0_ready"], 8 * (j + 1))
        else:
            need, back = NEEDS[g]
            pe.wait_ge(S["h_ready"], count(j - back, need))
        products(pe, event(j, g), lambda: layer0s(pe, j + 1, L0_MIDDLE.get(g, ())))

    def layer0s(pe, c, tiles):
        for i in tiles:
            layer0(pe, c, i)

    def products(pe, e, in_the_middle=None):
        layer, half, bank, _, _, _ = e
        src = lbuf[INPUT_OF[layer]]
        for t in range(tiles(layer)):
            if t == 2 and in_the_middle:
                in_the_middle()
            for k in range(3):
                at = 2 * (512 * half + P * t) + k
                mm = pe.matmul(psY[bank][:, t * C:(t + 1) * C], src[:, at:at + 2 * P - 1:2],
                               T["wt"][:, 3 * (layer - 1) + k, :], start=(k == 0), stop=(k == 2))
        mm.then_inc(S["conv_done"], 1)

    def transposes(pe, e):
        layer, _, _, par, number, _ = e
        pe.wait_ge(S["normed"], number)
        pe.wait_ge(S["h_ready"], number - 1)
        for t in range(tiles(layer)):
            mm = pe.transpose(psT[:, t * P:(t + 1) * P], T["yn"][:, par, t * C:(t + 1) * C], T["ident"][:, :])
        mm.then_inc(S["turned"], 1)

    def patch_transposes(pe, c, half):
        pe.wait_ge(S["patch_ready"], c + 1)
        if half == 0:
            pe.wait_ge(S["zz_done"], c + 3)
        else:
            pe.wait_ge(S["patch_copied"], 2 * c + 1)
        for n in range(8):
            q = 8 * half + n
            mm = pe.transpose(psPb[0:2 * ROWS, n * P:(n + 1) * P],
                              p60[:, 2 * q:2 * q + 2, :].rearrange("p a r -> p (a r)"), T["identb"][:, :])
        mm.then_inc(S["patch_turned"], 1)

    def window_transposes(pe, c):
        pe.wait_ge(S["x_loaded"], 16 * (c + 1))
        if not (isinstance(c, int) and c < 2):
            pe.wait_ge(S["patch_copied"], 2 * (c - 1))
        for h in range(2):
            at = h * STRIDE0 * HALF
            mm = pe.transpose(psPX[0:WINH, h * P:(h + 1) * P], xs[:, at:at + WINH], T["ident"][:, :])
        mm.then_inc(S["window_turned"], 1)

    def gram_product(pe, c):
        pe.wait_ge(S["window_copied"], c + 1)
        for h in range(2):
            mm = pe.matmul(psPX[:, h * HALF * TAPS0:(h + 1) * HALF * TAPS0], T["xT"][0:WINH, h, :],
                           T["band"][0:WINH, :], start=True, stop=True)
        mm.then_inc(S["gram_applied"], 1)

    def layer0(pe, c, i):
        if i % 4 == 0:
            pe.wait_ge(S["patch_copied"], 2 * c + i // 4 + 1)
        if not isinstance(c, int) or 8 * c + i >= 2:
            pe.wait_ge(S["l0_ready"], 8 * c + i - 1)
        q, slot = i // 2, i % 2
        pe.matmul(psL[i % 2][:, :], T["w60"][:, slot, :],
                  p60T[:, 4 * q:4 * q + 4, :].rearrange("r a p -> r (a p)"),
                  start=True, stop=True).then_inc(S["l0_done"], 1)

    def square(act, e):
        layer, _, bank, par, number, _ = e
        n = tiles(layer) * C
        act.wait_ge(S["conv_done"], number)
        act.wait_ge(S["summed"], number - 2)
        act.activation(T["sq"][:, par, 0:n], psY[bank][:, 0:n], ACT.Square).then_inc(S["squared"], 1)

    def gelu(act, e, carry=None):
        layer, half, _, _, number, column = e
        n = tiles(layer) * P
        act.wait_ge(S["turned"], number)
        if half == 0 and layer < 4:
            buf = lbuf[layer]
            act.wait_ge(S["h_ready"], number - 1)
            act.activation(buf[:, 0:1], buf[:, buf.shape[1] - 1:buf.shape[1]], ACT.Copy)\
                .then_inc(S[f"carried{layer}"], 1)
            act.wait_ge(S[f"carried{layer}"], carry)
        if layer == 4:
            dst = T["l4"][:, bass.ds(column, n)]
        else:
            dst = lbuf[layer][:, 1 + 512 * half:1 + 512 * half + n]
        act.activation(dst, psT[:, 0:n], ACT.Gelu, bias=T["cols"][:, 8 + layer:9 + layer],
                       scale=T["cols"][:, layer:layer + 1]).then_inc(S["h_ready"], 1)

    def gelu0(act, c, i):
        if i == 0:
            if not (isinstance(c, int) and c == 0):
                act.wait_ge(S["l0_ready"], 8 * c)
            act.wait_ge(S["l0_done"], 8 * c + 1)
            act.activation(T["l0"][:, 0:2], T["l0"][:, CHUNK:CHUNK + 2], ACT.Copy).then_inc(S["carried0"], 1)
            act.wait_ge(S["carried0"], c + 1)
        act.wait_ge(S["l0_done"], 8 * c + i + 1)
        q, slot = i // 2, i % 2
        act.activation(view(T["l0"][:, :], [[2, 4], [POS, P]], 2 + 8 * q + slot),
                       psL[i % 2][:, :].rearrange("c (a p) -> c a p", a=4), ACT.Gelu,
                       bias=T["cols"][:, 8:9], scale=T["cols"][:, 0:1]).then_inc(S["l0_ready"], 1)

    def stats(dve, e):
        layer, _, _, par, number, _ = e
        n = tiles(layer)
        dve.wait_ge(S["squared"], number)
        dve.reduce_sum(T["ss"][:, par, 0:n], T["sq"][:, par, 0:n * C].rearrange("p (t c) -> p t c", c=C), axis=AX.X)\
            .then_inc(S["summed"], 1)
        dve.wait_ge(S["summed"], number)
        dve.tensor_scalar(T["var"][:, par, 0:n], T["ss"][:, par, 0:n], 1.0 / C, EPS, ALU.mult, ALU.add)\
            .then_inc(S["var_ready"], 1)

    def normalise(dve, e):
        layer, _, bank, par, number, _ = e
        n = tiles(layer)
        dve.wait_ge(S["rstd_ready"], number)
        dve.wait_ge(S["turned"], number - 2)
        dve.tensor_tensor(T["yn"][:, par, 0:n * C].rearrange("p (t c) -> p t c", c=C),
                          psY[bank][:, 0:n * C].rearrange("p (t c) -> p t c", c=C),
                          bcast(T["rstd"][:, par, 0:n], C), ALU.mult).then_inc(S["normed"], 1)

    def copy_patches(dve, c, half):
        dve.wait_ge(S["patch_turned"], 2 * c + half + 1)
        if not (isinstance(c, int) and c == 0):
            dve.wait_ge(S["l0_done"], 8 * c)
        dve.tensor_copy(p60T[:, 8 * half:8 * half + 8, :].rearrange("r a p -> r (a p)"), psPb[0:2 * ROWS, :])\
            .then_inc(S["patch_copied"], 1)

    def copy_windows(dve, c):
        dve.wait_ge(S["window_turned"], c + 1)
        dve.tensor_copy(T["xT"][0:WINH, :, :].rearrange("r a p -> r (a p)"), psPX[0:WINH, 0:2 * P])\
            .then_inc(S["window_copied"], 1)

    def patch_squares(dve, c):
        dve.wait_ge(S["gram_applied"], c + 1)
        dve.tensor_tensor(T["zz"][:, :, :], psPX[:, 0:POS * TAPS0].rearrange("p (a k) -> p a k", k=TAPS0),
                          patches, ALU.mult).then_inc(S["zz_done"], 1)

    def patch_stats(dve, c):
        dve.wait_ge(S["zz_done"], c + 2)
        dve.reduce_sum(T["zs"][:, :], T["zz"][:, :, :], axis=AX.X).then_inc(S["zsum"], 1)
        dve.wait_ge(S["zsum"], c + 1)
        dve.tensor_scalar(T["zvar"][:, :], T["zs"][:, :], 1.0 / C, EPS, ALU.mult, ALU.add)\
            .then_inc(S["zvar_ready"], 1)

    def split_patches(dve, c, part):
        def at(n):
            return p60[:, :, n * TAPS0:(n + 1) * TAPS0]
        high, middle, low = ([n for n, (a, _) in enumerate(SPLIT) if a == want] for want in range(3))
        if part == 0:
            dve.wait_ge(S["zrstd_ready"], 4 * (c + 1))
            dve.tensor_tensor(T["scaled"][:, :, :], patches, bcast(T["zrstd"][:, :], TAPS0), ALU.mult)\
                .then_inc(S["scaled_ready"], 1)
            dve.wait_ge(S["scaled_ready"], 5 * c + 1)
            if not (isinstance(c, int) and c == 0):
                dve.wait_ge(S["patch_turned"], 2 * c)
            dve.tensor_copy(at(high[0]), T["scaled"][:, :, :]).then_inc(S["scaled_ready"], 1)
            dve.wait_ge(S["scaled_ready"], 5 * c + 2)
            dve.tensor_tensor(T["rest"][:, :, :], T["scaled"][:, :, :], at(high[0]), ALU.subtract)\
                .then_inc(S["scaled_ready"], 1)
            dve.wait_ge(S["scaled_ready"], 5 * c + 3)
            dve.tensor_copy(at(middle[0]), T["rest"][:, :, :]).then_inc(S["scaled_ready"], 1)
        else:
            dve.wait_ge(S["scaled_ready"], 5 * c + 4)
            dve.tensor_tensor(at(low[0]), T["rest"][:, :, :], at(middle[0]), ALU.subtract)
            for n in high[1:]:
                dve.tensor_copy(at(n), at(high[0]))
            dve.tensor_copy(at(middle[1]), at(middle[0])).then_inc(S["scaled_ready"], 1)
            dve.wait_ge(S["scaled_ready"], 5 * c + 5)
            dve.nop().then_inc(S["patch_ready"], 1)

    def root(pool, e):
        layer, _, _, par, number, _ = e
        n = tiles(layer)
        pool.wait_ge(S["var_ready"], number)
        pool.wait_ge(S["normed"], number - 2)
        pool.tensor_tensor(T["rstd"][:, par, 0:n], T["var"][:, par, 0:n], T["minus_half"][:, 0:n], ALU.pow)\
            .then_inc(S["rstd_ready"], 1)

    def patch_root(pool, c, part):
        pool.wait_ge(S["zvar_ready"], c + 1)
        s = slice(part * POS // 4, (part + 1) * POS // 4)
        pool.tensor_tensor(T["zrstd"][:, s], T["zvar"][:, s], T["minus_half"][:, 0:POS // 4], ALU.pow)\
            .then_inc(S["zrstd_ready"], 1)

    with nc.Block() as block:
        @block.sync
        def _(sp):
            def load(c):
                sp.wait_ge(S["scaled_ready"], 5 * c - 4)
                sp.dma_start(xs[:, :], x_chunk(io, c)).then_inc(S["x_loaded"], 16)
            load(1)
            load(2)
            with sp.Fori(0, CHUNKS) as j:
                load(j + 3)
            sp.wait_ge(S["x_loaded"], 16 * (CHUNKS + 3))

        @block.tensor
        def _(pe):
            pe.wait_ge(S["w60_loaded"], 16 * 2 * PARTS)
            pe.wait_ge(S["band_loaded"], 16 * HALF)
            for c in range(2):
                window_transposes(pe, c)
                gram_product(pe, c)
            patch_transposes(pe, 0, 0)
            patch_transposes(pe, 0, 1)
            layer0s(pe, 0, range(8))
            with pe.Fori(0, CHUNKS) as j:
                for g in range(NG):
                    conv(pe, j, g)
                    layer0s(pe, j + 1, L0_BEHIND.get(g, ()))
                    transposes(pe, event(j if g >= LAG else j - 1, (g - LAG) % NG))
                    if g == 0:
                        window_transposes(pe, j + 2)
                    if g == 1:
                        gram_product(pe, j + 2)
                    if g == 2:
                        patch_transposes(pe, j + 1, 0)
                    if g == 3:
                        patch_transposes(pe, j + 1, 1)
                    layer0s(pe, j + 1, L0_END.get(g, ()))
            transposes(pe, event(CHUNKS - 1, 6))
            transposes(pe, event(CHUNKS - 1, 7))
            for n, e in enumerate(TAIL):
                pe.wait_ge(S["h_ready"], END + n)
                products(pe, e)
                transposes(pe, e)

        @block.scalar
        def _(act):
            for i in range(8):
                gelu0(act, 0, i)
            with act.Fori(0, CHUNKS) as j:
                for g in range(NG):
                    for i in L0_MIDDLE.get(g, ()):
                        gelu0(act, j + 1, i)
                    square(act, event(j, g))
                    for i in L0_BEHIND.get(g, ()):
                        gelu0(act, j + 1, i)
                    back = 0 if g >= LAG else 1
                    gelu(act, event(j - back, (g - LAG) % NG), j - back + (2 if (g - LAG) % NG == 6 else 1))
                    for i in L0_END.get(g, ()):
                        gelu0(act, j + 1, i)
            gelu(act, event(CHUNKS - 1, 6), CHUNKS + 1)
            gelu(act, event(CHUNKS - 1, 7))
            for e in TAIL:
                square(act, e)
                gelu(act, e, CHUNKS + 1)

        @block.vector
        def _(dve):
            for name, n in (("normed", NG), ("turned", NG - LAG), ("h_ready", NG - LAG), ("summed", NG),
                            ("squared", NG), ("var_ready", NG), ("rstd_ready", NG), ("conv_done", NG), ("zz_done", 1)):
                dve.sem_inc(S[name], n)
            for c in range(2):
                copy_windows(dve, c)
                patch_squares(dve, c)
                patch_stats(dve, c)
                if c == 1:
                    copy_patches(dve, 0, 0)
                    copy_patches(dve, 0, 1)
                split_patches(dve, c, 0)
                split_patches(dve, c, 1)
            with dve.Fori(0, CHUNKS) as j:
                for g in range(NG):
                    if g == 0:
                        copy_windows(dve, j + 2)
                    stats(dve, event(j, g))
                    if g == 1:
                        patch_squares(dve, j + 2)
                    if g == 2:
                        copy_patches(dve, j + 1, 0)
                    if g == 3:
                        copy_patches(dve, j + 1, 1)
                    normalise(dve, event(j, g))
                    if g == 1:
                        patch_stats(dve, j + 2)
                    if g == 6:
                        split_patches(dve, j + 2, 0)
                    if g == 7:
                        split_patches(dve, j + 2, 1)
            for e in TAIL:
                stats(dve, e)
                normalise(dve, e)

        @block.gpsimd
        def _(pool):
            for c in range(2):
                for part in range(4):
                    patch_root(pool, c, part)
            with pool.Fori(0, CHUNKS) as j:
                for g in range(NG):
                    root(pool, event(j, g))
                    if 2 <= g <= 5:
                        patch_root(pool, j + 2, g - 2)
            for e in TAIL:
                root(pool, e)


D = 192
D1, D2 = 128, D - 128
LEN = 374
TOK = 125
TPB = 3
SEQ = TOK * TPB
TILES = B * TPB
N_EXPERT, HID = 4, 768
HC = HID // P
ROUTED = (B * SEQ + N_EXPERT * (P - 1)) // P
SOFT_E, SLOT, SOFT_H = 64, 16, 384
SLOTS = SOFT_E * SLOT
SC = SLOTS // P
SHC = SOFT_H // P


class Link:

    def __init__(self, eng, sem, per_round=0, round_=0):
        self.eng, self.sem, self.base, self.n = eng, sem, round_ * per_round, 0

    def __call__(self, ins):
        self.n += 1
        ins.then_inc(self.sem, 1)
        self.eng.wait_ge(self.sem, self.base + self.n)


def layers56(nc, T, S):
    psY, psT = T["psY"], T["psT"]

    def run(layer, groups, src, src_at, dst, sem):
        gap = 2 * SEQ
        s = {k: S[f"{k}{layer}"] for k in ("in", "conv", "sq", "sum", "var", "rstd", "norm", "turn", "out")}
        with nc.Block() as block:
            @block.tensor
            def _(pe):
                def turn(g):
                    pe.wait_ge(s["norm"], g + 1)
                    if g >= 1:
                        pe.wait_ge(s["out"], g)
                    for t in range(TPB):
                        mm = pe.transpose(psT[:, t * TOK:(t + 1) * TOK], T["yn"][0:TOK, g % 2, t * C:(t + 1) * C],
                                          T["ident"][0:TOK, 0:TOK])
                    mm.then_inc(s["turn"], 1)
                for g in range(groups):
                    pe.wait_ge(s["in"], g + 1)
                    if g >= BANKS:
                        pe.wait_ge(s["norm"], g - BANKS + 1)
                    for t in range(TPB):
                        for k in range(2):
                            at = 2 * TOK * t + k
                            mm = pe.matmul(psY[g % BANKS][0:TOK, t * C:(t + 1) * C],
                                           T["stage"][:, g % 2, at:at + 2 * TOK - 1:2],
                                           T["wt"][:, 12 + 2 * (layer - 5) + k, :], start=(k == 0), stop=(k == 1))
                    mm.then_inc(s["conv"], 1)
                    if g >= LAG:
                        turn(g - LAG)
                for g in range(groups - LAG, groups):
                    turn(g)

            @block.scalar
            def _(act):
                def gelu(g):
                    act.wait_ge(s["turn"], g + 1)
                    act.activation(T[dst][:, g * SEQ:(g + 1) * SEQ], psT[:, 0:SEQ], ACT.Gelu,
                                   bias=T["cols"][:, 8 + layer:9 + layer],
                                   scale=T["cols"][:, layer:layer + 1]).then_inc(s["out"], 1)
                for g in range(groups):
                    act.wait_ge(s["conv"], g + 1)
                    if g >= 2:
                        act.wait_ge(s["sum"], g - 1)
                    act.activation(T["sq"][0:TOK, g % 2, 0:TPB * C], psY[g % BANKS][0:TOK, 0:TPB * C], ACT.Square)\
                        .then_inc(s["sq"], 1)
                    if g >= LAG:
                        gelu(g - LAG)
                for g in range(groups - LAG, groups):
                    gelu(g)

            @block.vector
            def _(dve):
                def place(g):
                    if g >= 2:
                        dve.wait_ge(s["conv"], g - 1)
                    dve.tensor_copy(T["stage"][:, g % 2, 0:gap], T[src][:, src_at + g * gap:src_at + (g + 1) * gap])\
                        .then_inc(s["in"], 1)

                def normalise(g):
                    dve.wait_ge(s["rstd"], g + 1)
                    if g >= 2:
                        dve.wait_ge(s["turn"], g - 1)
                    dve.tensor_tensor(T["yn"][0:TOK, g % 2, 0:TPB * C].rearrange("p (t c) -> p t c", c=C),
                                      psY[g % BANKS][0:TOK, 0:TPB * C].rearrange("p (t c) -> p t c", c=C),
                                      bcast(T["rstd"][0:TOK, g % 2, 0:TPB], C), ALU.mult).then_inc(s["norm"], 1)
                place(0)
                for g in range(groups):
                    if g + 1 < groups:
                        place(g + 1)
                    dve.wait_ge(s["sq"], g + 1)
                    dve.reduce_sum(T["ss"][0:TOK, g % 2, 0:TPB],
                                   T["sq"][0:TOK, g % 2, 0:TPB * C].rearrange("p (t c) -> p t c", c=C), axis=AX.X)\
                        .then_inc(s["sum"], 1)
                    dve.wait_ge(s["sum"], g + 1)
                    dve.tensor_scalar(T["var"][0:TOK, g % 2, 0:TPB], T["ss"][0:TOK, g % 2, 0:TPB], 1.0 / C, EPS,
                                      ALU.mult, ALU.add).then_inc(s["var"], 1)
                    if g >= 1:
                        normalise(g - 1)
                normalise(groups - 1)

            @block.gpsimd
            def _(pool):
                for g in range(groups):
                    pool.wait_ge(s["var"], g + 1)
                    if g >= 2:
                        pool.wait_ge(s["norm"], g - 1)
                    pool.tensor_tensor(T["rstd"][0:TOK, g % 2, 0:TPB], T["var"][0:TOK, g % 2, 0:TPB],
                                       T["minus_half"][0:TOK, 0:TPB], ALU.pow).then_inc(s["rstd"], 1)

    run(5, 2 * B, "l4", 513, "l5", "l5_ready")
    run(6, B, "l5", 0, "l6", "l6_ready")


def norm_stats(dve, T, S, link, k, get, width):
    for t in range(TPB):
        ins = dve.bn_stats(T["bn"][0:TOK, t, :], get(t))
    link(ins)
    for t in range(TPB):
        ins = dve.bn_aggr(T["mv"][0:TOK, t, :], T["bn"][0:TOK, t, :])
    link(ins)
    dve.tensor_scalar(T["nvar"][0:TOK, 0:TPB], T["mv"][0:TOK, :, 1], EPS, None, ALU.add).then_inc(S["nvar"], 1)
    dve.wait_ge(S["nroot"], k + 1)


def norm_root(pool, T, S, k):
    pool.wait_ge(S["nvar"], k + 1)
    pool.tensor_tensor(T["nrstd"][0:TOK, 0:TPB], T["nvar"][0:TOK, 0:TPB], T["minus_half"][0:TOK, 0:TPB], ALU.pow)\
        .then_inc(S["nroot"], 1)


def norm_apply(dve, T, get, out):
    for t in range(TPB):
        ins = dve.tensor_scalar(out(t), get(t), T["mv"][0:TOK, t, 0:1], T["nrstd"][0:TOK, t:t + 1],
                                ALU.subtract, ALU.mult)
    return ins


def htile(T, b, t):
    return T["h"][0:TOK, TPB * b + t, :]


def tokens(nc, T, S):
    pA, pB, pC, pD = T["ps"][4:6], T["ps"][1], T["ps"][2], T["ps"][3]
    nTok, nCh = T["tA"], T["tB"]
    with nc.Block() as block:
        @block.tensor
        def _(pe):
            def turn(b):
                if b >= 2:
                    pe.wait_ge(S["tok_normed"], b - 1)
                for t in range(TPB):
                    mm = pe.transpose(pA[b % 2][0:TOK, t * C:(t + 1) * C],
                                      T["l6"][:, b * SEQ + t * TOK:b * SEQ + (t + 1) * TOK], T["ident"][:, :])
                mm.then_inc(S["tok_turned"], 1)

            def turn_back(b):
                pe.wait_ge(S["tok_normed"], b + 1)
                if b >= 1:
                    pe.wait_ge(S["tok_affine"], b)
                for t in range(TPB):
                    mm = pe.transpose(pB[:, t * TOK:(t + 1) * TOK], nTok[0:TOK, t * C:(t + 1) * C],
                                      T["ident"][0:TOK, 0:TOK])
                mm.then_inc(S["tok_back"], 1)

            def project(b):
                pe.wait_ge(S["tok_affine"], b + 1)
                if b >= 1:
                    pe.wait_ge(S["tok_out"], b)
                for t in range(TPB):
                    mm = pe.matmul((pC[0:TOK, t * D:(t + 1) * D] if t < 2 else pD[0:TOK, 0:D]),
                                   nCh[:, t * TOK:(t + 1) * TOK], T["proj_w"][:, :], start=True, stop=True)
                mm.then_inc(S["tok_projected"], 1)
            turn(0)
            for b in range(B + 1):
                if b + 1 < B:
                    turn(b + 1)
                if b >= 1:
                    project(b - 1)
                if b < B:
                    turn_back(b)

        @block.vector
        def _(dve):
            for b in range(B + 1):
                if b < B:
                    link = Link(dve, S["tok_link"], 2, b)
                    dve.wait_ge(S["tok_turned"], b + 1)
                    get = lambda t: pA[b % 2][0:TOK, t * C:(t + 1) * C]
                    norm_stats(dve, T, S, link, b, get, C)
                    if b >= 1:
                        dve.wait_ge(S["tok_back"], b)
                    norm_apply(dve, T, get, lambda t: nTok[0:TOK, t * C:(t + 1) * C]).then_inc(S["tok_normed"], 1)
                if b >= 1:
                    dve.wait_ge(S["tok_projected"], b)
                    for t in range(TPB):
                        o = pC[0:TOK, t * D:(t + 1) * D] if t < 2 else pD[0:TOK, 0:D]
                        ins = dve.tensor_tensor(htile(T, b - 1, t), o, T["rows"][0:TOK, 0, :], ALU.add)
                    ins.then_inc(S["tok_out"], 1)

        @block.gpsimd
        def _(pool):
            for b in range(B):
                norm_root(pool, T, S, b)

        @block.scalar
        def _(act):
            for b in range(B):
                act.wait_ge(S["tok_back"], b + 1)
                if b >= 1:
                    act.wait_ge(S["tok_projected"], b)
                act.activation(nCh[:, 0:SEQ], pB[:, 0:SEQ], ACT.Identity, bias=T["cols"][:, 15:16],
                               scale=T["cols"][:, 7:8]).then_inc(S["tok_affine"], 1)


def ssm_columns(T):
    names = ("dt are r th k y cos sin nr ni dr di q0 q1 q2 qr qi cm sm c2 s2 tmp ay").split()
    col = {n: T["sv"][:, i:i + 1] for i, n in enumerate(names)}
    col.update({n: T["cols"][:, 16 + i:17 + i] for i, n in enumerate(("logA", "Aim", "logdt"))})
    return col


def ssm_functions(act, T, S):
    col = ssm_columns(T)
    act.wait_ge(S["cols_loaded"], 16)
    act.activation(col["dt"], col["logdt"], ACT.Exp)
    act.activation(col["are"], col["logA"], ACT.Exp).then_inc(S["ssm_exp"], 1)
    act.wait_ge(S["ssm_r"], 1)
    act.activation(col["r"], col["nr"], ACT.Exp, scale=-1.0).then_inc(S["ssm_exp"], 1)
    act.wait_ge(S["ssm_angle"], 1)
    act.activation(col["sin"], col["y"], ACT.Sin)
    act.activation(col["cos"], col["ay"], ACT.Sin).then_inc(S["ssm_exp"], 1)


def ssm_tables(dve, T, S):
    col = ssm_columns(T)
    Aim = col["Aim"]
    TWO_PI = 6.283185307179586
    C1 = 6.28125
    C2 = 0.0019340515136718750
    C3 = TWO_PI - C1 - C2
    MAGIC = 12582912.0
    steps = LEN
    link = Link(dve, S["ssm_link"])
    tt = lambda o, a, b_, op: link(dve.tensor_tensor(o, a, b_, op))
    ts = lambda o, a, s1, s2, op0, op1=ALU.bypass: link(dve.tensor_scalar(o, a, s1, s2, op0, op1))
    stt = lambda o, a, s, b_, op0, op1: link(dve.scalar_tensor_tensor(out=o, in0=a, scalar=s, in1=b_, op0=op0, op1=op1))
    dve.wait_ge(S["ssm_exp"], 1)
    dve.tensor_tensor(col["nr"], col["are"], col["dt"], ALU.mult).then_inc(S["ssm_r"], 1)
    tt(col["th"], Aim, col["dt"], ALU.mult)
    ts(col["k"], col["th"], 1.0 / TWO_PI, None, ALU.mult)
    ts(col["k"], col["k"], MAGIC, None, ALU.add)
    ts(col["k"], col["k"], MAGIC, None, ALU.subtract)
    stt(col["y"], col["k"], -C1, col["th"], ALU.mult, ALU.add)
    stt(col["y"], col["k"], -C2, col["y"], ALU.mult, ALU.add)
    stt(col["y"], col["k"], -C3, col["y"], ALU.mult, ALU.add)
    ts(col["y"], col["y"], 3.1415925, -3.1415925, ALU.min, ALU.max)
    ts(col["tmp"], col["y"], -1.0, None, ALU.mult)
    tt(col["ay"], col["y"], col["tmp"], ALU.max)
    dve.tensor_scalar(col["ay"], col["ay"], -1.0, TWO_PI / 4, ALU.mult, ALU.add).then_inc(S["ssm_angle"], 1)
    dve.wait_ge(S["ssm_exp"], 3)
    tt(col["nr"], col["r"], col["cos"], ALU.mult)
    ts(col["nr"], col["nr"], -1.0, None, ALU.add)
    tt(col["ni"], col["r"], col["sin"], ALU.mult)
    ts(col["dr"], col["are"], -1.0, 1e-8, ALU.mult, ALU.add)
    tt(col["q0"], col["dr"], col["dr"], ALU.mult)
    tt(col["q1"], Aim, Aim, ALU.mult)
    tt(col["q0"], col["q0"], col["q1"], ALU.add)
    link(dve.reciprocal(col["q0"], col["q0"]))
    tt(col["qr"], col["ni"], Aim, ALU.mult)
    stt(col["qr"], col["nr"], col["dr"], col["qr"], ALU.mult, ALU.add)
    tt(col["qr"], col["qr"], col["q0"], ALU.mult)
    tt(col["qi"], col["nr"], Aim, ALU.mult)
    stt(col["qi"], col["ni"], col["dr"], col["qi"], ALU.mult, ALU.subtract)
    tt(col["qi"], col["qi"], col["q0"], ALU.mult)
    Cr, Ci, Wr, Wi = T["CT"][:, 0, :], T["CT"][:, 1, :], T["Cq"][:, 0, :], T["Cq"][:, 1, :]
    ts(Wr, Ci, col["qi"], None, ALU.mult)
    stt(Wr, Cr, col["qr"], Wr, ALU.mult, ALU.subtract)
    ts(Wi, Cr, col["qi"], -1.0, ALU.mult, ALU.mult)
    ts(T["Ctmp"][:, :], Ci, col["qr"], None, ALU.mult)
    tt(Wi, Wi, T["Ctmp"][:, :], ALU.subtract)
    cos, sin = T["cosT"], T["sinT"]
    link(dve.memset(cos[:, 0:1], 1.0))
    link(dve.memset(sin[:, 0:1], 0.0))
    ts(col["cm"], col["cos"], 1.0, None, ALU.mult)
    ts(col["sm"], col["sin"], 1.0, None, ALU.mult)
    m = 1
    while m < steps:
        n = min(m, steps - m)
        ts(T["rot"][:, 0:n], sin[:, 0:n], col["sm"], None, ALU.mult)
        stt(cos[:, m:m + n], cos[:, 0:n], col["cm"], T["rot"][:, 0:n], ALU.mult, ALU.subtract)
        ts(T["rot"][:, 0:n], cos[:, 0:n], col["sm"], None, ALU.mult)
        stt(sin[:, m:m + n], sin[:, 0:n], col["cm"], T["rot"][:, 0:n], ALU.mult, ALU.add)
        tt(col["c2"], col["cm"], col["cm"], ALU.mult)
        tt(col["s2"], col["sm"], col["sm"], ALU.mult)
        ts(col["sm"], col["sm"], col["cm"], 2.0, ALU.mult, ALU.mult)
        tt(col["cm"], col["c2"], col["s2"], ALU.subtract)
        m *= 2


def state_space(nc, T, S):
    pA, pB, pR, pI = T["ps"][0], T["ps"][1], T["ps"][2], T["ps"][3]
    pO = [T["ps"][4], T["ps"][5]]
    u, uA, uB = T["u"], T["uA"], T["uB"]
    cos, sin = T["cosT"][:, 0:LEN], T["sinT"][:, 0:LEN]
    decay = view(T["sv"][:, 2:3], [[0, LEN]])
    m1, m2, vr, vi, gr, gi, xr, xi = (T["seq"][:, i, 0:LEN] for i in range(8))
    with nc.Block() as block:
        @block.tensor
        def _(pe):
            def inputs(b):
                pe.wait_ge(S["u_ready"], b + 1)
                if b >= 1:
                    pe.wait_ge(S["uT_ready"], 2 * b)
                turn_tiles(pe, T, u, b, pA, pB).then_inc(S["u_turned"], 1)
                pe.wait_ge(S["uT_ready"], 2 * (b + 1))
                if b >= 1:
                    pe.wait_ge(S["ssm_in"], b)
                for part, dst in ((0, pR), (1, pI)):
                    pe.matmul(dst[:, 0:LEN], T["BTa"][:, part, :], uA[:, 0:LEN], start=True, stop=False)
                    mm = pe.matmul(dst[:, 0:LEN], T["BTb"][:, part, :], uB[:, 0:LEN], start=False, stop=True)
                mm.then_inc(S["Bu_ready"], 1)
            inputs(0)
            for b in range(B):
                if b + 1 < B:
                    inputs(b + 1)
                pe.wait_ge(S["x_ready"], b + 1)
                if b >= 1:
                    pe.wait_ge(S["ssm_out"], b)
                for t in range(TPB):
                    n = min(TOK, LEN - t * TOK)
                    o = pO[t // 2][0:n, (t % 2) * D:(t % 2 + 1) * D]
                    pe.matmul(o, xr[:, t * TOK:t * TOK + n], T["Cq"][:, 0, :], start=True, stop=False)
                    mm = pe.matmul(o, xi[:, t * TOK:t * TOK + n], T["Cq"][:, 1, :], start=False, stop=True)
                mm.then_inc(S["y_ready"], 1)

        @block.scalar
        def _(act):
            for b in range(B):
                act.wait_ge(S["u_turned"], b + 1)
                if b >= 1:
                    act.wait_ge(S["Bu_ready"], b)
                act.activation(uA[:, 0:SEQ], pA[:, 0:SEQ], ACT.Copy).then_inc(S["uT_ready"], 1)
                act.activation(uB[:, 0:SEQ], pB[0:D2, 0:SEQ], ACT.Copy).then_inc(S["uT_ready"], 1)

        @block.gpsimd
        def _(pool):
            norm_root(pool, T, S, B)
            for b in range(B):
                if b + 1 < B:
                    norm_root(pool, T, S, B + b + 1)
                pool.wait_ge(S["u_ready"], b + 1)
                if b >= 1:
                    pool.wait_ge(S["ssm_blink"], 2 * b)
                gain = view(T["rows"][0:TOK, 1, :], [[0, TPB], [1, D]])
                pool.tensor_tensor(T["uD"][0:TOK, :, :], u[0:TOK, b % 2, :, :], gain, ALU.mult).then_inc(S["ssm_blink"], 1)
                pool.wait_ge(S["ssm_blink"], 2 * b + 1)
                hb = T["h"][0:TOK, TPB * b:TPB * (b + 1), :]
                pool.tensor_tensor(hb, hb, T["uD"][0:TOK, :, :], ALU.add).then_inc(S["ssm_blink"], 1)

        @block.vector
        def _(dve):
            def norm(b):
                link = Link(dve, S["ssm_nlink"], 2, b)
                norm_stats(dve, T, S, link, B + b, lambda t: htile(T, b, t), D)
                if b >= 2:
                    dve.wait_ge(S["ssm_blink"], 2 * (b - 1) - 1)
                norm_apply(dve, T, lambda t: htile(T, b, t), lambda t: u[0:TOK, b % 2, t, :]).then_inc(S["u_ready"], 1)

            def add_outputs(b):
                dve.wait_ge(S["y_ready"], b + 1)
                dve.wait_ge(S["ssm_blink"], 2 * (b + 1))
                for t in range(TPB):
                    n = min(TOK, LEN - t * TOK)
                    h = htile(T, b, t)[0:n]
                    ins = dve.tensor_tensor(h, h, pO[t // 2][0:n, (t % 2) * D:(t % 2 + 1) * D], ALU.add)
                ins.then_inc(S["ssm_out"], 1)
            norm(0)
            for b in range(B):
                if b + 1 < B:
                    norm(b + 1)
                dve.wait_ge(S["Bu_ready"], b + 1)
                link = Link(dve, S["ssm_slink"], 9, b)
                R, I = pR[:, 0:LEN], pI[:, 0:LEN]
                tt = lambda o, a, b_, op: dve.tensor_tensor(o, a, b_, op)
                tt(m1, R, cos, ALU.mult)
                link(tt(m2, I, sin, ALU.mult))
                link(tt(vr, m1, m2, ALU.add))
                tt(m1, I, cos, ALU.mult)
                ins = tt(m2, R, sin, ALU.mult)
                link(ins)
                dve.nop().then_inc(S["ssm_in"], 1)
                link(tt(vi, m1, m2, ALU.subtract))
                dve.tensor_tensor_scan(gr, decay, vr, 0.0, ALU.mult, ALU.add)
                link(dve.tensor_tensor_scan(gi, decay, vi, 0.0, ALU.mult, ALU.add))
                tt(m1, gr, cos, ALU.mult)
                link(tt(m2, gi, sin, ALU.mult))
                if b >= 1:
                    add_outputs(b - 1)
                link(tt(xr, m1, m2, ALU.subtract))
                tt(m1, gi, cos, ALU.mult)
                link(tt(m2, gr, sin, ALU.mult))
                link(tt(xi, m1, m2, ALU.add))
                dve.nop().then_inc(S["x_ready"], 1)
            add_outputs(B - 1)


def turn_tiles(pe, T, src, b, pA, pB):
    for t in range(TPB):
        pe.transpose(pA[:, t * TOK:(t + 1) * TOK], src[0:TOK, b % 2, t, 0:D1], T["ident"][0:TOK, 0:TOK])
        mm = pe.transpose(pB[0:D2, t * TOK:(t + 1) * TOK], src[0:TOK, b % 2, t, D1:D], T["ident"][0:TOK, 0:TOK])
    return mm


def gate(nc, T, S, io):
    ps = T["ps"]
    pA, pB, pG, pR, pN = ps[0], ps[1], ps[2], ps[3], ps[4]
    v, vA, vB = T["v"], T["vA"], T["vB"]
    ROOTS = 8
    E = N_EXPERT
    with nc.Block() as block:
        @block.sync
        def _(sp):
            for name in ("w1a", "w1b", "w2", "b2", "upper", "steps"):
                sp.dma_start(T[name][:], io[name]).then_inc(S["weights_loaded"], 16)
            sp.wait_ge(S["zero_ready"], 1)
            src = bass.AP(T["zero"][:, :].tensor, 0, [[D, P], [0, ROUTED], [1, D]])
            sp.dma_start(io["sorted"].rearrange("(n p) d -> p n d", p=P), src).then_inc(S["cleared"], 16)
            sp.dma_start(T["phA"][:, :], io["phiA"]).then_inc(S["soft_loaded"], 16)
            sp.dma_start(T["phB"][:, :], io["phiB"]).then_inc(S["soft_loaded"], 16)
            sp.dma_start(T["egA"][:, :, :], io["egA"]).then_inc(S["soft_loaded"], 16)
            sp.dma_start(T["egB"][:, :, :], io["egB"]).then_inc(S["soft_loaded"], 16)
            for m in range(P // SLOT):
                src = bass.AP(io["soft_b2"].tensor, m * D, [[0, SLOT], [P // SLOT * D, SC], [1, D]])
                sp.dma_start(T["b2s"][m * SLOT:(m + 1) * SLOT, :, :], src).then_inc(S["soft_loaded"], 16)
            sp.wait_ge(S["weights_loaded"], 6 * 16)
            sp.wait_ge(S["soft_loaded"], 16 * (4 + P // SLOT))

        @block.gpsimd
        def _(pool):
            pool.memset(T["zero"][:, :], 0.0).then_inc(S["zero_ready"], 1)
            pool.memset(T["eB"][:, :, :], 1.0)
            pool.memset(T["one"][:, :], 1.0).then_inc(S["one_ready"], 1)
            pool.memset(T["phs"][:, 4 * SLOT:5 * SLOT], -0.5)
            for n in range(TILES // ROOTS):
                s = slice(n * ROOTS, (n + 1) * ROOTS)
                pool.wait_ge(S["ffn_var"], n + 1)
                pool.tensor_tensor(T["frstd"][0:TOK, s], T["fvar"][0:TOK, s], T["minus_half"][0:TOK, 0:ROOTS], ALU.pow)\
                    .then_inc(S["ffn_root"], 1)
        @block.tensor
        def _(pe):
            def turn(b):
                pe.wait_ge(S["v_ready"], TPB * (b + 1))
                if b >= 1:
                    pe.wait_ge(S["vT_ready"], 2 * b)
                for t in range(TPB):
                    pe.transpose(pA[:, t * TOK:(t + 1) * TOK], v[0:TOK, TPB * b + t, 0:D1], T["ident"][0:TOK, 0:TOK])
                    mm = pe.transpose(pB[0:D2, t * TOK:(t + 1) * TOK], v[0:TOK, TPB * b + t, D1:D],
                                      T["ident"][0:TOK, 0:TOK])
                mm.then_inc(S["v_turned"], 1)

            def scores(b):
                pe.wait_ge(S["vT_ready"], 2 * (b + 1))
                if b >= 1:
                    pe.wait_ge(S["scores_copied"], b)
                pe.matmul(pR[0:E, 0:SEQ], T["gate_wa"][:, :], vA[:, b % 2, :], start=True, stop=False)
                pe.matmul(pR[0:E, 0:SEQ], T["gate_wb"][:, :], vB[:, b % 2, :], start=False, stop=True)\
                    .then_inc(S["scores_made"], 1)

            def scores_turned(b):
                pe.wait_ge(S["scores_copied"], b + 1)
                for t in range(TPB):
                    k = TPB * b + t
                    mm = pe.transpose(pG[0:TOK, k * E:(k + 1) * E], T["scores"][:, t * TOK:(t + 1) * TOK],
                                      T["ident"][0:E, 0:E])
                mm.then_inc(S["scores_ready"], 1)
            turn(0)
            for b in range(B):
                if b + 1 < B:
                    turn(b + 1)
                scores(b)
                if b >= 1:
                    scores_turned(b - 1)
            scores_turned(B - 1)
            pe.wait_ge(S["mask_ready"], 1)
            pe.wait_ge(S["weights_loaded"], 6 * 16)
            pe.wait_ge(S["one_ready"], 1)
            mask = view(T["mask"][0:TOK, :, :], [[1, TILES * E]])
            pe.matmul(pR[0:TOK, 0:TILES * E], T["upper"][:, :], mask, start=True, stop=True)
            pe.matmul(pN[:, 0:TILES * E], T["one"][0:TOK, :], mask, start=True, stop=True).then_inc(S["ranks_ready"], 1)

        @block.scalar
        def _(act):
            def copy_scores(b):
                act.wait_ge(S["scores_made"], b + 1)
                if b >= 1:
                    act.wait_ge(S["scores_ready"], b)
                act.activation(T["scores"][:, :], pR[0:E, 0:SEQ], ACT.Copy).then_inc(S["scores_copied"], 1)
            for b in range(B):
                act.wait_ge(S["v_turned"], b + 1)
                if b >= 2:
                    act.wait_ge(S["scores_made"], b - 1)
                act.activation(vA[:, b % 2, :], pA[:, 0:SEQ], ACT.Copy).then_inc(S["vT_ready"], 1)
                act.activation(vB[:, b % 2, :], pB[0:D2, 0:SEQ], ACT.Copy).then_inc(S["vT_ready"], 1)
                if b >= 1:
                    copy_scores(b - 1)
            copy_scores(B - 1)
            act.wait_ge(S["z_ready"], 1)
            act.activation(T["ez"][0:TOK, :, :], T["z"][0:TOK, :, :], ACT.Exp).then_inc(S["ez_ready"], 1)

        @block.vector
        def _(dve):
            link = Link(dve, S["gate_link"], 99, 0)
            h, mv = T["h"], T["fmv"]
            for n in range(TILES // ROOTS):
                s = slice(n * ROOTS, (n + 1) * ROOTS)
                for k in range(n * ROOTS, (n + 1) * ROOTS):
                    ins = dve.bn_stats(T["fbn"][0:TOK, k, :], h[0:TOK, k, :])
                link(ins)
                for k in range(n * ROOTS, (n + 1) * ROOTS):
                    ins = dve.bn_aggr(mv[0:TOK, k, :], T["fbn"][0:TOK, k, :])
                link(ins)
                dve.tensor_scalar(T["fvar"][0:TOK, s], mv[0:TOK, s, 1], EPS, None, ALU.add).then_inc(S["ffn_var"], 1)
            for k in range(TILES):
                if k % ROOTS == 0:
                    dve.wait_ge(S["ffn_root"], k // ROOTS + 1)
                dve.tensor_scalar(v[0:TOK, k, :], h[0:TOK, k, :], mv[0:TOK, k, 0:1], T["frstd"][0:TOK, k:k + 1],
                                  ALU.subtract, ALU.mult).then_inc(S["v_ready"], 1)
            g = T["gate_row"]
            link(dve.tensor_tensor(g[0:TOK, 2 * E:3 * E], g[0:TOK, 0:E], g[0:TOK, E:2 * E], ALU.subtract))
            z, ez, m = T["z"][0:TOK, :, :], T["ez"][0:TOK, :, :], T["mask"][0:TOK, :, :]
            top, left = T["top"][0:TOK, :], T["left"][0:TOK, :]
            dve.wait_ge(S["scores_ready"], B)
            shift = view(g[0:TOK, 2 * E:3 * E], [[0, TILES], [1, E]])
            link(dve.tensor_tensor(z, pG[0:TOK, 0:TILES * E].rearrange("p (t e) -> p t e", e=E), shift, ALU.add))
            link(dve.tensor_reduce(top, z, AX.X, ALU.max))
            dve.tensor_tensor(z, z, bcast(top, E), ALU.subtract).then_inc(S["z_ready"], 1)
            dve.wait_ge(S["ez_ready"], 1)
            link(dve.reduce_sum(top, ez, axis=AX.X))
            link(dve.reciprocal(top, top))
            link(dve.tensor_tensor(ez, ez, bcast(top, E), ALU.mult))
            link(dve.tensor_reduce(top, ez, AX.X, ALU.max))
            link(dve.tensor_tensor(m, ez, bcast(top, E), ALU.is_ge))
            link(dve.tensor_scalar(left, m[:, :, 0], -1.0, 1.0, ALU.mult, ALU.add))
            for e in range(1, E):
                link(dve.tensor_tensor(m[:, :, e], m[:, :, e], left, ALU.mult))
                if e + 1 < E:
                    link(dve.tensor_tensor(left, left, m[:, :, e], ALU.subtract))
            dve.nop().then_inc(S["mask_ready"], 1)
            dve.wait_ge(S["ranks_ready"], 1)
            n, upto, steps = T["number"], T["upto"], T["steps"]
            link(dve.tensor_copy(view(n[:, :, :], [[1, TILES * E]]), pN[:, 0:TILES * E]))
            for e in range(E):
                ins = dve.tensor_tensor_scan(upto[:, :, e], T["one"][:, 0:TILES], n[:, :, e], 0.0, ALU.mult, ALU.add)
            link(ins)
            full = T["full"]
            link(dve.tensor_tensor(full[:, :, 0:TILES], bcast(upto[:, TILES - 1, :], TILES),
                                   view(steps[:, 0:TILES], [[0, E], [1, TILES]]), ALU.is_gt))
            first = T["first"]
            link(dve.reduce_sum(first[:, E:2 * E], full[:, :, 0:TILES], axis=AX.X))
            link(dve.tensor_scalar(first[:, 0:E], first[:, E:2 * E], 0.0, None, ALU.mult))
            for e in range(1, E):
                link(dve.tensor_tensor(first[:, e:e + 1], first[:, e - 1:e], first[:, E + e - 1:E + e], ALU.add))
            at = view(steps[:, TILES:TILES + ROUTED], [[1, ROUTED], [0, E - 1]])
            begun = view(T["begun"][:, :, :], [[E - 1, ROUTED], [1, E - 1]])
            link(dve.tensor_tensor(begun, at, view(first[:, 1:E], [[0, ROUTED], [1, E - 1]]), ALU.is_ge))
            link(dve.reduce_sum(T["which"][:, :], begun, axis=AX.X))
            dve.tensor_copy(T["expert"][:, :], T["which"][:, :]).then_inc(S["expert_ready"], 1)
            link(dve.tensor_tensor(upto[:, :, :], upto[:, :, :], n[:, :, :], ALU.subtract))
            link(dve.tensor_scalar(first[:, E:2 * E], first[:, 0:E], float(P), None, ALU.mult))
            link(dve.tensor_tensor(upto[:, :, :], upto[:, :, :], view(first[:, E:2 * E], [[0, TILES], [1, E]]), ALU.add))
            link(dve.tensor_tensor(z, upto[0:TOK, :, :], pR[0:TOK, 0:TILES * E].rearrange("p (t e) -> p t e", e=E), ALU.add))
            link(dve.tensor_tensor(z, z, m, ALU.mult))
            link(dve.reduce_sum(top, z, axis=AX.X))
            dve.tensor_copy(T["row"][0:TOK, :], top).then_inc(S["rows_ready"], 1)


PHI = (("phA", P), ("phB", D2))
LOADS = [3, 6, 6, 6, 6]


def routed_ffn(nc, T, S, io):
    ps = T["ps"]
    pH, pGT, pX, pO = (ps[0:2], ps[2:4]), ps[4:6], ps[6], ps[7]
    r, eA, eB, G, GT = T["routed"], T["eA"], T["eB"], T["G"], T["GT"]
    HALF_H = HID // 2
    starts = [sum(LOADS[:n]) for n in range(len(LOADS) + 1)]
    rows = io["sorted"].rearrange("(n p) d -> p n d", p=P)
    outs = io["routed"].rearrange("(n p) d -> p n d", p=P)
    with nc.Block() as block:
        @block.sync
        def _(sp):
            sp.wait_ge(S["scattered"], 16 * TILES)
            for n in range(len(LOADS)):
                s = slice(starts[n], starts[n + 1])
                sp.dma_start(r[:, s, :], rows[:, s, :]).then_inc(S[f"routed_loaded{n}"], 16)
            for n in range(len(LOADS)):
                s = slice(starts[n], starts[n + 1])
                sp.wait_ge(S["routed_done"], starts[n + 1])
                sp.dma_start(outs[:, s, :], r[:, s, :]).then_inc(S["routed_stored"], 16)
            sp.wait_ge(S["routed_stored"], 16 * len(LOADS))

        @block.gpsimd
        def _(pool):
            pool.wait_ge(S["cleared"], 16)
            for k in range(TILES):
                pool.indirect_dma_start(io["sorted"], bass.IndirectOffsetOnAxis(ap=T["row"][0:TOK, k:k + 1], axis=0),
                                        T["v"][0:TOK, k, :], None).then_inc(S["scattered"], 16)
            for n, (_, rows) in enumerate(PHI):
                pool.wait_ge(S["phi_sum"], n + 1)
                s = T["phs"]
                pool.tensor_tensor(s[0:rows, (2 + n) * SLOT:(3 + n) * SLOT], s[0:rows, n * SLOT:(n + 1) * SLOT],
                                   s[0:rows, 4 * SLOT:5 * SLOT], ALU.pow).then_inc(S["phi_root"], 1)

        @block.tensor
        def _(pe):
            expert = {}

            def turn_rows(i):
                if i in starts:
                    pe.wait_ge(S[f"routed_loaded{starts.index(i)}"], 16)
                if i >= 1:
                    pe.wait_ge(S["rows_copied"], i)
                pe.transpose(pX[:, 0:P], r[:, i, 0:D1], T["ident"][:, :])
                pe.transpose(pX[0:D2, P:2 * P], r[:, i, D1:D], T["ident"][:, :]).then_inc(S["rows_turned"], 1)

            def up(i):
                expert[i] = pe.value_load(T["expert"][0:1, i:i + 1], min_val=0, max_val=N_EXPERT - 1)
                pe.wait_ge(S["rows_copied"], i + 1)
                if i >= 2:
                    pe.wait_ge(S["hidden"], 2 * (i - 1))
                for n in range(2):
                    w = bass.ds(expert[i] * HID + n * HALF_H, HALF_H)
                    o = pH[i % 2][n][:, 0:HALF_H]
                    pe.matmul(o, eA[:, i % 2, :], T["w1a"][:, w], start=True, stop=False)
                    pe.matmul(o, eB[:, i % 2, :], T["w1b"][:, w], start=False, stop=True).then_inc(S["hidden_done"], 1)

            def turn_hidden(i):
                for n in range(2):
                    pe.wait_ge(S["hidden"], 2 * i + n + 1)
                    if i >= 1:
                        pe.wait_ge(S["hidden_copied"], 2 * (i - 1) + n + 1)
                    for c in range(HC // 2):
                        at = n * HC // 2 + c
                        mm = pe.transpose(pGT[n][:, c * P:(c + 1) * P], G[:, i % 2, at * P:(at + 1) * P], T["ident"][:, :])
                    mm.then_inc(S["hidden_turned"], 1)

            def down(i):
                pe.wait_ge(S["hidden_copied"], 2 * (i + 1))
                if i >= 1:
                    pe.wait_ge(S["routed_done"], i)
                for c in range(HC):
                    pe.matmul(pO[:, 0:D], GT[:, i % 2, c * P:(c + 1) * P],
                              T["w2"][:, bass.ds(expert[i] * (HC * D) + c * D, D)], start=(c == 0), stop=False)
                pe.matmul(pO[:, 0:D], T["one"][0:1, :], T["b2"][0:1, bass.ds(expert[i] * D, D)], start=False, stop=True)\
                    .then_inc(S["routed_out"], 1)
            turn_rows(0)
            for i in range(ROUTED + 2):
                if i < ROUTED:
                    up(i)
                if 1 <= i <= ROUTED:
                    turn_hidden(i - 1)
                if i + 1 < ROUTED:
                    turn_rows(i + 1)
                if i >= 2:
                    down(i - 2)

        @block.scalar
        def _(act):
            for i in range(ROUTED):
                for n in range(2):
                    act.wait_ge(S["hidden_done"], 2 * i + n + 1)
                    if i >= 2:
                        act.wait_ge(S["hidden_turned"], 2 * (i - 2) + n + 1)
                    act.activation(G[:, i % 2, n * HALF_H:(n + 1) * HALF_H], pH[i % 2][n][:, 0:HALF_H], ACT.Gelu)\
                        .then_inc(S["hidden"], 1)

        @block.vector
        def _(dve):
            def copy_rows(i):
                dve.wait_ge(S["rows_turned"], i + 1)
                if i >= 2:
                    dve.wait_ge(S["hidden_done"], 2 * (i - 1))
                dve.tensor_copy(eA[:, i % 2, :], pX[:, 0:P])
                dve.tensor_copy(eB[0:D2, i % 2, :], pX[0:D2, P:2 * P]).then_inc(S["rows_copied"], 1)

            def copy_hidden(i):
                for n in range(2):
                    dve.wait_ge(S["hidden_turned"], 2 * i + n + 1)
                    if i >= 2:
                        dve.wait_ge(S["routed_out"], i - 1)
                    dve.tensor_copy(GT[:, i % 2, n * HALF_H:(n + 1) * HALF_H], pGT[n][:, 0:HALF_H])\
                        .then_inc(S["hidden_copied"], 1)

            def copy_out(i):
                dve.wait_ge(S["routed_out"], i + 1)
                dve.tensor_copy(r[:, i, :], pO[:, 0:D]).then_inc(S["routed_done"], 1)
            phi_link = Link(dve, S["phi_link"])
            for n, (name, rows) in enumerate(PHI):
                phi, sq, s = T[name], T["phq"], T["phs"][0:rows, n * SLOT:(n + 1) * SLOT]
                phi_link(dve.tensor_tensor(sq[0:rows, :], phi[:, :], phi[:, :], ALU.mult))
                phi_link(dve.reduce_sum(s, sq[0:rows, :].rearrange("d (n p) -> d p n", p=SLOT), axis=AX.X))
                dve.tensor_scalar(s, s, 1e-6, None, ALU.add).then_inc(S["phi_sum"], 1)
            copy_rows(0)
            for i in range(ROUTED + 2):
                if i == ROUTED // 2:
                    for n, (name, rows) in enumerate(PHI):
                        dve.wait_ge(S["phi_root"], n + 1)
                        phi = T[name][:, :].rearrange("d (n p) -> d n p", p=SLOT)
                        root = view(T["phs"][0:rows, (2 + n) * SLOT:(3 + n) * SLOT], [[0, SOFT_E], [1, SLOT]])
                        dve.tensor_tensor(phi, phi, root, ALU.mult)
                if 1 <= i <= ROUTED:
                    copy_hidden(i - 1)
                if i + 1 < ROUTED:
                    copy_rows(i + 1)
                if i >= 2:
                    copy_out(i - 2)


RETURNS = 1


def two_way_scan(nc, T, S, io):
    ps = T["ps"]
    pA, pB, pX, pC, pO = ps[0], ps[1], [ps[2], ps[3]], [ps[4], ps[5], ps[6]], [ps[7], ps[1]]
    a, xh, nA, nB, xA, xB = T["u"], T["xh"], T["nA"], T["nB"], T["xA"], T["xB"]
    cols = lambda i, m: T["mcol"][:, 3 * i + m:3 * i + m + 1]
    three = lambda i: T["mcol"][:, 3 * i:3 * i + 3]
    BIAS, LOGIT, B_, C_, D_, BB, DB = range(7)
    zA, zB = T["zA"], T["zB"]
    with nc.Block() as block:
        @block.tensor
        def _(pe):
            def inputs(b):
                pe.wait_ge(S["xh_ready"], b + 1)
                if b >= 2:
                    pe.wait_ge(S["two_out"], b - 1)
                turn_tiles(pe, T, xh, 0, pA, pB).then_inc(S["xh_turned"], 1)
                pe.wait_ge(S["n_ready"], 2 * (b + 1))
                for i in range(4):
                    k = 4 * b + i
                    if k >= 2:
                        pe.wait_ge(S["proj_read"], k - 1)
                    o = pX[k % 2][:, 0:LEN]
                    pe.matmul(o, T["Wia"][:, i, :], nA[:, 0:LEN], start=True, stop=False)
                    pe.matmul(o, T["Wib"][:, i, :], nB[:, 0:LEN], start=False, stop=True).then_inc(S["proj_done"], 1)

            def conv(b, m):
                if m == 0:
                    pe.wait_ge(S["proj_read"], 4 * b + 2)
                if b >= 1:
                    pe.wait_ge(S["conv_read"], 6 * (b - 1) + 2 * (m + 1))
                o = pC[m][:, 0:LEN]
                for k in range(3):
                    pe.matmul(o, T["Wca"][:, k, m * P:(m + 1) * P], xA[:, k:k + LEN], start=(k == 0), stop=False)
                pe.matmul(o, T["Wcb"][:, m * P:(m + 1) * P], xB[:, 0:LEN], start=False, stop=False)
                pe.matmul(o, T["Wcc"][0:D2, m * P:(m + 1) * P], xB[0:D2, 2:2 + LEN], start=False, stop=True)\
                    .then_inc(S["conv2_done"], 1)

            def outputs(b):
                pe.wait_ge(S["y2_ready"], b + 1)
                if b >= 1:
                    pe.wait_ge(S["two_out"], b)
                for t in range(TPB):
                    n = min(TOK, LEN - t * TOK)
                    o = pO[t // 2][0:n, (t % 2) * D:(t % 2 + 1) * D]
                    pe.matmul(o, T["yA"][:, t * TOK:t * TOK + n], T["Woa"][:, :], start=True, stop=False)
                    mm = pe.matmul(o, T["yB"][:, t * TOK:t * TOK + n], T["Wob"][:, :], start=False, stop=True)
                mm.then_inc(S["two_done"], 1)
            inputs(0)
            for m in range(3):
                conv(0, m)
            for b in range(1, B):
                inputs(b)
                conv(b, 0)
                conv(b, 1)
                outputs(b - 1)
                conv(b, 2)
            outputs(B - 1)

        @block.scalar
        def _(act):
            act.activation(three(LOGIT), three(LOGIT), ACT.Exp, scale=-1.0).then_inc(S["sig"], 1)
            act.wait_ge(S["sig"], 3)
            act.wait_ge(S["zero_ready"], 2)
            for b in range(B):
                act.wait_ge(S["xh_turned"], b + 1)
                if b >= 1:
                    act.wait_ge(S["proj_done"], 4 * b)
                act.activation(nA[:, 0:SEQ], pA[:, 0:SEQ], ACT.Identity, bias=T["lncol"][:, 2:3],
                               scale=T["lncol"][:, 0:1]).then_inc(S["n_ready"], 1)
                act.activation(nB[:, 0:SEQ], pB[0:D2, 0:SEQ], ACT.Identity, bias=T["lncol"][0:D2, 3:4],
                               scale=T["lncol"][0:D2, 1:2]).then_inc(S["n_ready"], 1)
                if b >= 1:
                    act.wait_ge(S["conv2_done"], 3 * b)
                if b >= 2:
                    act.wait_ge(S["y2_ready"], b - 1)
                bi = lambda i, lo=0, hi=P: T["lncol"][lo:hi, 4 + i:5 + i]
                for i in range(4):
                    k = 4 * b + i
                    act.wait_ge(S["proj_done"], k + 1)
                    src = pX[k % 2]
                    if i == 0:
                        ins = act.activation(xA[:, 1:1 + LEN], src[:, 0:LEN], ACT.Identity, bias=bi(i))
                    elif i == 1:
                        act.activation(xB[0:D2, 1:1 + LEN], src[0:D2, 0:LEN], ACT.Identity, bias=bi(i, 0, D2))
                        ins = act.activation(xB[D2:P, 0:LEN], src[D2:P, 0:LEN], ACT.Identity, bias=bi(i, D2, P))
                    else:
                        ins = act.activation((zA if i == 2 else zB)[:, b % 2, 0:LEN], src[:, 0:LEN], ACT.Silu, bias=bi(i))
                    ins.then_inc(S["proj_read"], 1)
                if b >= 1:
                    act.wait_ge(S["y2_ready"], b)
                for m in range(3):
                    act.wait_ge(S["conv2_done"], 3 * b + m + 1)
                    act.activation(T["bu"][:, m, 0:LEN], pC[m][:, 0:LEN], ACT.Identity, bias=cols(BB, m), scale=cols(B_, m))\
                        .then_inc(S["conv_read"], 1)
                    act.activation(T["du"][:, m, 0:LEN], pC[m][:, 0:LEN], ACT.Identity, bias=cols(DB, m), scale=cols(D_, m))\
                        .then_inc(S["conv_read"], 1)

        @block.gpsimd
        def _(pool):
            pool.memset(T["xA"][:, :], 0.0)
            pool.memset(T["xB"][:, :], 0.0).then_inc(S["zero_ready"], 1)
            for b in range(B):
                if b % RETURNS == 0:
                    for k in range(TPB * b, TPB * (b + RETURNS)):
                        pool.indirect_dma_start(T["v"][0:TOK, k, :], None, io["routed"],
                                                bass.IndirectOffsetOnAxis(ap=T["row"][0:TOK, k:k + 1], axis=0))\
                            .then_inc(S[f"gathered{b // RETURNS}"], 16)
                norm_root(pool, T, S, 2 * B + 2 * b)
                norm_root(pool, T, S, 2 * B + 2 * b + 1)

        @block.vector
        def _(dve):
            def norm(b):
                link = Link(dve, S["two_nlink"], 6, b)
                s = slice(TPB * b, TPB * (b + 1))
                dve.wait_ge(S[f"gathered{b // RETURNS}"], 16 * TPB * RETURNS)
                link(dve.tensor_tensor(T["h"][0:TOK, s, :], T["h"][0:TOK, s, :], T["v"][0:TOK, s, :], ALU.add))
                norm_stats(dve, T, S, link, 2 * B + 2 * b, lambda t: htile(T, b, t), D)
                at = lambda t: a[0:TOK, b % 2, t, :]
                link(norm_apply(dve, T, lambda t: htile(T, b, t), at))
                norm_stats(dve, T, S, link, 2 * B + 2 * b + 1, at, D)
                if b >= 1:
                    dve.wait_ge(S["xh_turned"], b)
                norm_apply(dve, T, at, lambda t: xh[0:TOK, 0, t, :]).then_inc(S["xh_ready"], 1)
            dve.wait_ge(S["sig"], 1)
            dve.tensor_scalar(three(LOGIT), three(LOGIT), 1.0, None, ALU.add).then_inc(S["sig"], 1)
            dve.wait_ge(S["sig"], 2)
            dve.reciprocal(three(LOGIT), three(LOGIT))
            dve.tensor_tensor(three(BB), three(BIAS), three(B_), ALU.mult)
            dve.tensor_tensor(three(DB), three(BIAS), three(D_), ALU.mult).then_inc(S["sig"], 1)
            dve.wait_ge(S["sig"], 3)
            norm(0)
            norm(1)
            for b in range(B):
                link = Link(dve, S["two_link"], 10, b)
                s, bu, du = T["scan"], T["bu"], T["du"]
                flip = lambda ap: view(ap, [[-1, LEN]], LEN - 1)
                for m, rows, back in ((0, slice(0, P), False), (1, slice(0, P), True),
                                      (2, slice(0, D2), False), (2, slice(D2, P), True)):
                    dve.wait_ge(S["conv_read"], 6 * b + 2 * m + 1)
                    src, dst = bu[rows, m, 0:LEN], s[rows, m, 0:LEN]
                    if back:
                        src, dst = flip(src), flip(dst)
                    ins = dve.tensor_tensor_scan(dst, view(T["mcol"][rows, 3 * LOGIT + m:3 * LOGIT + m + 1], [[0, LEN]]),
                                                 src, 0.0, ALU.mult, ALU.add)
                    link(ins)
                dve.wait_ge(S["conv_read"], 6 * b + 6)
                for m in range(3):
                    ins = dve.scalar_tensor_tensor(out=s[:, m, 0:LEN], in0=s[:, m, 0:LEN], scalar=cols(C_, m),
                                                   in1=du[:, m, 0:LEN], op0=ALU.mult, op1=ALU.add)
                link(ins)
                link(dve.tensor_tensor(s[:, 0, 0:LEN], s[:, 0, 0:LEN], s[:, 1, 0:LEN], ALU.add))
                dve.wait_ge(S["proj_read"], 4 * b + 4)
                if b >= 1:
                    dve.wait_ge(S["two_done"], b)
                dve.tensor_tensor(T["yA"][:, 0:LEN], s[:, 0, 0:LEN], zA[:, b % 2, 0:LEN], ALU.mult)
                link(dve.tensor_tensor(T["yB"][:, 0:LEN], s[:, 2, 0:LEN], zB[:, b % 2, 0:LEN], ALU.mult))
                dve.nop().then_inc(S["y2_ready"], 1)
                hb = T["h"][0:TOK, TPB * b:TPB * (b + 1), :]
                link(dve.tensor_tensor(hb, hb, a[0:TOK, b % 2, :, :], ALU.add))
                link(dve.tensor_tensor(hb, hb, view(T["rows"][0:TOK, 2, :], [[0, TPB], [1, D]]), ALU.add))
                if b + 2 < B:
                    norm(b + 2)
                dve.wait_ge(S["two_done"], b + 1)
                for t in range(TPB):
                    n = min(TOK, LEN - t * TOK)
                    ins = dve.tensor_tensor(htile(T, b, t)[0:n], htile(T, b, t)[0:n],
                                            pO[t // 2][0:n, (t % 2) * D:(t % 2 + 1) * D], ALU.add)
                link(ins)
                dve.nop().then_inc(S["two_out"], 1)


def dispatch(nc, T, S, io):
    ps = T["ps"]
    pL = [(ps[2], ps[3]), (ps[0], ps[1])]
    pQ = pL[1]
    LOGITS_AT, TILE_AT = {3: (0, 1), 4: (2,), 5: (3,), 6: (4, 5)}, {4: 0, 6: 1, 7: 2}
    PAIRS_B, STEPS = SC // 2, SC * B
    FIRST = SC + 5

    def pair_at(k):
        after = k - FIRST
        if after >= 0 and after % SC < PAIRS_B and after // SC < B:
            return PAIRS_B * (after // SC) + after % SC

    def pairs_before(k):
        after = max(k - FIRST, 0)
        return PAIRS_B * (after // SC) + min(after % SC, PAIRS_B)
    pX = ps[0:4]
    pT, pE, pC = [ps[4], ps[5]], ps[6], ps[7]
    q, qA, qB, L, EC, EDT, ED, ECT = (T[n] for n in ("q", "qA", "qB", "L", "EC", "EDT", "ED", "ECT"))
    HALVES = SLOTS // 512
    rows = lambda t: min(TOK, LEN - t * TOK)
    with nc.Block() as block:
        @block.tensor
        def _(pe):
            def turn(b):
                pe.wait_ge(S["q_ready"], b + 1)
                if b >= 2:
                    pe.wait_ge(S["xs_read"], SC // 2 * (b - 1) - 2)
                elif b == 1:
                    pe.wait_ge(S["lg_read"], TPB)
                for t in range(TPB):
                    s = slice(t * TOK, (t + 1) * TOK)
                    pe.transpose(pQ[0][:, s], q[0:TOK, b % 3, t, 0:D1], T["ident"][0:TOK, 0:TOK])
                    mm = pe.transpose(pQ[1][0:D2, s], q[0:TOK, b % 3, t, D1:D], T["ident"][0:TOK, 0:TOK])
                mm.then_inc(S["q_turned"], 1)

            def logits(b, i):
                t, half = i // HALVES, i % HALVES
                k = TPB * b + t
                if i == 0:
                    pe.wait_ge(S["qT_ready"], 2 * (b + 1))
                if i == 0 and b >= 2:
                    pe.wait_ge(S["xs_read"], SC // 2 * (b - 1))
                if half == 0 and t >= 2:
                    pe.wait_ge(S["lg_read"], k - 1)
                s, w = slice(t * TOK, (t + 1) * TOK), slice(512 * half, 512 * (half + 1))
                o = pL[t % 2][half][0:TOK, :]
                pe.matmul(o, qA[:, b % 2, s], T["phA"][:, w], start=True, stop=False)
                mm = pe.matmul(o, qB[:, b % 2, s], T["phB"][:, w], start=False, stop=True)
                if half == HALVES - 1:
                    mm.then_inc(S["lg_done"], 1)

            def logits_turned(b, c):
                k = SC * b + c
                if c == 0:
                    pe.wait_ge(S["lg_read"], TPB * (b + 1))
                if k >= 2:
                    pe.wait_ge(S["edt_ready"], k - 1)
                for t in range(TPB):
                    mm = pe.transpose(pT[k % 2][:, t * TOK:t * TOK + TOK], L[0:TOK, b % 2, t, c * P:(c + 1) * P],
                                      T["ident"][0:TOK, 0:TOK])
                mm.then_inc(S["lt_done"], 1)

            def slot_weights_turned(k, at):
                pe.wait_ge(S["edt_ready"], k + 1)
                if pairs_before(at) >= 1:
                    pe.wait_ge(S["ht_read"], 2 * pairs_before(at))
                if k >= 1:
                    pe.wait_ge(S["ed_read"], k)
                for t in range(TPB):
                    mm = pe.transpose(pE[0:rows(t), t * P:(t + 1) * P], EDT[:, k % 3, t * TOK:t * TOK + rows(t)],
                                      T["ident"][:, :])
                mm.then_inc(S["ed_turned"], 1)

            def token_weights_turned(b, c):
                k = SC * b + c
                if k >= 1:
                    pe.wait_ge(S["ect_read"], k)
                for t in range(TPB):
                    mm = pe.transpose(pC[:, t * TOK:(t + 1) * TOK], EC[0:TOK, b % 2, t, c * P:(c + 1) * P],
                                      T["ident"][0:TOK, 0:TOK])
                mm.then_inc(S["ect_turned"], 1)

            def slot_inputs(b, p):
                if p == 0:
                    pe.wait_ge(S["ed_read"], SC * (b + 1))
                for cc in range(2):
                    c = 2 * p + cc
                    for t in range(TPB):
                        mm = pe.matmul(pX[p][:, cc * D:(cc + 1) * D], ED[0:rows(t), b % 2, t, c * P:(c + 1) * P],
                                       q[0:rows(t), b % 3, t, :], start=(t == 0), stop=(t == TPB - 1))
                mm.then_inc(S["xs_done"], 1)

            def slot_inputs_turned(k, chunks):
                p = k % PAIRS_B
                pe.wait_ge(S["hat_ready"], k + 1)
                pe.wait_ge(S["ed_read"], chunks)
                if k >= 1:
                    pe.wait_ge(S["ht_read"], 2 * k)
                for cc in range(2):
                    pe.transpose(pE[:, cc * P:(cc + 1) * P], T["xs2"][:, p, cc, 0:D1], T["ident"][:, :])
                    mm = pe.transpose(pE[0:D2, (2 + cc) * P:(3 + cc) * P], T["xs2"][:, p, cc, D1:D], T["ident"][:, :])
                mm.then_inc(S["ht_done"], 1)

            turn(0)
            for i in range(TPB * HALVES):
                logits(0, i)
            for k in range(STEPS + 2):
                b, c = k // SC, k % SC
                if b + 1 < B and c == 3:
                    turn(b + 1)
                if k < STEPS:
                    logits_turned(b, c)
                if k >= 2:
                    slot_weights_turned(k - 2, k)
                if k < STEPS:
                    token_weights_turned(b, c)
                if b >= 1 and c in (1, 2):
                    slot_inputs(b - 1, 2 * c - 2)
                    slot_inputs(b - 1, 2 * c - 1)
                if b + 1 < B:
                    for i in LOGITS_AT.get(c, ()):
                        logits(b + 1, i)
                if pair_at(k) is not None:
                    slot_inputs_turned(pair_at(k), k - 1)
            for p in (2, 3):
                slot_inputs(B - 1, p)
            for k in range(pairs_before(STEPS + 2), PAIRS_B * B):
                slot_inputs_turned(k, STEPS)

        @block.scalar
        def _(act):
            def copy_q(b):
                act.wait_ge(S["q_turned"], b + 1)
                act.activation(qA[:, b % 2, :], pQ[0][:, 0:SEQ], ACT.Copy).then_inc(S["qT_ready"], 1)
                act.activation(qB[:, b % 2, :], pQ[1][0:D2, 0:SEQ], ACT.Copy).then_inc(S["qT_ready"], 1)

            def read_logits(b, t):
                k = TPB * b + t
                act.wait_ge(S["lg_max"], k + 1)
                if t == 0 and b >= 2:
                    act.wait_ge(S["ect_turned"], SC * (b - 1))
                for half in range(HALVES):
                    w = slice(512 * half, 512 * (half + 1))
                    act.activation(EC[0:TOK, b % 2, t, w], pL[t % 2][half][0:TOK, :], ACT.Exp,
                                   bias=T["lgm"][0:TOK, k % 2, 2:3],
                                   accum_out=T["zc2"][0:TOK, k, half:half + 1])
                for half in range(HALVES):
                    w = slice(512 * half, 512 * (half + 1))
                    ins = act.activation(L[0:TOK, b % 2, t, w], pL[t % 2][half][0:TOK, :], ACT.Copy)
                ins.then_inc(S["lg_read"], 1)

            copy_q(0)
            for t in range(TPB):
                read_logits(0, t)
            def copy_slot_inputs(k):
                b, p = k // PAIRS_B, k % PAIRS_B
                act.wait_ge(S["ht_done"], k + 1)
                for name, r, at in (("H1", P, 0), ("H2", D2, 2 * P)):
                    act.activation(view(T[name][:, :], [[P, 2 * P // SLOT], [1, SLOT]], 2 * p * (P // SLOT) * P + b * SLOT),
                                   pE[0:r, at:at + 2 * P].rearrange("d (n s) -> d n s", s=SLOT), ACT.Copy)\
                        .then_inc(S["ht_read"], 1)

            for k in range(STEPS + 2):
                b, c = k // SC, k % SC
                if b + 1 < B and c == 3:
                    copy_q(b + 1)
                if k < STEPS:
                    act.wait_ge(S["lt_max"], k + 1)
                    if k >= 3:
                        act.wait_ge(S["ed_turned"], k - 2)
                    act.activation(EDT[:, k % 3, 0:LEN], pT[k % 2][:, 0:LEN], ACT.Exp, bias=T["ltm"][:, k % 2:k % 2 + 1],
                                   accum_out=T["zd"][:, k:k + 1]).then_inc(S["edt_ready"], 1)
                    act.wait_ge(S["ect_turned"], k + 1)
                    half, place = c // (SC // 2), c % (SC // 2)
                    if place == 0 and b >= 1:
                        act.wait_ge(S[f"ect_stored{half}"], 16 * b)
                    act.activation(ECT[:, half, place, :], pC[:, 0:SEQ], ACT.Copy).then_inc(S["ect_read"], 1)
                if b + 1 < B and c in TILE_AT:
                    read_logits(b + 1, TILE_AT[c])
                if pair_at(k) is not None:
                    copy_slot_inputs(pair_at(k))
            for k in range(pairs_before(STEPS + 2), PAIRS_B * B):
                copy_slot_inputs(k)

        @block.sync
        def _(sp):
            for b in range(B):
                for half in range(2):
                    n = SC // 2
                    sp.wait_ge(S["ect_read"], SC * b + n * (half + 1))
                    sp.dma_start(io["ect"][b][:, n * half:n * (half + 1), :], ECT[:, half, :, :])\
                        .then_inc(S[f"ect_stored{half}"], 16)
            for half in range(2):
                sp.wait_ge(S[f"ect_stored{half}"], 16 * B)

        @block.gpsimd
        def _(pool):
            norm_root(pool, T, S, 4 * B)
            for b in range(B + 1):
                if b + 1 < B:
                    norm_root(pool, T, S, 4 * B + b + 1)
                if b >= 1:
                    pool.wait_ge(S["xvar"], b)
                    pool.tensor_tensor(T["xrstd"][:, :], T["xv"][:, :], T["minus_half"][:, 0:SC], ALU.pow)\
                        .then_inc(S["xroot"], 1)

        @block.vector
        def _(dve):
            def norm(b):
                link = Link(dve, S["soft_nlink"], 2, b)
                norm_stats(dve, T, S, link, 4 * B + b, lambda t: htile(T, b, t), D)
                norm_apply(dve, T, lambda t: htile(T, b, t), lambda t: q[0:TOK, b % 3, t, :]).then_inc(S["q_ready"], 1)

            def token_max(b, t):
                k = TPB * b + t
                link = Link(dve, S["lg_link"], 1, k)
                dve.wait_ge(S["lg_done"], k + 1)
                if k >= 2:
                    dve.wait_ge(S["lg_read"], k - 1)
                m = T["lgm"][0:TOK, k % 2, :]
                for half in range(HALVES):
                    ins = dve.tensor_reduce(m[:, half:half + 1], pL[t % 2][half][0:TOK, :], AX.X, ALU.max)
                link(ins)
                dve.tensor_reduce(m[:, 2:3], m[:, 0:2], AX.X, ALU.max, negate=True).then_inc(S["lg_max"], 1)

            def slot_sums(b):
                dve.reciprocal(T["rzd"][:, 0:SC], T["zd"][:, SC * b:SC * (b + 1)]).then_inc(S["rzd_ready"], 1)
                dve.wait_ge(S["rzd_ready"], b + 1)
                if b >= 1:
                    dve.wait_ge(S["ht_done"], SC // 2 * b)

            def read_slot_inputs(b, pairs):
                for p in pairs:
                    dve.wait_ge(S["xs_done"], SC // 2 * b + p + 1)
                    dve.tensor_tensor(T["xs2"][:, p, :, :], pX[p][:, 0:2 * D].rearrange("s (c d) -> s c d", d=D),
                                      bcast(T["rzd"][:, 2 * p:2 * p + 2], D), ALU.mult).then_inc(S["xs_read"], 1)

            def slot_input_stats(b):
                link = Link(dve, S["xs_link"], 2, b)
                dve.wait_ge(S["xs_read"], SC // 2 * (b + 1))
                for c in range(SC):
                    ins = dve.bn_stats(T["xbn"][:, c, :], T["xs2"][:, c // 2, c % 2, :])
                link(ins)
                for c in range(SC):
                    ins = dve.bn_aggr(T["xmv"][:, c, :], T["xbn"][:, c, :])
                link(ins)
                dve.tensor_scalar(T["xv"][:, :], T["xmv"][:, :, 1], EPS, None, ALU.add).then_inc(S["xvar"], 1)

            def normalise_slot_inputs(b, p):
                dve.wait_ge(S["xroot"], b + 1)
                for cc in range(2):
                    c = 2 * p + cc
                    ins = dve.tensor_scalar(T["xs2"][:, p, cc, :], T["xs2"][:, p, cc, :], T["xmv"][:, c, 0:1],
                                            T["xrstd"][:, c:c + 1], ALU.subtract, ALU.mult)
                ins.then_inc(S["hat_ready"], 1)

            norm(0)
            for t in range(TPB):
                token_max(0, t)
            def ed_read(k):
                b, c = k // SC, k % SC
                dve.wait_ge(S["ed_turned"], k + 1)
                if c == 0 and b >= 2:
                    dve.wait_ge(S["xs_done"], SC // 2 * (b - 1))
                last = TPB - 1
                dve.tensor_copy(ED[0:TOK, b % 2, 0:last, c * P:(c + 1) * P],
                                pE[0:TOK, 0:last * P].rearrange("m (t s) -> m t s", s=P))
                dve.tensor_copy(ED[0:rows(last), b % 2, last, c * P:(c + 1) * P], pE[0:rows(last), last * P:TPB * P])\
                    .then_inc(S["ed_read"], 1)

            for k in range(STEPS + 2):
                b, c = k // SC, k % SC
                if b + 1 < B and c in TILE_AT:
                    token_max(b + 1, TILE_AT[c])
                if k < STEPS:
                    dve.wait_ge(S["lt_done"], k + 1)
                    if k >= 2:
                        dve.wait_ge(S["edt_ready"], k - 1)
                    dve.tensor_reduce(T["ltm"][:, k % 2:k % 2 + 1], pT[k % 2][:, 0:LEN], AX.X, ALU.max, negate=True)\
                        .then_inc(S["lt_max"], 1)
                if k >= 2:
                    ed_read(k - 2)
                if c == 1 and b + 1 < B:
                    norm(b + 1)
                if b >= 1:
                    if c == 2:
                        slot_sums(b - 1)
                        read_slot_inputs(b - 1, (0, 1))
                    if c == 3:
                        read_slot_inputs(b - 1, (2, 3))
                        slot_input_stats(b - 1)
                    if 4 <= c < 4 + PAIRS_B:
                        normalise_slot_inputs(b - 1, c - 4)
            slot_sums(B - 1)
            read_slot_inputs(B - 1, range(SC // 2))
            slot_input_stats(B - 1)
            for p in range(SC // 2):
                normalise_slot_inputs(B - 1, p)
            zc2 = T["zc2"][0:TOK, :, :]
            dve.tensor_tensor(T["rzc"][0:TOK, :], zc2[:, :, 0], zc2[:, :, 1], ALU.add).then_inc(S["rzc_sum"], 1)
            dve.wait_ge(S["rzc_sum"], 1)
            dve.reciprocal(T["rzc"][0:TOK, :], T["rzc"][0:TOK, :])


RING = 4
MIX_PIECES = 4
MIX_RING = 3


def experts(nc, T, S, io):
    ps = T["ps"]
    pH, pY = [ps[0], ps[1]], [ps[2], ps[3]]
    W = SOFT_H + SHC * D
    n_rows = B * SLOT

    def load(sp, n, r):
        sp.dma_start(T["w12"][:, r, :], bass.AP(io["w12"].tensor, n * P * W, [[W, P], [1, W]]))\
            .then_inc(S[f"expert_loaded{r}"], 16)
        sp.dma_start(T["w1x"][:, r, :], bass.AP(io["w1x"].tensor, n * (D2 + 1) * SOFT_H, [[SOFT_H, D2 + 1], [1, SOFT_H]]))\
            .then_inc(S[f"expert_loaded{r}"], 16)

    with nc.Block() as block:
        @block.sync
        def _(sp):
            for r in range(RING):
                load(sp, r, r)
            def store(sp, n, r):
                sp.wait_ge(S["expert_read"], n + 3)
                dst = bass.AP(io["ys"].tensor, n * SLOT * D, [[SLOTS * D, B], [D, SLOT], [1, D]])
                sp.dma_start(dst, T["ye"][:, r, :]).then_inc(S[f"y_stored{r}"], 16)
            with sp.Fori(0, SOFT_E - 2 * RING + 1, RING) as i:
                for r in range(RING):
                    sp.wait_ge(S["expert_out"], i + r + 1)
                    load(sp, i + r + RING, r)
                    store(sp, i + r, r)
            for r in range(RING):
                store(sp, SOFT_E - RING + r, r)
            for r in range(RING):
                sp.wait_ge(S[f"y_stored{r}"], 16 * SOFT_E // RING + 16)

        @block.gpsimd
        def _(pool):
            for n in range(MIX_RING * MIX_PIECES):
                pool.wait_ge(S["expert_out"], SOFT_E * (n + 1) // (MIX_RING * MIX_PIECES + 1))
                b, c = n // MIX_PIECES, n % MIX_PIECES * (SC // MIX_PIECES)
                s = slice(c, c + SC // MIX_PIECES)
                pool.dma_start(T["ectb"][:, b, s, :], io["ect"][b][:, s, :]).then_inc(S[f"mix_ahead{b}"], 16)

        @block.tensor
        def _(pe):
            def up(n, r, loaded):
                pe.wait_ge(S[f"expert_loaded{r}"], loaded)
                pe.wait_ge(S["slots_ready"], 2 * n + 2)
                for c in range(SHC):
                    o = pH[r % 2][:, c * n_rows:(c + 1) * n_rows]
                    pe.matmul(o, T["w12"][:, r, c * P:(c + 1) * P], T["a1"][:, r, :], start=True, stop=False)
                    mm = pe.matmul(o, T["w1x"][:, r, c * P:(c + 1) * P], T["a2"][:, r, :], start=False, stop=True)
                mm.then_inc(S["expert_hid"], 1)

            def down(n, r):
                pe.wait_ge(S["expert_act"], n + 1)
                pe.wait_ge(S["expert_read"], n + 1)
                for c in range(SHC):
                    mm = pe.matmul(pY[r % 2][:, 0:D], T["eg"][:, r % 2, c * n_rows:(c + 1) * n_rows],
                                   T["w12"][:, r, SOFT_H + c * D:SOFT_H + (c + 1) * D], start=(c == 0), stop=(c == SHC - 1))
                mm.then_inc(S["expert_out"], 1)

            def products(i, last=False):
                for r in range(RING):
                    if not (last and r == RING - 1):
                        ahead = (r + 1) // RING
                        up(i + r + 1, (r + 1) % RING, 32 // RING * i + 32 * (1 + ahead))
                    down(i + r, r)
            up(0, 0, 32)
            with pe.Fori(0, SOFT_E - 2 * RING + 1, RING) as i:
                products(i)
            products(SOFT_E - RING, last=True)

        @block.scalar
        def _(act):
            def gelu(n, r):
                act.wait_ge(S["expert_hid"], n + RING + 1)
                act.activation(T["eg"][:, r % 2, :], pH[r % 2][:, 0:SHC * n_rows], ACT.Gelu)\
                    .then_inc(S["expert_act"], 1)

            def copy(n, r, stored):
                act.wait_ge(S["expert_out"], n + 1)
                act.wait_ge(S[f"y_stored{r}"], stored)
                act.activation(T["ye"][:, r, :], pY[r % 2][:, 0:D], ACT.Copy).then_inc(S["expert_read"], 1)

            def activations(i, last=False):
                for r in range(RING):
                    if not (last and r == RING - 1):
                        gelu(i + r + 1, (r + 1) % RING)
                    copy(i + r, r, 16 // RING * i + 16)
            gelu(0, 0)
            with act.Fori(0, SOFT_E - 2 * RING + 1, RING) as i:
                activations(i)
            activations(SOFT_E - RING, last=True)

        @block.vector
        def _(dve):
            dve.sem_inc(S["expert_hid"], RING)
            dve.sem_inc(S["expert_read"], 2)
            for r in range(RING):
                dve.sem_inc(S[f"y_stored{r}"], 16)
            with dve.Fori(0, SOFT_E - RING + 1, RING) as i:
                for r in range(RING):
                    dve.wait_ge(S["expert_hid"], i + r + 1)
                    for name, src, g, rows in (("a1", "H1", "egA", P), ("a2", "H2", "egB", D2)):
                        dve.tensor_scalar(T[name][0:rows, r, :], T[src][:, bass.ds((i + r) * n_rows, n_rows)],
                                          T[g][:, 0, bass.ds(i + r, 1)], T[g][:, 1, bass.ds(i + r, 1)], ALU.mult, ALU.add)\
                            .then_inc(S["slots_ready"], 1)


def combine(nc, T, S, io):
    pO = T["ps"][0:2]
    with nc.Block() as block:
        @block.scalar
        def _(act):
            for b in range(B):
                if b >= MIX_RING:
                    act.wait_ge(S["mixed"], TPB * (b - MIX_RING + 1))
                    act.dma_start(T["ectb"][:, b % MIX_RING, :, :], io["ect"][b])\
                        .then_inc(S[f"mix_loaded{b % MIX_RING}"], 16)
                src = bass.AP(io["ys"].tensor, b * SLOTS * D, [[D, P], [P * D, SC], [1, D]])
                act.dma_start(T["yb"][:, b % MIX_RING, :, :], src).then_inc(S[f"mix_loaded{b % MIX_RING}"], 16)

        @block.sync
        def _(sp):
            for b in range(B):
                for t in range(TPB):
                    k = TPB * b + t
                    n = min(TOK, LEN - t * TOK)
                    sp.wait_ge(S["mix_out"], k + 1)
                    sp.dma_start(io["out"][b, t * TOK:t * TOK + n, :], T["o"][0:n, k % 4, :])\
                        .then_inc(S[f"stored{k % 4}"], 16)
            for r in range(4):
                sp.wait_ge(S[f"stored{r}"], 16 * TILES // 4)

        @block.vector
        def _(dve):
            def bias(b):
                if b < MIX_RING:
                    dve.wait_ge(S[f"mix_ahead{b}"], 16 * MIX_PIECES)
                dve.wait_ge(S[f"mix_loaded{b % MIX_RING}"], 16 + 32 * (b // MIX_RING))
                dve.tensor_tensor(T["yb"][:, b % MIX_RING, :, :], T["yb"][:, b % MIX_RING, :, :], T["b2s"][:, :, :], ALU.add)\
                    .then_inc(S["yb_ready"], 1)
            bias(0)
            for b in range(B):
                if b + 1 < B:
                    bias(b + 1)
                for t in range(TPB):
                    k = TPB * b + t
                    n = min(TOK, LEN - t * TOK)
                    dve.wait_ge(S["mixed"], k + 1)
                    if k >= 4:
                        dve.wait_ge(S[f"stored{k % 4}"], 16 * (k // 4))
                    dve.scalar_tensor_tensor(out=T["o"][0:n, k % 4, :], in0=pO[k % 2][0:n, 0:D], scalar=T["rzc"][0:n, k:k + 1],
                                             in1=htile(T, b, t)[0:n], op0=ALU.mult, op1=ALU.add).then_inc(S["mix_out"], 1)

        @block.tensor
        def _(pe):
            for b in range(B):
                pe.wait_ge(S["yb_ready"], b + 1)
                for t in range(TPB):
                    k = TPB * b + t
                    n = min(TOK, LEN - t * TOK)
                    if k >= 2:
                        pe.wait_ge(S["mix_out"], k - 1)
                    for c in range(SC):
                        mm = pe.matmul(pO[k % 2][0:n, 0:D], T["ectb"][:, b % MIX_RING, c, t * TOK:t * TOK + n],
                                       T["yb"][:, b % MIX_RING, c, :], start=(c == 0), stop=(c == SC - 1))
                    mm.then_inc(S["mixed"], 1)


def program(nc, io):
    with ExitStack() as ctx:
        def sb(name, shape, dt=F32, on=ctx):
            T[name] = on.enter_context(nc.sbuf_tensor(f"t{len(made)}_" + name, shape, dt))
            made.append(name)

        T, S, made = {}, {}, []
        psum = [ctx.enter_context(nc.psum_tensor(f"bank{i}", [P, 512], F32)) for i in range(8)]
        T["ps"] = psum
        T["psY"], T["psT"], T["psL"], T["psPX"] = psum[0:4], psum[4], psum[5:7], psum[7]
        for name in ("nvar nroot tok_link tok_turned tok_normed tok_back tok_affine tok_projected tok_out "
                     "ssm_exp ssm_r ssm_angle ssm_link u_ready u_turned uT_ready ssm_in Bu_ready x_ready "
                     "ssm_out y_ready ssm_nlink ssm_slink ssm_blink rows_loaded weights_loaded small_loaded readout_loaded v_ready "
                     "v_turned vT_ready scores_ready mask_ready "
                     "z_ready ez_ready gate_link xh_ready xh_turned two_out "
                     "n_ready proj_read proj_done conv_read conv2_done y2_ready two_done two_nlink two_link "
                     "sig phi_link phi_sum phi_root q_ready lg_read q_turned qT_ready "
                     "lg_done xs_read edt_ready lt_done ht_read ed_read ed_turned ect_read ect_turned xs_done "
                     "hat_ready ht_done lg_max lt_max ect_stored0 ect_stored1 xvar xroot soft_nlink lg_link rzd_ready "
                     "xs_link rzc_sum expert_out slots_ready expert_hid expert_act expert_read y_stored0 y_stored1 y_stored2 y_stored3 "
                     "soft_loaded mixed mix_out stored0 stored1 stored2 stored3 yb_ready mix_loaded0 mix_loaded1 mix_loaded2 expert_loaded0 "
                     "expert_loaded1 expert_loaded2 expert_loaded3").split():
            S[name] = ctx.enter_context(nc.semaphore(name))
        early_names = ("wt_loaded w0_loaded gram_ready band_loaded w0_split w60_loaded ident_zero identb_ready "
                       "pool_zero dve w0_centred wt_centred w0c_ready w0c_copied gram_done normed l0_ready "
                       "h_ready conv_done turned patch_ready zz_done patch_copied patch_turned window_turned "
                       "window_copied gram_applied l0_done summed squared carried0 carried1 carried2 carried3 "
                       "var_ready rstd_ready zsum zvar_ready zrstd_ready scaled_ready x_loaded cols_loaded "
                       "ident_ready").split()
        for name in early_names:
            S[name] = nc.alloc_semaphore(name=name)
        late_names = [f"{name}{layer}" for layer in (5, 6)
                      for name in ("in", "conv", "sq", "sum", "var", "rstd", "norm", "turn", "out")]
        late_names += ("scores_made scores_copied zero_ready cleared one_ready ffn_var ffn_root scattered ranks_ready expert_ready rows_ready "
                       "routed_done routed_stored rows_copied rows_turned hidden hidden_done hidden_copied "
                       "hidden_turned routed_out mix_ahead0 mix_ahead1 mix_ahead2 gathered0 gathered1 gathered2 gathered3 gathered4 gathered5 gathered6 gathered7 routed_loaded0 "
                       "routed_loaded1 routed_loaded2 routed_loaded3 routed_loaded4").split()

        sb("ident", [P, P])
        sb("minus_half", [P, 8])
        sb("bn", [P, TPB, 6])
        sb("mv", [P, TPB, 2])
        sb("nvar", [P, 4])
        sb("nrstd", [P, 4])
        sb("h", [P, TILES, D])
        sb("phA", [P, SLOTS])
        sb("phB", [D2, SLOTS])
        sb("egA", [P, 2, SOFT_E])
        sb("egB", [D2, 2, SOFT_E])
        sb("b2s", [P, SC, D])
        with ExitStack() as weights:
            def sw(name, shape, dt=F32):
                sb(name, shape, dt, weights)
            sw("cols", [P, 19])
            sw("rows", [TOK, 3, D])
            sw("gate_row", [TOK, 3 * N_EXPERT])
            sw("proj_w", [P, D])
            sw("CT", [P, 2, D])
            sw("BTa", [P, 2, P])
            sw("BTb", [D2, 2, P])
            sw("gate_wa", [P, N_EXPERT])
            sw("gate_wb", [D2, N_EXPERT])
            sw("Wia", [P, 4, P])
            sw("Wib", [D2, 4, P])
            sw("Wca", [P, 3, 3 * P])
            sw("Wcb", [P, 3 * P])
            sw("Wcc", [D2, 3 * P])
            sw("Woa", [P, D])
            sw("Wob", [P, D])
            sw("mcol", [P, 21])
            sw("lncol", [P, 8])
            sw("sv", [P, 24])
            sw("Cq", [P, 2, D])
            sw("cosT", [P, LEN])
            sw("sinT", [P, LEN])
            with ExitStack() as conv:
                def sc(name, shape, dt=F32):
                    sb(name, shape, dt, conv)
                sc("wt", [P, 16, C])
                sc("l4", [P, CHUNK // 16 * (CHUNKS + 2)])
                sc("sq", [P, 2, 512])
                sc("yn", [P, 2, 512])
                sc("ss", [P, 2, 4])
                sc("var", [P, 2, 4])
                sc("rstd", [P, 2, 4])
                with ExitStack() as early:
                    def se(name, shape, dt=F32):
                        sb(name, shape, dt, early)
                    se("identb", [P, P], BF16)
                    se("wmean", [P, 16])
                    se("w0T", [TAPS0, C])
                    se("w0mean", [TAPS0, 1])
                    se("w0parts", [TAPS0, 3, C], BF16)
                    se("w0rest", [TAPS0, C])
                    se("w0c", [P, TAPS0])
                    se("gram", [TAPS0, TAPS0])
                    se("band", [WINH, HALF * TAPS0])
                    se("w60", [2 * ROWS, 2, C], BF16)
                    se("xs", [P, WIN])
                    se("xT", [WINH, 2, P])
                    se("zz", [P, POS, TAPS0])
                    se("zs", [P, POS])
                    se("zvar", [P, POS])
                    se("zrstd", [P, POS])
                    se("scaled", [P, POS, TAPS0])
                    se("rest", [P, POS, TAPS0])
                    se("p60", [P, POS, ROWS], BF16)
                    se("p60T", [2 * ROWS, PAIRS, P], BF16)
                    se("l0", [P, 2 + CHUNK])
                    se("l1", [P, 1 + CHUNK // 2])
                    se("l2", [P, 1 + CHUNK // 4])
                    se("l3", [P, 1 + CHUNK // 8])
                    se("rot", [P, LEN])
                    se("Ctmp", [P, D])
                    setup(nc, T, S, io)
                    stream(nc, T, S, io)
                nc.all_engine_barrier()
                nc.clear_and_free_semaphores([S[name] for name in early_names])
                nc.all_engine_barrier()
                for name in late_names:
                    S[name] = nc.alloc_semaphore(name=name)
                with ExitStack() as late:
                    sb("l5", [P, 2 * B * SEQ], on=late)
                    sb("l6", [P, B * SEQ], on=late)
                    sb("stage", [P, 2, 2 * SEQ], on=late)
                    sb("tA", [P, TPB * C], on=late)
                    sb("tB", [P, SEQ], on=late)
                    layers56(nc, T, S)
                    tokens(nc, T, S)
            with ExitStack() as attn:
                def sa(name, shape, dt=F32):
                    sb(name, shape, dt, attn)
                sa("u", [TOK, 2, TPB, D])
                sa("uD", [TOK, TPB, D])
                sa("uA", [P, SEQ])
                sa("uB", [D2, SEQ])
                sa("seq", [P, 8, LEN])
                state_space(nc, T, S)
            sw("v", [TOK, TILES, D])
            sw("row", [P, TILES], I32)
            with ExitStack() as ffn:
                def sf(name, shape, dt=F32):
                    sb(name, shape, dt, ffn)
                sf("scores", [N_EXPERT, SEQ])
                sf("w1a", [P, N_EXPERT * HID])
                sf("w1b", [D2 + 1, N_EXPERT * HID])
                sf("w2", [P, N_EXPERT * HC * D])
                sf("b2", [1, N_EXPERT * D])
                sf("upper", [TOK, TOK])
                sf("steps", [P, TILES + ROUTED])
                sf("zero", [P, D])
                sf("one", [P, P])
                sf("vA", [P, 2, SEQ])
                sf("vB", [D2, 2, SEQ])
                sf("routed", [P, ROUTED, D])
                sf("eA", [P, 2, P])
                sf("eB", [D2 + 1, 2, P])
                sf("G", [P, 2, HID])
                sf("GT", [P, 2, HID])
                sf("fbn", [TOK, TILES, 6])
                sf("fmv", [TOK, TILES, 2])
                sf("fvar", [TOK, TILES])
                sf("frstd", [TOK, TILES])
                for name in ("z", "ez", "mask", "number", "upto"):
                    sf(name, [P, TILES, N_EXPERT])
                sf("top", [P, TILES])
                sf("left", [P, TILES])
                sf("full", [P, N_EXPERT, TILES])
                sf("first", [P, 2 * N_EXPERT])
                sf("begun", [P, ROUTED, N_EXPERT - 1])
                sf("which", [P, ROUTED])
                sf("expert", [P, ROUTED], I32)
                sf("phq", [P, SLOTS])
                sf("phs", [P, 5 * SLOT])
                gate(nc, T, S, io)
                routed_ffn(nc, T, S, io)
            with ExitStack() as two:
                def s2(name, shape, dt=F32):
                    sb(name, shape, dt, two)
                s2("u", [TOK, 2, TPB, D])
                s2("xh", [TOK, 2, TPB, D])
                s2("nA", [P, SEQ])
                s2("nB", [D2, SEQ])
                s2("xA", [P, LEN + 2])
                s2("xB", [P, LEN + 2])
                s2("zA", [P, 2, LEN])
                s2("zB", [P, 2, LEN])
                s2("yA", [P, LEN])
                s2("yB", [P, LEN])
                s2("bu", [P, 3, LEN])
                s2("du", [P, 3, LEN])
                s2("scan", [P, 3, LEN])
                two_way_scan(nc, T, S, io)
        with ExitStack() as soft:
            sb("H1", [P, SOFT_E * P], on=soft)
            sb("H2", [D2, SOFT_E * P], on=soft)
            sb("zc2", [TOK, TILES, 2], on=soft)
            sb("rzc", [TOK, TILES], on=soft)
            with ExitStack() as disp:
                def sd(name, shape, dt=F32):
                    sb(name, shape, dt, disp)
                sd("q", [TOK, 3, TPB, D])
                sd("qA", [P, 2, SEQ])
                sd("qB", [D2, 2, SEQ])
                sd("L", [TOK, 2, TPB, SLOTS])
                sd("EC", [TOK, 2, TPB, SLOTS])
                sd("EDT", [P, 3, LEN])
                sd("ED", [TOK, 2, TPB, SLOTS])
                sd("ECT", [P, 2, SC // 2, SEQ])
                sd("lgm", [TOK, 2, 3])
                sd("ltm", [P, 2])
                sd("zd", [P, SC * B])
                sd("rzd", [P, SC])
                sd("xs2", [P, SC // 2, 2, D])
                sd("xbn", [P, SC, 6])
                sd("xmv", [P, SC, 2])
                sd("xv", [P, SC])
                sd("xrstd", [P, SC])
                dispatch(nc, T, S, io)
            def sx(name, shape, dt=F32):
                sb(name, shape, dt, soft)
            sx("w12", [P, RING, SOFT_H + SHC * D])
            sx("w1x", [D2 + 1, RING, SOFT_H])
            sx("a1", [P, RING, P])
            sx("a2", [D2 + 1, RING, P])
            sx("eg", [P, 2, SOFT_H])
            sx("ye", [P, RING, D])
            with nc.Block() as block:
                @block.gpsimd
                def _(pool):
                    pool.memset(T["a2"][:, :, :], 1.0)
            sx("yb", [P, MIX_RING, SC, D])
            sx("ectb", [P, MIX_RING, SC, SEQ])
            experts(nc, T, S, io)
            sx("o", [TOK, 4, D])
            combine(nc, T, S, io)


def kernel(**inputs):
    import numpy as np
    import concourse.bacc as bacc
    from concourse.bass_utils import run_bass_kernel_spmd as launch

    a = {k: np.asarray(v) for k, v in inputs.items()}
    x = np.concatenate([a["x"].reshape(-1), np.zeros(((CHUNKS + 3) * STEP + WIN - a["x"].size,), a["x"].dtype)])
    conv_w = np.concatenate([a[f"L0_tok_conv_w{l}"].transpose(1, 2, 0) for l in range(1, 7)], axis=1)
    at, ff, tw = (lambda n, p=p: a[p + n] for p in ("L0_attn_", "L0_ffn_", "L1_attn_"))
    cols = np.stack([a[f"L0_tok_ln_g{l}"] for l in range(7)] + [a["L0_tok_fln_g"]]
                    + [a[f"L0_tok_ln_b{l}"] for l in range(7)] + [a["L0_tok_fln_b"]]
                    + [at("log_A_real"), at("A_imag"), at("log_dt")], axis=1)
    arrays = {"x": x, "conv_w": conv_w, "conv_w0": a["L0_tok_conv_w0"][:, 0, :].T, "cols": cols}
    arrays["proj_w"] = a["L0_tok_proj_w"]
    arrays["rows"] = np.stack([a["L0_tok_proj_b"], at("D"), tw("bo")])
    arrays["gate_row"] = np.concatenate([ff("gate_b"), ff("gate_center")])
    arrays["CT"] = np.stack([at("C_re").T, at("C_im").T], axis=1)
    BT = np.stack([at("B_re").T, at("B_im").T], axis=1)
    arrays["BTa"], arrays["BTb"] = BT[:D1], BT[D1:]
    arrays["gate_wa"], arrays["gate_wb"] = ff("gate_w")[:D1], ff("gate_w")[D1:]
    arrays["b2"] = ff("b2").reshape(1, N_EXPERT * D)
    arrays["upper"] = np.triu(np.ones((TOK, TOK), np.float32), 1)
    arrays["steps"] = np.tile(np.concatenate([P * np.arange(TILES), np.arange(ROUTED)]).astype(np.float32), (P, 1))
    w1 = ff("w1").transpose(1, 0, 2).reshape(D, N_EXPERT * HID)
    arrays["w1a"], arrays["w1b"] = w1[:D1], np.concatenate([w1[D1:], ff("b1").reshape(1, N_EXPERT * HID)])
    arrays["w2"] = ff("w2").reshape(N_EXPERT * HC, P, D).transpose(1, 0, 2).reshape(P, N_EXPERT * HC * D)

    def halves(v):
        return v[..., :D1], np.concatenate([v[..., D1:], v[..., D1:]], axis=-1)
    Wi, bi = tw("Wi"), tw("bi")
    W = np.stack(halves(Wi[:, :D]) + halves(Wi[:, D:]), axis=1)
    arrays["Wia"], arrays["Wib"] = W[:D1], W[D1:]
    g, g2 = halves(tw("ln_g"))
    b, b2 = halves(tw("ln_b"))
    arrays["lncol"] = np.stack((g, g2, b, b2) + halves(bi[:D]) + halves(bi[D:]), axis=1)

    def mixed(f, b):
        return np.concatenate([f[..., :D1], b[..., :D1], f[..., D1:], b[..., D1:]], axis=-1)
    Wc = mixed(tw("Wf_conv").transpose(1, 2, 0), tw("Wb_conv").transpose(1, 2, 0)[:, ::-1])
    arrays["Wca"] = Wc[:D1]
    arrays["Wcb"] = np.concatenate([Wc[D1:, 0], Wc[D1:, 1]])
    arrays["Wcc"] = Wc[D1:, 2]
    arrays["Woa"], arrays["Wob"] = tw("Wo")[:D1], np.concatenate([tw("Wo")[D1:], tw("Wo")[D1:]])
    arrays["mcol"] = np.concatenate([mixed(tw(f), tw(b)).reshape(3, P).T for f, b in
                                     (("bf_conv", "bb_conv"), ("af", "ab"), ("bf", "bb"), ("cf", "cb"), ("df", "db"))],
                                    axis=1)
    so = lambda n: a["L1_ffn_" + n]
    phi = so("phi").transpose(2, 0, 1).reshape(D, SLOTS)
    arrays["phiA"], arrays["phiB"] = phi[:D1], phi[D1:]
    arrays["w12"] = np.concatenate([so("w1")[:, :D1], so("w2").reshape(SOFT_E, SHC, P, D).transpose(0, 2, 1, 3)
                                    .reshape(SOFT_E, P, SHC * D)], axis=2)
    arrays["w1x"] = np.concatenate([so("w1")[:, D1:], so("b1")[:, None]], axis=1)
    eg = np.stack([so("ln_g").T, so("ln_b").T], axis=1)
    arrays["egA"], arrays["egB"] = eg[:D1], eg[D1:]
    arrays["soft_b2"] = so("b2")
    arrays = {k: np.ascontiguousarray(v) for k, v in arrays.items()}
    nc = bacc.Bacc("TRN2", target_bir_lowering=False, num_devices=1)
    io = {k: nc.dram_tensor("in_" + k, v.shape, mybir.dt.from_np(v.dtype), kind="ExternalInput").ap()
          for k, v in arrays.items()}
    io["out"] = nc.dram_tensor("out", [B, LEN, D], F32, kind="ExternalOutput").ap()
    for name in ("sorted", "routed"):
        io[name] = nc.dram_tensor(name, [ROUTED * P, D], F32, kind="Internal").ap()
    io["ect"] = nc.dram_tensor("ect", [B, P, SC, SEQ], F32, kind="Internal").ap()
    io["ys"] = nc.dram_tensor("ys", [B, SLOTS, D], F32, kind="Internal").ap()
    program(nc, io)
    r = launch(nc, [{"in_" + k: v for k, v in arrays.items()}], core_ids=[0])
    return r.results[0]["out"]
```
